# Optimizing a Trainium2 kernel written in Bass

```python
import numpy as np
import jax
import jax.numpy as jnp

def _softmax(x, axis=-1):
    return jax.nn.softmax(x, axis=axis)

def _gelu(x):
    return jax.nn.gelu(x, approximate=True)

def _silu(x):
    return jax.nn.silu(x)

def _sigmoid(x):
    return jax.nn.sigmoid(x)

def _layernorm(x, axis=-1, eps=1e-05):
    m = jnp.mean(x, axis=axis, keepdims=True)
    v = jnp.var(x, axis=axis, keepdims=True)
    return (x - m) / jnp.sqrt(v + eps)

def _scatter_add(tgt, idx, src, axis=0):
    return tgt.at[idx].add(src)

def _segment_sum(src, seg, n):
    return jax.ops.segment_sum(src, seg, n)
kernel_name = 'mk_cond_seq_d4_seqx_r8_44e1ef'

def setup_inputs(seed: int=0):
    np.random.seed(seed)
    _w = jnp.asarray

    def _rec_inputs():
        import jax
        import jax.numpy as jnp
        _rk = jax.random.key(seed)
        x = 7.22e-05 + 1 * jax.random.normal(jax.random.fold_in(_rk, 1), (8, 256, 128), jnp.float32)
        _lenS = 256 - jax.random.randint(jax.random.fold_in(_rk, 7), (8,), 0, max(1, 256 // 4) + 1, jnp.int32)
        _lenS2 = 256 - jax.random.randint(jax.random.fold_in(_rk, 8), (8,), 0, max(1, 256 // 4) + 1, jnp.int32)
        cond_2048 = 0.00782532 + 1.00527 * jax.random.normal(jax.random.fold_in(_rk, 11), (8, 256), jnp.float32)
        _validS = jnp.arange(256)[None, :] < _lenS[:, None]
        _validS2 = jnp.arange(256)[None, :] < _lenS2[:, None]
        _causal = jnp.tril(jnp.ones((256, 256), dtype=bool))
        mask_BxSx1_fk1 = jnp.where(jnp.ones((8, 256, 1), dtype=bool), 1.0, 0.0).astype(jnp.float32)
        mask_BxS_ik0 = jnp.where(jnp.broadcast_to(_validS[:, :], (8, 256)), 0, 1).astype(jnp.int32)
        mask_BxS_ff1 = jnp.where(jnp.ones((8, 256), dtype=bool), 1.0, 0.0).astype(jnp.float32)
        return (x, cond_2048, mask_BxSx1_fk1, mask_BxS_ik0, mask_BxS_ff1)
    x, cond_2048, mask_BxSx1_fk1, mask_BxS_ik0, mask_BxS_ff1 = _rec_inputs()

    def _L0_cond_setup():
        import jax, jax.numpy as jnp
        import numpy as np
        B, T, D, H, TE = (4, 256, 128, 8, 256)
        EPS = 1e-05

        def _ln(x, w, b):
            m = jnp.mean(x, axis=-1, keepdims=True)
            v = jnp.mean((x - m) ** 2, axis=-1, keepdims=True)
            return (x - m) * jax.lax.rsqrt(v + EPS) * w + b
        key = jax.random.key(seed)
        ks = jax.random.split(key, 16)
        s = 0.02
        inp = {'x': jax.random.normal(ks[0], (B, T, D), jnp.float32), 'emb': jax.random.normal(ks[1], (B, TE), jnp.float32), 'src_mask': (jax.random.uniform(ks[2], (B, T, 1)) > 0.2).astype(jnp.float32), 'num_head': H, 'ln_w': jnp.ones((D,), jnp.float32), 'ln_b': jnp.zeros((D,), jnp.float32), 'Wq': jax.random.normal(ks[3], (D, D), jnp.float32) * s, 'bq': jnp.zeros((D,), jnp.float32), 'Wk': jax.random.normal(ks[4], (D, D), jnp.float32) * s, 'bk': jnp.zeros((D,), jnp.float32), 'Wv': jax.random.normal(ks[5], (D, D), jnp.float32) * s, 'bv': jnp.zeros((D,), jnp.float32), 'W_emb': jax.random.normal(ks[6], (TE, 2 * D), jnp.float32) * s, 'b_emb': jnp.zeros((2 * D,), jnp.float32), 'ln2_w': jnp.ones((D,), jnp.float32), 'ln2_b': jnp.zeros((D,), jnp.float32), 'W_out': jax.random.normal(ks[7], (D, D), jnp.float32) * s, 'b_out': jnp.zeros((D,), jnp.float32)}
        return inp
    _L0_cond_all = _L0_cond_setup()
    _L0_cond_in = {k: v for k, v in _L0_cond_all.items() if k in ('ln_w', 'ln_b', 'Wq', 'bq', 'Wk', 'bk', 'Wv', 'bv', 'W_emb', 'b_emb', 'ln2_w', 'ln2_b', 'W_out', 'b_out')}
    del _L0_cond_all

    def _L1_cond_setup():
        import jax, jax.numpy as jnp
        import numpy as np
        H = 16
        LN_EPS = 1e-05

        def _layernorm(x, scale, bias):
            mu = jnp.mean(x, axis=-1, keepdims=True)
            var = jnp.var(x, axis=-1, keepdims=True)
            return (x - mu) * jax.lax.rsqrt(var + LN_EPS) * scale + bias
        key = jax.random.key(seed)
        ks = jax.random.split(key, 8)
        B, T, D, E = (4, 512, 128, 256)
        s = 0.02
        return {'x': jax.random.normal(ks[0], (B, T, D), jnp.float32), 'emb': jax.random.normal(ks[1], (B, E), jnp.float32), 'src_mask': jax.random.randint(ks[2], (B, T), 0, 2).astype(jnp.int32), 'norm_scale': jnp.ones((D,), jnp.float32), 'norm_bias': jnp.zeros((D,), jnp.float32), 'Wq': jax.random.normal(ks[3], (D, D), jnp.float32) * s, 'bq': jnp.zeros((D,), jnp.float32), 'Wk': jax.random.normal(ks[4], (D, D), jnp.float32) * s, 'bk': jnp.zeros((D,), jnp.float32), 'Wv': jax.random.normal(ks[5], (D, D), jnp.float32) * s, 'bv': jnp.zeros((D,), jnp.float32), 'film_emb_W': jax.random.normal(ks[6], (E, 2 * D), jnp.float32) * s, 'film_emb_b': jnp.zeros((2 * D,), jnp.float32), 'film_norm_scale': jnp.ones((D,), jnp.float32), 'film_norm_bias': jnp.zeros((D,), jnp.float32), 'film_out_W': jax.random.normal(ks[7], (D, D), jnp.float32) * s, 'film_out_b': jnp.zeros((D,), jnp.float32)}
    _L1_cond_all = _L1_cond_setup()
    _L1_cond_in = {k: v for k, v in _L1_cond_all.items() if k in ('norm_scale', 'norm_bias', 'Wq', 'bq', 'Wk', 'bk', 'Wv', 'bv', 'film_emb_W', 'film_emb_b', 'film_norm_scale', 'film_norm_bias', 'film_out_W', 'film_out_b')}
    del _L1_cond_all

    def _L2_cond_setup():
        import jax, jax.numpy as jnp
        import numpy as np
        D = 128
        DI = 256
        N = 16
        DT_RANK = 64
        D_CONV = 4
        EPS = 1e-05

        def _layernorm(x, g, b):
            mu = jnp.mean(x, axis=-1, keepdims=True)
            var = jnp.mean((x - mu) ** 2, axis=-1, keepdims=True)
            return (x - mu) * jax.lax.rsqrt(var + EPS) * g + b

        def _mamba(xn, in_proj_w, conv_w, conv_b, x_proj_w, dt_proj_w, dt_proj_b, A_log, D_param, out_proj_w):
            b, sl, _ = xn.shape
            xz = jnp.einsum('bsd,ed->bse', xn, in_proj_w)
            x_in, z = jnp.split(xz, 2, axis=-1)
            xt = jnp.transpose(x_in, (0, 2, 1))
            u = jax.lax.conv_general_dilated(xt, conv_w[:, None, :], (1,), [(D_CONV - 1, 0)], feature_group_count=DI, dimension_numbers=('NCH', 'OIH', 'NCH')) + conv_b[None, :, None]
            u = jax.nn.silu(jnp.transpose(u, (0, 2, 1)))
            x_dbl = jnp.einsum('bsd,ed->bse', u, x_proj_w)
            dt_r, B, C = jnp.split(x_dbl, [DT_RANK, DT_RANK + N], axis=-1)
            dt = jax.nn.softplus(jnp.einsum('bsr,dr->bsd', dt_r, dt_proj_w) + dt_proj_b)
            A = -jnp.exp(A_log)

            def step(h, inp):
                dt_t, B_t, C_t, u_t = inp
                dA = jnp.exp(dt_t[:, :, None] * A)
                h = h * dA + (dt_t * u_t)[:, :, None] * B_t[:, None, :]
                y = jnp.einsum('bdn,bn->bd', h, C_t)
                return (h, y)
            seq = (jnp.transpose(dt, (1, 0, 2)), jnp.transpose(B, (1, 0, 2)), jnp.transpose(C, (1, 0, 2)), jnp.transpose(u, (1, 0, 2)))
            h0 = jnp.zeros((b, DI, N), xn.dtype)
            _, ys = jax.lax.scan(step, h0, seq)
            y = jnp.transpose(ys, (1, 0, 2)) + u * D_param
            y = y * jax.nn.silu(z)
            return jnp.einsum('bsd,ed->bse', y, out_proj_w)
        key = jax.random.key(seed)
        ks = jax.random.split(key, 16)
        s = lambda fan: 1.0 / np.sqrt(fan)
        inp = {'x': jax.random.normal(ks[0], (2, 256, D), jnp.float32), 'c': jax.random.normal(ks[1], (2, 2 * D), jnp.float32), 'ln_g': jnp.ones((D,), jnp.float32), 'ln_b': jnp.zeros((D,), jnp.float32), 'ada_w': jax.random.normal(ks[2], (3 * D, 2 * D), jnp.float32) * s(2 * D), 'ada_b': jnp.zeros((3 * D,), jnp.float32), 'in_proj_w': jax.random.normal(ks[3], (2 * DI, D), jnp.float32) * s(D), 'conv_w': jax.random.normal(ks[4], (DI, D_CONV), jnp.float32) * s(D_CONV), 'conv_b': jnp.zeros((DI,), jnp.float32), 'x_proj_w': jax.random.normal(ks[5], (DT_RANK + 2 * N, DI), jnp.float32) * s(DI), 'dt_proj_w': jax.random.normal(ks[6], (DI, DT_RANK), jnp.float32) * s(DT_RANK), 'dt_proj_b': jax.random.uniform(ks[7], (DI,), jnp.float32, -4.0, -2.0), 'A_log': jnp.tile(jnp.log(jnp.arange(1, N + 1, dtype=jnp.float32)), (DI, 1)), 'D_param': jnp.ones((DI,), jnp.float32), 'out_proj_w': jax.random.normal(ks[8], (D, DI), jnp.float32) * s(DI)}
        return inp
    _L2_cond_all = _L2_cond_setup()
    _L2_cond_in = {k: v for k, v in _L2_cond_all.items() if k in ('ln_g', 'ln_b', 'ada_w', 'ada_b', 'in_proj_w', 'conv_w', 'conv_b', 'x_proj_w', 'dt_proj_w', 'dt_proj_b', 'A_log', 'D_param', 'out_proj_w')}
    del _L2_cond_all

    def _L3_cond_setup():
        import jax, jax.numpy as jnp
        import numpy as np
        B, T, D, H, TE = (8, 128, 128, 16, 256)
        LN_EPS = 1e-05

        def layer_norm(x, w, b):
            m = jnp.mean(x, axis=-1, keepdims=True)
            v = jnp.var(x, axis=-1, keepdims=True)
            return (x - m) / jnp.sqrt(v + LN_EPS) * w + b
        key = jax.random.key(seed)
        ks = jax.random.split(key, 8)
        s = lambda k, sh: jax.random.normal(k, sh, jnp.float32) * 0.02
        return dict(x=jax.random.normal(ks[0], (B, T, D), jnp.float32), emb=jax.random.normal(ks[1], (B, TE), jnp.float32), src_mask=jnp.ones((B, T), jnp.float32), norm_w=jnp.ones((D,), jnp.float32), norm_b=jnp.zeros((D,), jnp.float32), q_w=s(ks[2], (D, D)), q_b=jnp.zeros((D,), jnp.float32), k_w=s(ks[3], (D, D)), k_b=jnp.zeros((D,), jnp.float32), v_w=s(ks[4], (D, D)), v_b=jnp.zeros((D,), jnp.float32), emb_w=s(ks[5], (TE, 2 * D)), emb_b=jnp.zeros((2 * D,), jnp.float32), sb_norm_w=jnp.ones((D,), jnp.float32), sb_norm_b=jnp.zeros((D,), jnp.float32), out_w=s(ks[6], (D, D)), out_b=jnp.zeros((D,), jnp.float32))
    _L3_cond_all = _L3_cond_setup()
    _L3_cond_in = {k: v for k, v in _L3_cond_all.items() if k in ('norm_w', 'norm_b', 'q_w', 'q_b', 'k_w', 'k_b', 'v_w', 'v_b', 'emb_w', 'emb_b', 'sb_norm_w', 'sb_norm_b', 'out_w', 'out_b')}
    del _L3_cond_all
    return {'x': x, 'cond_2048': cond_2048, 'mask_BxSx1_fk1': mask_BxSx1_fk1, 'mask_BxS_ik0': mask_BxS_ik0, 'mask_BxS_ff1': mask_BxS_ff1, 'L0_cond_ln_w': _L0_cond_in['ln_w'], 'L0_cond_ln_b': _L0_cond_in['ln_b'], 'L0_cond_Wq': _L0_cond_in['Wq'], 'L0_cond_bq': _L0_cond_in['bq'], 'L0_cond_Wk': _L0_cond_in['Wk'], 'L0_cond_bk': _L0_cond_in['bk'], 'L0_cond_Wv': _L0_cond_in['Wv'], 'L0_cond_bv': _L0_cond_in['bv'], 'L0_cond_W_emb': _L0_cond_in['W_emb'], 'L0_cond_b_emb': _L0_cond_in['b_emb'], 'L0_cond_ln2_w': _L0_cond_in['ln2_w'], 'L0_cond_ln2_b': _L0_cond_in['ln2_b'], 'L0_cond_W_out': _L0_cond_in['W_out'], 'L0_cond_b_out': _L0_cond_in['b_out'], 'L1_cond_norm_scale': _L1_cond_in['norm_scale'], 'L1_cond_norm_bias': _L1_cond_in['norm_bias'], 'L1_cond_Wq': _L1_cond_in['Wq'], 'L1_cond_bq': _L1_cond_in['bq'], 'L1_cond_Wk': _L1_cond_in['Wk'], 'L1_cond_bk': _L1_cond_in['bk'], 'L1_cond_Wv': _L1_cond_in['Wv'], 'L1_cond_bv': _L1_cond_in['bv'], 'L1_cond_film_emb_W': _L1_cond_in['film_emb_W'], 'L1_cond_film_emb_b': _L1_cond_in['film_emb_b'], 'L1_cond_film_norm_scale': _L1_cond_in['film_norm_scale'], 'L1_cond_film_norm_bias': _L1_cond_in['film_norm_bias'], 'L1_cond_film_out_W': _L1_cond_in['film_out_W'], 'L1_cond_film_out_b': _L1_cond_in['film_out_b'], 'L2_cond_ln_g': _L2_cond_in['ln_g'], 'L2_cond_ln_b': _L2_cond_in['ln_b'], 'L2_cond_ada_w': _L2_cond_in['ada_w'], 'L2_cond_ada_b': _L2_cond_in['ada_b'], 'L2_cond_in_proj_w': _L2_cond_in['in_proj_w'], 'L2_cond_conv_w': _L2_cond_in['conv_w'], 'L2_cond_conv_b': _L2_cond_in['conv_b'], 'L2_cond_x_proj_w': _L2_cond_in['x_proj_w'], 'L2_cond_dt_proj_w': _L2_cond_in['dt_proj_w'], 'L2_cond_dt_proj_b': _L2_cond_in['dt_proj_b'], 'L2_cond_A_log': _L2_cond_in['A_log'], 'L2_cond_D_param': _L2_cond_in['D_param'], 'L2_cond_out_proj_w': _L2_cond_in['out_proj_w'], 'L3_cond_norm_w': _L3_cond_in['norm_w'], 'L3_cond_norm_b': _L3_cond_in['norm_b'], 'L3_cond_q_w': _L3_cond_in['q_w'], 'L3_cond_q_b': _L3_cond_in['q_b'], 'L3_cond_k_w': _L3_cond_in['k_w'], 'L3_cond_k_b': _L3_cond_in['k_b'], 'L3_cond_v_w': _L3_cond_in['v_w'], 'L3_cond_v_b': _L3_cond_in['v_b'], 'L3_cond_emb_w': _L3_cond_in['emb_w'], 'L3_cond_emb_b': _L3_cond_in['emb_b'], 'L3_cond_sb_norm_w': _L3_cond_in['sb_norm_w'], 'L3_cond_sb_norm_b': _L3_cond_in['sb_norm_b'], 'L3_cond_out_w': _L3_cond_in['out_w'], 'L3_cond_out_b': _L3_cond_in['out_b']}

def reference(x, cond_2048, mask_BxSx1_fk1, mask_BxS_ik0, mask_BxS_ff1, L0_cond_ln_w, L0_cond_ln_b, L0_cond_Wq, L0_cond_bq, L0_cond_Wk, L0_cond_bk, L0_cond_Wv, L0_cond_bv, L0_cond_W_emb, L0_cond_b_emb, L0_cond_ln2_w, L0_cond_ln2_b, L0_cond_W_out, L0_cond_b_out, L1_cond_norm_scale, L1_cond_norm_bias, L1_cond_Wq, L1_cond_bq, L1_cond_Wk, L1_cond_bk, L1_cond_Wv, L1_cond_bv, L1_cond_film_emb_W, L1_cond_film_emb_b, L1_cond_film_norm_scale, L1_cond_film_norm_bias, L1_cond_film_out_W, L1_cond_film_out_b, L2_cond_ln_g, L2_cond_ln_b, L2_cond_ada_w, L2_cond_ada_b, L2_cond_in_proj_w, L2_cond_conv_w, L2_cond_conv_b, L2_cond_x_proj_w, L2_cond_dt_proj_w, L2_cond_dt_proj_b, L2_cond_A_log, L2_cond_D_param, L2_cond_out_proj_w, L3_cond_norm_w, L3_cond_norm_b, L3_cond_q_w, L3_cond_q_b, L3_cond_k_w, L3_cond_k_b, L3_cond_v_w, L3_cond_v_b, L3_cond_emb_w, L3_cond_emb_b, L3_cond_sb_norm_w, L3_cond_sb_norm_b, L3_cond_out_w, L3_cond_out_b):
    import jax
    import jax.numpy as jnp

    def _L0_cond_ref(x, emb, src_mask, num_head, ln_w, ln_b, Wq, bq, Wk, bk, Wv, bv, W_emb, b_emb, ln2_w, ln2_b, W_out, b_out):
        import jax, jax.numpy as jnp
        import numpy as np
        B, T, D, H, TE = (4, 256, 128, 8, 256)
        EPS = 1e-05

        def _ln(x, w, b):
            m = jnp.mean(x, axis=-1, keepdims=True)
            v = jnp.mean((x - m) ** 2, axis=-1, keepdims=True)
            return (x - m) * jax.lax.rsqrt(v + EPS) * w + b
        b, t, d = x.shape
        h = num_head
        dh = d // h
        xn = _ln(x, ln_w, ln_b)
        q = xn @ Wq + bq
        k = xn @ Wk + bk + (1.0 - src_mask) * -1000000.0
        q = jax.nn.softmax(q.reshape(b, t, h, dh), axis=-1)
        k = jax.nn.softmax(k.reshape(b, t, h, dh), axis=1)
        v = ((xn @ Wv + bv) * src_mask).reshape(b, t, h, dh)
        att = jnp.einsum('bnhd,bnhl->bhdl', k, v)
        y = jnp.einsum('bnhd,bhdl->bnhl', q, att).reshape(b, t, d)
        emb_out = (jax.nn.silu(emb) @ W_emb + b_emb)[:, None, :]
        scale, shift = jnp.split(emb_out, 2, axis=2)
        hh = _ln(y, ln2_w, ln2_b) * (1.0 + scale) + shift
        hh = jax.nn.silu(hh) @ W_out + b_out
        return x + hh

    def _L1_cond_ref(x, emb, src_mask, norm_scale, norm_bias, Wq, bq, Wk, bk, Wv, bv, film_emb_W, film_emb_b, film_norm_scale, film_norm_bias, film_out_W, film_out_b):
        import jax, jax.numpy as jnp
        import numpy as np
        H = 16
        LN_EPS = 1e-05

        def _layernorm(x, scale, bias):
            mu = jnp.mean(x, axis=-1, keepdims=True)
            var = jnp.var(x, axis=-1, keepdims=True)
            return (x - mu) * jax.lax.rsqrt(var + LN_EPS) * scale + bias
        B, T, D = x.shape
        dh = D // H
        xn = _layernorm(x, norm_scale, norm_bias)
        q = xn @ Wq + bq
        k = xn @ Wk + bk
        v = xn @ Wv + bv
        mask = (src_mask == 1)[:, :, None]
        k = jnp.where(mask, -jnp.inf, k)
        v = jnp.where(mask, 0.0, v)
        q = q.reshape(B, T, H, dh).transpose(0, 2, 1, 3)
        k = k.reshape(B, T, H, dh).transpose(0, 2, 1, 3)
        v = v.reshape(B, T, H, dh).transpose(0, 2, 1, 3)
        q = jax.nn.softmax(q, axis=-1)
        k = jax.nn.softmax(k, axis=2)
        attn = jnp.einsum('bhse,bhsd->bhed', k, v)
        y = jnp.einsum('bhtd,bhed->bhte', q, attn)
        y = y.transpose(0, 2, 1, 3).reshape(B, T, D)
        emb_out = jax.nn.silu(emb) @ film_emb_W + film_emb_b
        scale, shift = jnp.split(emb_out, 2, axis=-1)
        h = _layernorm(y, film_norm_scale, film_norm_bias) * (1.0 + scale[:, None, :]) + shift[:, None, :]
        h = jax.nn.silu(h) @ film_out_W + film_out_b
        return x + h

    def _L2_cond_ref(x, c, ln_g, ln_b, ada_w, ada_b, in_proj_w, conv_w, conv_b, x_proj_w, dt_proj_w, dt_proj_b, A_log, D_param, out_proj_w):
        import jax, jax.numpy as jnp
        import numpy as np
        D = 128
        DI = 256
        N = 16
        DT_RANK = 64
        D_CONV = 4
        EPS = 1e-05

        def _layernorm(x, g, b):
            mu = jnp.mean(x, axis=-1, keepdims=True)
            var = jnp.mean((x - mu) ** 2, axis=-1, keepdims=True)
            return (x - mu) * jax.lax.rsqrt(var + EPS) * g + b

        def _mamba(xn, in_proj_w, conv_w, conv_b, x_proj_w, dt_proj_w, dt_proj_b, A_log, D_param, out_proj_w):
            b, sl, _ = xn.shape
            xz = jnp.einsum('bsd,ed->bse', xn, in_proj_w)
            x_in, z = jnp.split(xz, 2, axis=-1)
            xt = jnp.transpose(x_in, (0, 2, 1))
            u = jax.lax.conv_general_dilated(xt, conv_w[:, None, :], (1,), [(D_CONV - 1, 0)], feature_group_count=DI, dimension_numbers=('NCH', 'OIH', 'NCH')) + conv_b[None, :, None]
            u = jax.nn.silu(jnp.transpose(u, (0, 2, 1)))
            x_dbl = jnp.einsum('bsd,ed->bse', u, x_proj_w)
            dt_r, B, C = jnp.split(x_dbl, [DT_RANK, DT_RANK + N], axis=-1)
            dt = jax.nn.softplus(jnp.einsum('bsr,dr->bsd', dt_r, dt_proj_w) + dt_proj_b)
            A = -jnp.exp(A_log)

            def step(h, inp):
                dt_t, B_t, C_t, u_t = inp
                dA = jnp.exp(dt_t[:, :, None] * A)
                h = h * dA + (dt_t * u_t)[:, :, None] * B_t[:, None, :]
                y = jnp.einsum('bdn,bn->bd', h, C_t)
                return (h, y)
            seq = (jnp.transpose(dt, (1, 0, 2)), jnp.transpose(B, (1, 0, 2)), jnp.transpose(C, (1, 0, 2)), jnp.transpose(u, (1, 0, 2)))
            h0 = jnp.zeros((b, DI, N), xn.dtype)
            _, ys = jax.lax.scan(step, h0, seq)
            y = jnp.transpose(ys, (1, 0, 2)) + u * D_param
            y = y * jax.nn.silu(z)
            return jnp.einsum('bsd,ed->bse', y, out_proj_w)
        ada = jnp.einsum('bc,ec->be', jax.nn.silu(c), ada_w) + ada_b
        shift, scale, gate = jnp.split(ada, 3, axis=1)
        xn = _layernorm(x, ln_g, ln_b)
        xn = xn * (1.0 + scale[:, None, :]) + shift[:, None, :]
        x_ssm = _mamba(xn, in_proj_w, conv_w, conv_b, x_proj_w, dt_proj_w, dt_proj_b, A_log, D_param, out_proj_w)
        return x + gate[:, None, :] * x_ssm

    def _L3_cond_ref(x, emb, src_mask, norm_w, norm_b, q_w, q_b, k_w, k_b, v_w, v_b, emb_w, emb_b, sb_norm_w, sb_norm_b, out_w, out_b):
        import jax, jax.numpy as jnp
        import numpy as np
        B, T, D, H, TE = (8, 128, 128, 16, 256)
        LN_EPS = 1e-05

        def layer_norm(x, w, b):
            m = jnp.mean(x, axis=-1, keepdims=True)
            v = jnp.var(x, axis=-1, keepdims=True)
            return (x - m) / jnp.sqrt(v + LN_EPS) * w + b
        Bx, Tx, Dx = x.shape
        xn = layer_norm(x, norm_w, norm_b)
        q = (xn @ q_w + q_b).reshape(Bx, Tx, H, -1)
        k = (xn @ k_w + k_b).reshape(Bx, Tx, H, -1)
        att = jnp.einsum('bnhl,bmhl->bnmh', q, k)
        mask = src_mask.reshape(Bx, 1, Tx, 1)
        att = att + (1.0 - mask) * -1000000.0
        att = jax.nn.softmax(att, axis=2)
        v = ((xn @ v_w + v_b) * src_mask[:, :, None]).reshape(Bx, Tx, H, -1)
        y = jnp.einsum('bnmh,bmhl->bnhl', att, v).reshape(Bx, Tx, Dx)
        e = jax.nn.silu(emb) @ emb_w + emb_b
        scale, shift = jnp.split(e[:, None, :], 2, axis=2)
        h = layer_norm(y, sb_norm_w, sb_norm_b) * (1.0 + scale) + shift
        h = jax.nn.silu(h) @ out_w + out_b
        return x + h
    x = _L0_cond_ref(x, cond_2048, mask_BxSx1_fk1, 8, L0_cond_ln_w, L0_cond_ln_b, L0_cond_Wq, L0_cond_bq, L0_cond_Wk, L0_cond_bk, L0_cond_Wv, L0_cond_bv, L0_cond_W_emb, L0_cond_b_emb, L0_cond_ln2_w, L0_cond_ln2_b, L0_cond_W_out, L0_cond_b_out)
    x = _L1_cond_ref(x, cond_2048, mask_BxS_ik0, L1_cond_norm_scale, L1_cond_norm_bias, L1_cond_Wq, L1_cond_bq, L1_cond_Wk, L1_cond_bk, L1_cond_Wv, L1_cond_bv, L1_cond_film_emb_W, L1_cond_film_emb_b, L1_cond_film_norm_scale, L1_cond_film_norm_bias, L1_cond_film_out_W, L1_cond_film_out_b)
    x = _L2_cond_ref(x, cond_2048, L2_cond_ln_g, L2_cond_ln_b, L2_cond_ada_w, L2_cond_ada_b, L2_cond_in_proj_w, L2_cond_conv_w, L2_cond_conv_b, L2_cond_x_proj_w, L2_cond_dt_proj_w, L2_cond_dt_proj_b, L2_cond_A_log, L2_cond_D_param, L2_cond_out_proj_w)
    x = _L3_cond_ref(x, cond_2048, mask_BxS_ff1, L3_cond_norm_w, L3_cond_norm_b, L3_cond_q_w, L3_cond_q_b, L3_cond_k_w, L3_cond_k_b, L3_cond_v_w, L3_cond_v_b, L3_cond_emb_w, L3_cond_emb_b, L3_cond_sb_norm_w, L3_cond_sb_norm_b, L3_cond_out_w, L3_cond_out_b)
    return x

_drawn_inputs = setup_inputs


def setup_inputs(seed=0):
    import zlib

    import numpy as np

    out = dict(_drawn_inputs(seed))
    spreads = {'L0_cond_ln_w': (1.0, 0.6),
     'L0_cond_ln_b': (0.0, 0.1),
     'L0_cond_bq': (0.0, 0.8),
     'L0_cond_bk': (0.0, 0.8),
     'L0_cond_bv': (0.0, 0.1),
     'L0_cond_b_emb': (0.0, 0.267),
     'L0_cond_ln2_w': (1.0, 0.2),
     'L0_cond_ln2_b': (0.0, 0.563),
     'L0_cond_b_out': (0.0, 0.1),
     'L1_cond_norm_scale': (1.0, 0.6),
     'L1_cond_norm_bias': (0.0, 0.319),
     'L1_cond_bq': (0.0, 0.8),
     'L1_cond_bk': (0.0, 0.8),
     'L1_cond_bv': (0.0, 0.1),
     'L1_cond_film_emb_b': (0.0, 0.449),
     'L1_cond_film_norm_scale': (1.0, 0.2),
     'L1_cond_film_norm_bias': (0.0, 0.445),
     'L1_cond_film_out_b': (0.0, 0.1),
     'L2_cond_ln_g': (1.0, 0.2),
     'L2_cond_ln_b': (0.0, 0.1),
     'L2_cond_ada_b': (0.0, 0.1),
     'L2_cond_conv_b': (0.0, 0.1),
     'L2_cond_D_param': (1.0, 0.2),
     'L3_cond_norm_w': (1.0, 0.6),
     'L3_cond_norm_b': (0.0, 0.297),
     'L3_cond_q_b': (0.0, 0.8),
     'L3_cond_k_b': (0.0, 0.8),
     'L3_cond_v_b': (0.0, 0.1),
     'L3_cond_emb_b': (0.0, 0.415),
     'L3_cond_sb_norm_w': (1.0, 0.2),
     'L3_cond_sb_norm_b': (0.0, 0.633),
     'L3_cond_out_b': (0.0, 0.1)}
    factors = {'L0_cond_Wq': 8.0,
     'L0_cond_Wk': 8.0,
     'L1_cond_Wk': 6.247,
     'L3_cond_q_w': 8.0,
     'L3_cond_k_w': 8.0}
    for name, (base, spread) in spreads.items():
        noise = np.random.default_rng([zlib.crc32(name.encode()), seed]).standard_normal(out[name].shape)
        drawn = base * np.exp(spread * noise) if base else spread * noise
        out[name] = jnp.asarray(drawn.astype(out[name].dtype))
    for name, factor in factors.items():
        out[name] = (out[name] * factor).astype(out[name].dtype)
    return out
```

```python
import concourse.bass as bass
from concourse import mybir
from contextlib import ExitStack

B, T, D, TE = 8, 256, 128, 256
N = B * T
HALVES = 2
NH = N // HALVES
BH = B // HALVES
TILES = NH // 128
BANK = 512
DI, NS, RANK, TAPS = 256, 16, 64, 4
CH = DI // 128
HEADS = (8, 16, 16)
EPS = 1e-5
LOG_EXP = "natural_log_exp_and_others"

MATS0 = [("q0", 128), ("k0", 128), ("v0", 128), ("emb0", 512), ("out0", 128)]
MATS1 = [("q1", 128), ("k1", 128), ("v1", 128), ("emb1", 512), ("out1", 128)]
MATS2 = [("ada", 768), ("inp", 512), ("xdt", 128), ("xbc", 64), ("outp", 256), ("alog", 32), ("convw", 8),
         ("q3", 128), ("k3", 128), ("v3", 128), ("emb3", 512), ("out3", 128)]
LAYER_COLS = ["lnw", "lnb", "bq", "bk", "embs", "embt", "ln2w", "ln2b", "bout"]
COLS = [c + i for i in "013" for c in LAYER_COLS] + [
    "g2", "b2", "adat", "adas", "adag", "convb_0", "convb_1", "dtb_0", "dtb_1", "dp_0", "dp_1"]
ROWS = ["bq0", "bv0", "bq1", "bv1", "bv3"]


def offsets(mats):
    at, out = 0, {}
    for name, width in mats:
        out[name] = (at, width)
        at += width
    return out, at


def cond_seq_kernel(nc, a_x, a_cond, a_w0, a_w1, a_w2, a_dtp, a_convt, a_cols, a_rows, a_keep0, a_mask1, a_keep3,
                    out):
    f32, bf16, i32 = mybir.dt.float32, mybir.dt.bfloat16, mybir.dt.int32
    ALU, ACT, AX = mybir.AluOpType, mybir.ActivationFunctionType, mybir.AxisListType

    ctx = ExitStack()
    with ctx:
        def sb(name, shape, dt=f32, on=ctx):
            return on.enter_context(nc.sbuf_tensor(name, shape, dt))

        def ps(name, shape, dt=f32, on=ctx):
            return on.enter_context(nc.psum_tensor(name, shape, dt))

        def sem(name, on=ctx):
            return on.enter_context(nc.semaphore(name))

        xT = sb("xT", [D, N])
        off0, n0 = offsets(MATS0)
        off1, n1 = offsets(MATS1)
        off2, n2 = offsets(MATS2)
        w0, w1, w2 = sb("w0", [D, n0]), sb("w1", [D, n1]), sb("w2", [D, n2])
        dtp = sb("dtp", [RANK, DI])
        cols = sb("cols", [D, len(COLS)])
        rows = sb("rows", [1, len(ROWS) * 128])
        cond = sb("cond", [D, 2 * B])

        def mat(name, i=0, n=None):
            for w, off in ((w0, off0), (w1, off1), (w2, off2)):
                if name in off:
                    at, width = off[name]
                    n = n or width
                    return w[:, at + i * n:at + (i + 1) * n]
            raise KeyError(name)

        def col(name):
            c = COLS.index(name)
            return cols[:, c:c + 1]

        def row(name):
            c = ROWS.index(name) * 128
            return rows[0:1, c:c + 128]

        center = sb("center", [D, D])
        mean = sb("mean", [D, D])
        ident = sb("ident", [D, D])
        ones = sb("ones", [3, 128], bf16)
        heads0, heads1 = sb("heads0", [D, D]), sb("heads1", [D, D])
        eps = sb("eps", [D, 1])
        wqkv = [sb(f"wqkv{i}", [D, 3 * D]) for i in range(3)]
        bfold = [sb(f"bfold{i}", [D, 2]) for i in range(3)]
        brow = [sb(f"brow{i}", [3, 3 * D], bf16) for i in range(3)]
        mrow = sb("mrow", [3, 3 * N], bf16)
        film_s = [sb(f"film_s{i}", [D, B]) for i in range(4)]
        film_t = [sb(f"film_t{i}", [D, B]) for i in range(4)]
        gate = sb("gate", [D, B])
        keep = [sb(f"keep{i}", [128, N // 128]) for i in range(3)]
        semb = sb("semb", [D, 2 * B])

        with ExitStack() as on:
            s_cols, s_w0, s_w1, s_w2, s_x = (sem(n, on) for n in ("s_cols", "s_w0", "s_w1", "s_w2", "s_x"))
            s_m = sem("s_m", on)
            s_cst, s_pool, s_dve = sem("s_cst", on), sem("s_pool", on), sem("s_dve", on)
            s_ce, s_semb, s_fold, s_folded = (sem(n, on) for n in ("s_ce", "s_semb", "s_fold", "s_folded"))
            s_keepT = sem("s_keepT", on)
            ce, ce1, cr = (sb(n, [D, 2 * B], f32, on) for n in ("ce", "ce1", "cr"))
            m0, m3 = sb("m0", [N // 128, 128], f32, on), sb("m3", [N // 128, 128], f32, on)
            m1i, m1 = sb("m1i", [N // 128, 128], i32, on), sb("m1", [N // 128, 128], f32, on)
            madd = sb("madd", [N // 128, 3 * 128], f32, on)
            mleft = sb("mleft", [N // 128, 3 * 128], f32, on)
            mpart = [sb(f"mpart{j}", [N // 128, 3 * 128], bf16, on) for j in range(3)]
            brow32, bleft = sb("brow32", [1, 9 * D], f32, on), sb("bleft", [1, 9 * D], f32, on)
            bpart = [sb(f"bpart{j}", [1, 9 * D], bf16, on) for j in range(3)]
            s_mpart, s_bpart, s_rows = sem("s_mpart", on), sem("s_bpart", on), sem("s_rows", on)
            sc1, sh = sb("sc1", [D, 4 * B], f32, on), sb("sh", [D, 4 * B], f32, on)
            Pcol = [ps(f"Pcol{i}", [D, BANK], f32, on) for i in range(4)]
            Pemb = [p[:, 0:3 * B] for p in Pcol]
            Pbias = [p[:, 4 * B:4 * B + 2] for p in Pcol]
            Prow = [ps(f"Prow{i}", [128, BANK], f32, on) for i in range(3)]
            Pkeep = ps("Pkeep", [128, BANK], f32, on)

            block = on.enter_context(nc.Block())

            @block.sync
            def _(sp):
                sp.dma_start(cols[:, :], a_cols).then_inc(s_cols, 16)
                sp.dma_start(cond[:, :], a_cond).then_inc(s_cols, 16)
                sp.dma_start(rows[:, :], a_rows).then_inc(s_cols, 16)
                sp.dma_start(w0[:, :], a_w0).then_inc(s_w0, 16)
                sp.dma_start(xT[:, :], a_x).then_inc(s_x, 16)
                sp.dma_start(w1[:, :], a_w1).then_inc(s_w1, 16)
                sp.dma_start(w2[:, :], a_w2).then_inc(s_w2, 16)
                sp.dma_start(dtp[:, :], a_dtp).then_inc(s_w2, 16)
                sp.wait_ge(s_mpart, 1)
                for j in range(3):
                    for i in range(3):
                        sp.dma_start(mrow[j:j + 1, i * N:(i + 1) * N].rearrange("p (a b) -> p a b", b=128),
                                     mpart[j][:, i * 128:(i + 1) * 128]).then_inc(s_rows, 16)
                for i in range(3):
                    sp.wait_ge(s_bpart, i + 1)
                    for j in range(3):
                        sp.dma_start(brow[i][j:j + 1, :], bpart[j][:, i * 3 * D:(i + 1) * 3 * D]).then_inc(s_rows, 16)
                sp.wait_ge(s_rows, 16 * 18)
                sp.wait_ge(s_x, 16)
                sp.wait_ge(s_w2, 32)

            @block.gpsimd
            def _(pool):
                pool.memset(center[:, :], -1.0 / D).then_inc(s_pool, 1)
                pool.memset(ident[:, :], 0.0).then_inc(s_pool, 1)
                pool.memset(heads0[:, :], 1.0).then_inc(s_pool, 1)
                pool.memset(heads1[:, :], 1.0).then_inc(s_pool, 1)
                pool.memset(mean[:, :], 1.0 / D).then_inc(s_cst, 1)
                pool.memset(ones[:, :], 1.0).then_inc(s_cst, 1)
                pool.memset(eps[:, :], EPS).then_inc(s_cst, 1)
                pool.wait_ge(s_pool, 4)
                pool.affine_select(out=center[:, :], in_=center[:, :], compare_op=ALU.not_equal, fill=1.0 - 1.0 / D,
                                   base=0, pattern=[[-1, D]], channel_multiplier=1).then_inc(s_cst, 1)
                pool.affine_select(out=ident[:, :], in_=ident[:, :], compare_op=ALU.not_equal, fill=1.0,
                                   base=0, pattern=[[-1, D]], channel_multiplier=1).then_inc(s_cst, 1)
                for tile, heads in ((heads0, HEADS[0]), (heads1, HEADS[1])):
                    w = D // heads
                    v = tile[:, :].rearrange("p (h w) -> p h w", w=w)
                    pool.affine_select(out=v, in_=v, compare_op=ALU.is_ge, fill=0.0, base=0,
                                       pattern=[[-w, heads], [0, w]], channel_multiplier=1).then_inc(s_pool, 1)
                pool.wait_ge(s_pool, 6)
                for tile, heads in ((heads0, HEADS[0]), (heads1, HEADS[1])):
                    w = D // heads
                    v = tile[:, :].rearrange("p (h w) -> p h w", w=w)
                    pool.affine_select(out=v, in_=v, compare_op=ALU.is_ge, fill=0.0, base=w - 1,
                                       pattern=[[w, heads], [0, w]], channel_multiplier=-1).then_inc(s_cst, 1)

            @block.scalar
            def _(act):
                act.preload_act_table_set(LOG_EXP)
                act.dma_start(m0[:, :], a_keep0).then_inc(s_m, 16)
                act.dma_start(m1i[:, :], a_mask1).then_inc(s_m, 16)
                act.dma_start(m3[:, :], a_keep3).then_inc(s_m, 16)
                act.wait_ge(s_cols, 48)
                act.activation(ce[:, :], cond[:, :], ACT.Exp, scale=-1.0).then_inc(s_ce, 1)

            layers = (("0", w0, 0), ("1", w1, 1), ("3", w2, 2))

            @block.vector
            def _(dve):
                done = [0]

                def link(ins):
                    done[0] += 1
                    ins.then_inc(s_dve, 1)
                    dve.wait_ge(s_dve, done[0])

                dve.wait_ge(s_ce, 1)
                link(dve.tensor_scalar(ce1[:, :], ce[:, :], 1.0, None, ALU.add))
                link(dve.reciprocal(cr[:, :], ce1[:, :]))
                dve.tensor_tensor(semb[:, :], cond[:, :], cr[:, :], ALU.mult).then_inc(s_semb, 1)
                dve.wait_ge(s_m, 48)
                link(dve.tensor_scalar(m1[:, :], m1i[:, :], 1.0, None, ALU.not_equal))
                link(dve.tensor_scalar(mleft[:, 0:128], m0[:, :], -1.0, 1.0, ALU.mult, ALU.add))
                link(dve.tensor_scalar(mleft[:, 256:384], m3[:, :], -1.0, 1.0, ALU.mult, ALU.add))
                link(dve.tensor_scalar(madd[:, 0:128], mleft[:, 0:128], -1e6, None, ALU.mult))
                link(dve.tensor_scalar(madd[:, 256:384], mleft[:, 256:384], -1e6, None, ALU.mult))
                link(dve.tensor_scalar(madd[:, 128:256], m1i[:, :], 1.0, -1e30, ALU.is_equal, ALU.mult))

                def parts(whole, left, part):
                    link(dve.tensor_copy(part[0], whole))
                    link(dve.tensor_tensor(left, whole, part[0], ALU.subtract))
                    link(dve.tensor_copy(part[1], left))
                    return dve.tensor_tensor(part[2], left, part[1], ALU.subtract)

                parts(madd[:, :], mleft[:, :], [p[:, :] for p in mpart]).then_inc(s_mpart, 1)
                dve.sem_inc(s_keepT, 1)
                dve.wait_ge(s_keepT, 2)
                for i in range(3):
                    link(dve.tensor_copy(keep[i][:, :], Pkeep[:, i * 16:(i + 1) * 16]))
                for name, w, i in layers:
                    dve.wait_ge((s_w0, s_w1, s_w2)[i], 16 if i < 2 else 32)
                    at = {"0": off0, "1": off1, "3": off2}[name]["q" + name][0]
                    link(dve.tensor_scalar(wqkv[i][:, :], w[:, at:at + 3 * D], col("lnw" + name), None, ALU.mult))
                    dve.wait_ge(s_fold, i + 1)
                    link(dve.tensor_tensor(bfold[i][:, 0:1], Pbias[i][:, 0:1], col("bq" + name), ALU.add))
                    link(dve.tensor_tensor(bfold[i][:, 1:2], Pbias[i][:, 1:2], col("bk" + name), ALU.add))
                    at = i * 3 * D
                    link(dve.tensor_copy(brow32[:, at:at + 3 * D], Prow[i][0:1, 0:3 * D]))
                    if name != "3":
                        link(dve.tensor_tensor(brow32[:, at:at + D], brow32[:, at:at + D], row("bq" + name), ALU.add))
                    rv = brow32[:, at + 2 * D:at + 3 * D]
                    link(dve.tensor_tensor(rv, rv, row("bv" + name), ALU.add))
                    r = slice(at, at + 3 * D)
                    parts(brow32[:, r], bleft[:, r], [p[:, r] for p in bpart]).then_inc(s_bpart, 1)
                for i, (s, t, lw, lb) in enumerate((("embs0", "embt0", "ln2w0", "ln2b0"), ("embs1", "embt1", "ln2w1", "ln2b1"),
                                                    ("embs3", "embt3", "ln2w3", "ln2b3"), ("adas", "adat", "g2", "b2"))):
                    dve.wait_ge(s_fold, min(i + 1, 3))
                    link(dve.tensor_scalar(sc1[:, i * B:(i + 1) * B], Pemb[i][:, 0:B], col(s), 1.0, ALU.add, ALU.add))
                    link(dve.tensor_scalar(sh[:, i * B:(i + 1) * B], Pemb[i][:, B:2 * B], col(t), None, ALU.add))
                    half = 1.0 if s == "adas" else 0.5
                    sci, shi = sc1[:, i * B:(i + 1) * B], sh[:, i * B:(i + 1) * B]
                    link(dve.tensor_scalar(film_s[i][:, :], sci, col(lw), half, ALU.mult, ALU.mult))
                    link(dve.scalar_tensor_tensor(shi, sci, col(lb), shi, ALU.mult, ALU.add))
                    link(dve.tensor_scalar(film_t[i][:, :], shi, half, None, ALU.mult))
                link(dve.tensor_scalar(gate[:, :], Pemb[3][:, 2 * B:3 * B], col("adag"), None, ALU.add))

            @block.tensor
            def _(pe):
                pe.wait_ge(s_cst, 7)
                pe.wait_ge(s_m, 48)
                pe.wait_ge(s_keepT, 1)
                pe.transpose(Pkeep[:, 0:16], m0[:, :], ident[0:16, 0:16])
                pe.transpose(Pkeep[:, 16:32], m1[:, :], ident[0:16, 0:16])
                pe.transpose(Pkeep[:, 32:48], m3[:, :], ident[0:16, 0:16]).then_inc(s_keepT, 1)
                pe.wait_ge(s_semb, 1)
                pe.wait_ge(s_cols, 48)
                for name, w, i in layers:
                    pe.wait_ge((s_w0, s_w1, s_w2)[i], 16 if i < 2 else 32)
                    for j, n in enumerate("qk"):
                        pe.matmul(Pbias[i][:, j:j + 1], mat(n + name), col("lnb" + name), start=True, stop=True)
                    at = {"0": off0, "1": off1, "3": off2}[name]["q" + name][0]
                    pe.matmul(Prow[i][0:1, 0:3 * D], col("lnb" + name), w[:, at:at + 3 * D], start=True, stop=True)
                    for part in range(2):
                        for c in range(2):
                            last = pe.matmul(Pemb[i][:, part * B:(part + 1) * B],
                                             mat("emb" + name, c, 256)[:, part * 128:(part + 1) * 128],
                                             semb[:, c * B:(c + 1) * B], start=(c == 0), stop=(c == 1))
                    if i == 2:
                        for part, src in ((0, 1), (1, 0), (2, 2)):
                            for c in range(2):
                                last = pe.matmul(Pemb[3][:, part * B:(part + 1) * B],
                                                 mat("ada", c, 384)[:, src * 128:(src + 1) * 128],
                                                 semb[:, c * B:(c + 1) * B], start=(c == 0), stop=(c == 1))
                    last.then_inc(s_fold, 1)

        attention_steps = ("mean1", "sq1", "var1", "lnv1", "rstd1", "z", "k", "kmax", "kbias", "knb", "ek", "rk", "ekt", "ektc",
                 "q", "qmax", "qs", "eq", "qsum", "rq", "qn", "qnt", "qtc", "v", "vk", "att", "attm", "attc",
                 "attcr", "y", "sq2", "var2", "lnv2", "rstd2", "z2", "h", "he", "hs", "o", "x")
        s_layer = {n: sem(f"l_{n}") for n in attention_steps}

        def attention_layer(i):
            heads = HEADS[i]
            hw = D // heads
            blockmask = (heads0, heads1)[i]
            name = "01"[i]
            with ExitStack() as on:
                s = s_layer
                before = i * HALVES
                two = range(HALVES)

                def pair(n, shape, dt=f32):
                    return [sb(f"{n}{i}_{h}", shape, dt, on) for h in two]

                tmp, rstd, z = pair("tmp", [D, NH]), pair("rstd", [D, NH]), pair("z", [D, NH])
                kmax, knb, ksum, rk, kbias = (pair(n, [D, BH]) for n in ("kmax", "knb", "ksum", "rk", "kbias"))
                ek, ekT = pair("ek", [D, NH]), pair("ekT", [128, NH])
                qmax, qsum, rq = (pair(n, [128, TILES * heads]) for n in ("qmax", "qsum", "rq"))
                qs, qT, vk = pair("qs", [128, NH]), pair("qT", [D, NH]), pair("vk", [128, NH])
                attm, attc = pair("attm", [D, BH * D]), pair("attc", [D, BH * D])
                hb, he, hs = pair("hb", [D, NH]), pair("he", [D, NH]), pair("hs", [D, NH])
                Pa = [ps(f"Pa{i}_{h}", [128, NH], f32, on) for h in two]
                Pb = [ps(f"Pb{i}_{h}", [128, NH], f32, on) for h in two]
                mask = mrow[:, i * N:(i + 1) * N]

                def toks(h):
                    return slice(h * NH, (h + 1) * NH)

                block = on.enter_context(nc.Block())

                @block.tensor
                def _(pe):
                    def wide(out_, lhsT, rhs, signal, stop=True):
                        for c in range(0, NH, BANK):
                            last = pe.matmul(out_[:, c:c + BANK], lhsT, rhs[:, c:c + BANK], start=True, stop=stop)
                        last.then_inc(signal, 1)

                    for h in two:
                        wide(Pa[h], center[:, :], xT[:, toks(h)], s["mean1"])
                    for h in two:
                        pe.wait_ge(s["sq1"], before + h + 1)
                        wide(Pb[h], mean[:, :], tmp[h], s["var1"])
                    for h in two:
                        pe.wait_ge(s["z"], before + h + 1)
                        for c in range(0, NH, BANK):
                            pe.matmul(Pa[h][:, c:c + BANK], wqkv[i][:, D:2 * D], z[h][:, c:c + BANK], start=True, stop=False)
                            last = pe.matmul(Pa[h][:, c:c + BANK], ones[:, :], mask[:, h * NH + c:h * NH + c + BANK],
                                             start=False, stop=True)
                        last.then_inc(s["k"], 1)
                    for h in two:
                        pe.wait_ge(s["rstd1"], before + h + 1)
                        for t in range(TILES):
                            pe.matmul(Pb[h][:, t * D:(t + 1) * D], z[h][:, t * 128:(t + 1) * 128], wqkv[i][:, 0:D],
                                      start=True, stop=False)
                            last = pe.matmul(Pb[h][:, t * D:(t + 1) * D], ones[:, :], brow[i][:, 0:D], start=False, stop=True)
                        last.then_inc(s["q"], 1)
                    for h in two:
                        pe.wait_ge(s["ek"], BH * (before + h + 1))
                        for t in range(TILES):
                            last = pe.transpose(Pa[h][:, t * 128:(t + 1) * 128], ek[h][:, t * 128:(t + 1) * 128], ident[:, :])
                        last.then_inc(s["ekt"], 1)
                    for h in two:
                        pe.wait_ge(s["ektc"], before + h + 1)
                        for t in range(TILES):
                            pe.matmul(Pa[h][:, t * D:(t + 1) * D], z[h][:, t * 128:(t + 1) * 128], wqkv[i][:, 2 * D:3 * D],
                                      start=True, stop=False)
                            last = pe.matmul(Pa[h][:, t * D:(t + 1) * D], ones[:, :], brow[i][:, 2 * D:3 * D],
                                             start=False, stop=True)
                        last.then_inc(s["v"], 1)
                    for h in two:
                        pe.wait_ge(s["qn"], before + h + 1)
                        for t in range(TILES):
                            last = pe.transpose(Pb[h][:, t * 128:(t + 1) * 128], qs[h][:, t * 128:(t + 1) * 128], ident[:, :])
                        last.then_inc(s["qnt"], 1)
                    for h in two:
                        pe.wait_ge(s["vk"], before + h + 1)
                        for b in range(BH):
                            for t in (2 * b, 2 * b + 1):
                                one, other = (vk[h], ekT[h]) if i == 0 else (ekT[h], vk[h])
                                last = pe.matmul(Pa[h][:, b * D:(b + 1) * D], one[:, t * D:(t + 1) * D],
                                                 other[:, t * D:(t + 1) * D], start=(t == 2 * b), stop=(t == 2 * b + 1))
                        last.then_inc(s["att"], 1)
                    for h in two:
                        pe.wait_ge(s["attm"], before + h + 1)
                        for b in range(BH):
                            last = pe.matmul(Pa[h][:, BANK + b * D:BANK + (b + 1) * D], attm[h][:, b * D:(b + 1) * D],
                                             center[:, :], start=True, stop=True)
                        last.then_inc(s["attc"], 1)
                    for h in two:
                        pe.wait_ge(s["attcr"], before + h + 1)
                        pe.wait_ge(s["qtc"], before + h + 1)
                        for b in range(BH):
                            last = pe.matmul(Pa[h][:, b * T:(b + 1) * T], attc[h][:, b * D:(b + 1) * D],
                                             qT[h][:, b * T:(b + 1) * T], start=True, stop=True)
                        last.then_inc(s["y"], 1)
                    for h in two:
                        pe.wait_ge(s["sq2"], before + h + 1)
                        wide(Pb[h], mean[:, :], tmp[h], s["var2"])
                    for h in two:
                        pe.wait_ge(s["hs"], before + h + 1)
                        wide(Pb[h], mat("out" + name), hs[h], s["o"])

                @block.scalar
                def _(act):
                    for h in two:
                        act.wait_ge(s["mean1"], before + h + 1)
                        act.activation(tmp[h][:, :], Pa[h][:, :], ACT.Square).then_inc(s["sq1"], 1)
                    for h in two:
                        act.wait_ge(s["var1"], before + h + 1)
                        act.activation(tmp[h][:, :], Pb[h][:, :], ACT.Ln, bias=eps[:, :]).then_inc(s["lnv1"], 1)
                        act.wait_ge(s["lnv1"], before + h + 1)
                        act.activation(rstd[h][:, :], tmp[h][:, :], ACT.Exp, scale=-0.5).then_inc(s["rstd1"], 1)
                    for h in two:
                        act.wait_ge(s["knb"], before + h + 1)
                        for b in range(BH):
                            act.activation(ek[h][:, b * T:(b + 1) * T], Pa[h][:, b * T:(b + 1) * T], ACT.Exp,
                                           bias=knb[h][:, b:b + 1], accum_out=ksum[h][:, b:b + 1]).then_inc(s["ek"], 1)
                    for h in two:
                        act.wait_ge(s["qs"], before + h + 1)
                        act.activation(qs[h][:, :], qs[h][:, :], ACT.Exp).then_inc(s["eq"], 1)
                    for h in two:
                        act.wait_ge(s["ekt"], before + h + 1)
                        act.activation(ekT[h][:, :], Pa[h][:, :], ACT.Copy).then_inc(s["ektc"], 1)
                    for h in two:
                        act.wait_ge(s["qnt"], before + h + 1)
                        act.activation(qT[h][:, :], Pb[h][:, :], ACT.Copy).then_inc(s["qtc"], 1)
                    for h in two:
                        act.wait_ge(s["y"], before + h + 1)
                        act.activation(tmp[h][:, :], Pa[h][:, :], ACT.Square).then_inc(s["sq2"], 1)
                    for h in two:
                        act.wait_ge(s["var2"], before + h + 1)
                        act.activation(tmp[h][:, :], Pb[h][:, :], ACT.Ln, bias=eps[:, :]).then_inc(s["lnv2"], 1)
                        act.wait_ge(s["lnv2"], before + h + 1)
                        act.activation(rstd[h][:, :], tmp[h][:, :], ACT.Exp, scale=-0.5).then_inc(s["rstd2"], 1)
                    for h in two:
                        act.wait_ge(s["h"], BH * (before + h + 1))
                        act.activation(he[h][:, :], hb[h][:, :], ACT.Tanh).then_inc(s["he"], 1)
                    act.preload_act_table_set(LOG_EXP)

                @block.vector
                def _(dve):
                    for h in two:
                        dve.wait_ge(s["rstd1"], before + h + 1)
                        dve.tensor_tensor(z[h][:, :], Pa[h][:, :], rstd[h][:, :], ALU.mult).then_inc(s["z"], 1)
                    for h in two:
                        dve.wait_ge(s["k"], before + h + 1)
                        dve.tensor_reduce(kmax[h][:, :], Pa[h][:, :].rearrange("p (b t) -> p b t", t=T), AX.X,
                                          ALU.max).then_inc(s["kmax"], 1)
                        dve.wait_ge(s["kmax"], before + h + 1)
                        dve.tensor_scalar(kbias[h][:, :], kmax[h][:, :], bfold[i][:, 1:2], None, ALU.add).then_inc(s["kbias"], 1)
                        dve.wait_ge(s["kbias"], before + h + 1)
                        dve.tensor_scalar(knb[h][:, :], kbias[h][:, :], -1.0, bfold[i][:, 1:2], ALU.mult,
                                          ALU.add).then_inc(s["knb"], 1)
                    for h in two:
                        dve.wait_ge(s["q"], before + h + 1)
                        qv = Pb[h][:, :].rearrange("p (g w) -> p g w", w=hw)
                        dve.tensor_reduce(qmax[h][:, :], qv, AX.X, ALU.max).then_inc(s["qmax"], 1)
                        dve.wait_ge(s["qmax"], before + h + 1)
                        dve.tensor_tensor(qs[h][:, :].rearrange("p (g w) -> p g w", w=hw), qv,
                                          qmax[h][:, :].unsqueeze(2).to_broadcast([128, TILES * heads, hw]),
                                          ALU.subtract).then_inc(s["qs"], 1)
                    for h in two:
                        dve.wait_ge(s["eq"], before + h + 1)
                        dve.tensor_reduce(qsum[h][:, :], qs[h][:, :].rearrange("p (g w) -> p g w", w=hw), AX.X,
                                          ALU.add).then_inc(s["qsum"], 1)
                        dve.wait_ge(s["qsum"], before + h + 1)
                        dve.reciprocal(rq[h][:, :], qsum[h][:, :]).then_inc(s["rq"], 1)
                    for h in two:
                        dve.wait_ge(s["v"], before + h + 1)
                        dve.tensor_tensor(vk[h][:, :].rearrange("p (t d) -> p t d", d=D),
                                          Pa[h][:, :].rearrange("p (t d) -> p t d", d=D),
                                          keep[i][:, h * TILES:(h + 1) * TILES].unsqueeze(2).to_broadcast([128, TILES, D]),
                                          ALU.mult).then_inc(s["vk"], 1)
                        dve.wait_ge(s["ek"], BH * (before + h + 1))
                        dve.reciprocal(rk[h][:, :], ksum[h][:, :]).then_inc(s["rk"], 1)
                    for h in two:
                        dve.wait_ge(s["att"], before + h + 1)
                        if i == 0:
                            dve.tensor_tensor(attm[h][:, :].rearrange("p (b d) -> p b d", d=D),
                                              Pa[h][:, 0:BH * D].rearrange("p (b d) -> p b d", d=D),
                                              blockmask[:, :].unsqueeze(1).to_broadcast([D, BH, D]),
                                              ALU.mult).then_inc(s["attm"], 1)
                        else:
                            dve.wait_ge(s["rk"], before + h + 1)
                            for b in range(BH):
                                last = dve.scalar_tensor_tensor(attm[h][:, b * D:(b + 1) * D], Pa[h][:, b * D:(b + 1) * D],
                                                                rk[h][:, b:b + 1], blockmask[:, :], ALU.mult, ALU.mult)
                            last.then_inc(s["attm"], 1)
                    for h in two:
                        dve.wait_ge(s["attc"], before + h + 1)
                        if i == 0:
                            dve.wait_ge(s["rk"], before + h + 1)
                            dve.tensor_tensor(attc[h][:, :].rearrange("p (b d) -> p b d", d=D),
                                              Pa[h][:, BANK:BANK + BH * D].rearrange("p (b d) -> p b d", d=D),
                                              rk[h][:, :].unsqueeze(2).to_broadcast([D, BH, D]),
                                              ALU.mult).then_inc(s["attcr"], 1)
                        else:
                            dve.tensor_copy(attc[h][:, :], Pa[h][:, BANK:BANK + BH * D]).then_inc(s["attcr"], 1)
                    for h in two:
                        dve.wait_ge(s["rstd2"], before + h + 1)
                        dve.tensor_tensor(z[h][:, :], Pa[h][:, :], rstd[h][:, :], ALU.mult).then_inc(s["z2"], 1)
                    for h in two:
                        dve.wait_ge(s["he"], before + h + 1)
                        dve.scalar_tensor_tensor(hs[h][:, :], he[h][:, :], 1.0, hb[h][:, :], ALU.add,
                                                 ALU.mult).then_inc(s["hs"], 1)
                    for h in two:
                        dve.wait_ge(s["o"], before + h + 1)
                        dve.scalar_tensor_tensor(xT[:, toks(h)], Pb[h][:, :], col("bout" + name), xT[:, toks(h)],
                                                 ALU.add, ALU.add).then_inc(s["x"], 1)

                @block.gpsimd
                def _(pool):
                    for h in two:
                        pool.wait_ge(s["rq"], before + h + 1)
                        v = qs[h][:, :].rearrange("p (g w) -> p g w", w=hw)
                        pool.tensor_tensor(v, v, rq[h][:, :].unsqueeze(2).to_broadcast([128, TILES * heads, hw]),
                                           ALU.mult).then_inc(s["qn"], 1)
                    for h in two:
                        pool.wait_ge(s["z2"], before + h + 1)
                        for b in range(BH):
                            g = h * BH + b
                            pool.tensor_scalar(hb[h][:, b * T:(b + 1) * T], z[h][:, b * T:(b + 1) * T], film_s[i][:, g:g + 1],
                                               film_t[i][:, g:g + 1], ALU.mult, ALU.add).then_inc(s["h"], 1)

        def mamba_layer():
            with ExitStack() as keep2:
                u = [sb(f"u{c}", [128, N], f32, keep2) for c in range(CH)]
                zs = [sb(f"zs{c}", [128, N], f32, keep2) for c in range(CH)]
                dt = [sb(f"dt{c}", [128, N], f32, keep2) for c in range(CH)]
                dtu = [sb(f"dtu{c}", [128, N], f32, keep2) for c in range(CH)]
                bc = sb("bc", [128, N], bf16, keep2)
                sel = sb("sel", [128, 2 * NS, 128], bf16, keep2)
                acoef = sb("acoef", [128, CH * NS], f32, keep2)
                dskip = sb("dskip", [128, CH * 128], f32, keep2)
                mamba_projections(u, zs, dt, dtu, bc, sel, acoef, dskip)
                mamba_scan(u, zs, dt, dtu, bc, sel, acoef, dskip)

        def mamba_projections(u, zs, dt, dtu, bc, sel, acoef, dskip):
            with ExitStack() as on:
                names = ("mean", "sq", "var", "lnv", "rstd", "z", "xn", "u", "tu", "tu1", "us", "zp", "tz", "zs", "bcp", "bc1",
                         "r1", "bc2", "r2", "bc3", "dtr", "dtrc", "dtp", "ab", "eab", "lab", "mx", "dt", "dtu", "dtA",
                         "sel", "pad", "wb", "ws", "ea", "xbc", "conv", "cbh")
                s = {n: sem(f"m_{n}", on) for n in names}
                two = range(HALVES)

                def pair(n, shape, dt_=f32):
                    return [sb(f"m{n}_{h}", shape, dt_, on) for h in two]

                wb = sb("wb", [D, TAPS * DI], f32, on)
                wconv = sb("wconv", [D, TAPS * DI], f32, on)
                wz = sb("wz", [D, DI], f32, on)
                xbc3 = sb("xbc3", [D, CH * 128], f32, on)
                cbh = sb("cbh", [128, CH], f32, on)
                one = sb("one", [128, 1], f32, on)
                ea = sb("ea", [128, CH * NS], f32, on)
                tmp, rstd, z = pair("tmp", [D, NH]), pair("rstd", [D, NH]), pair("z", [D, NH])
                xp = pair("xp", [D, BH * (T + TAPS - 1)])
                dtr = pair("dtr", [RANK, NH])
                Pa = [ps(f"mPa_{h}", [128, NH], f32, on) for h in two]
                Pb = [ps(f"mPb_{h}", [128, NH], f32, on) for h in two]
                P = [[Pa[h], Pb[h]] for h in two]

                def toks(h):
                    return slice(h * NH, (h + 1) * NH)

                def padded(h):
                    return xp[h][:, :].rearrange("p (b t) -> p b t", t=T + TAPS - 1)

                block = on.enter_context(nc.Block())

                @block.sync
                def _(sp):
                    sp.dma_start(wb[:, :], a_convt.to_broadcast([D, TAPS * DI])).then_inc(s["wb"], 16)
                    sp.wait_ge(s["wb"], 16)

                @block.gpsimd
                def _(pool):
                    for h in two:
                        pool.memset(padded(h)[:, :, 0:TAPS - 1], 0.0).then_inc(s["pad"], 1)
                    pool.memset(one[:, :], 1.0).then_inc(s["pad"], 1)
                    pool.memset(xbc3[:, :], 0.0).then_inc(s["pad"], 1)
                    pool.wait_ge(s["pad"], 4)
                    for c in range(CH):
                        for at in (0, 64, 96):
                            pool.tensor_copy(xbc3[:, c * 128 + at:c * 128 + at + 2 * NS], mat("xbc", c, 2 * NS)).then_inc(s["xbc"], 1)
                    for h in two:
                        pool.wait_ge(s["z"], h + 1)
                        for b in range(BH):
                            g = h * BH + b
                            pool.tensor_scalar(padded(h)[:, b, TAPS - 1:], z[h][:, b * T:(b + 1) * T], film_s[3][:, g:g + 1],
                                               film_t[3][:, g:g + 1], ALU.mult, ALU.add).then_inc(s["xn"], 1)
                    for h in two:
                        for c in range(CH):
                            pool.wait_ge(s["tu"], h * CH + c + 1)
                            pool.tensor_scalar(u[c][:, toks(h)], u[c][:, toks(h)], 1.0, 1.0, ALU.add,
                                               ALU.mult).then_inc(s["tu1"], 1)
                    pool.memset(sel[:, :, :], 0.0).then_inc(s["sel"], 1)
                    for j, at in enumerate((0, 64, 96)):
                        pool.wait_ge(s["sel"], j + 1)
                        pool.affine_select(out=sel[:, :, :], in_=sel[:, :, :], compare_op=ALU.not_equal, fill=1.0, base=-at,
                                           pattern=[[-1, 2 * NS], [0, 128]], channel_multiplier=1).then_inc(s["sel"], 1)
                    for h in two:
                        for c in range(CH):
                            k = h * CH + c + 1
                            pool.wait_ge(s["lab"], k)
                            pool.wait_ge(s["mx"], k)
                            pool.tensor_tensor(dt[c][:, toks(h)], dt[c][:, toks(h)], dtu[c][:, toks(h)], ALU.add).then_inc(s["dt"], 1)
                            pool.wait_ge(s["dt"], k)
                            pool.tensor_tensor(dtu[c][:, toks(h)], dt[c][:, toks(h)], u[c][:, toks(h)], ALU.mult).then_inc(s["dtu"], 1)
                            pool.wait_ge(s["dtu"], k)
                            pool.memset(dt[c][:, toks(h)].rearrange("p (b t) -> p b t", t=T)[:, :, 0:1], 1e37).then_inc(s["dtA"], 1)

                @block.tensor
                def _(pe):
                    def wide(out_, lhsT, rhs, start=True, stop=True):
                        for c in range(0, NH, BANK):
                            last = pe.matmul(out_[:, c:c + BANK], lhsT, rhs[:, c:c + BANK], start=start, stop=stop)
                        return last

                    for h in two:
                        wide(Pa[h], center[:, :], xT[:, toks(h)]).then_inc(s["mean"], 1)
                    for h in two:
                        pe.wait_ge(s["sq"], h + 1)
                        wide(Pb[h], mean[:, :], tmp[h]).then_inc(s["var"], 1)
                    pe.wait_ge(s["conv"], TAPS)
                    pe.wait_ge(s["pad"], 4)
                    for h in two:
                        pe.wait_ge(s["xn"], BH * (h + 1))
                        for c in range(CH):
                            for k2 in range(0, BH, 2):
                                for k in range(TAPS):
                                    last = pe.matmul(P[h][c][:, k2 * T:(k2 + 2) * T],
                                                     wconv[:, k * DI + c * 128:k * DI + (c + 1) * 128],
                                                     padded(h)[:, k2:k2 + 2, k:k + T], start=(k == 0), stop=(k == TAPS - 1))
                            last.then_inc(s["u"], 1)
                    pe.wait_ge(s["ws"], 1)
                    for h in two:
                        for c in range(CH):
                            pe.wait_ge(s["us"], h * CH + c + 1)
                            for k2 in range(0, BH, 2):
                                last = pe.matmul(P[h][c][:, k2 * T:(k2 + 2) * T], wz[:, c * 128:(c + 1) * 128],
                                                 padded(h)[:, k2:k2 + 2, TAPS - 1:], start=True, stop=True)
                            last.then_inc(s["zp"], 1)
                    pe.wait_ge(s["xbc"], 3 * CH)
                    for h in two:
                        pe.wait_ge(s["zs"], CH * h + 1)
                        for k in range(0, NH, BANK):
                            for c in range(CH):
                                last = pe.matmul(Pa[h][0:RANK, k:k + BANK], mat("xdt", c, RANK),
                                                 u[c][:, h * NH + k:h * NH + k + BANK], start=(c == 0), stop=(c == CH - 1))
                        last.then_inc(s["dtr"], 1)
                        pe.wait_ge(s["zs"], CH * h + 2)
                        for k in range(0, NH, BANK):
                            for c in range(CH):
                                last = pe.matmul(Pb[h][:, k:k + BANK], xbc3[:, c * 128:(c + 1) * 128],
                                                 u[c][:, h * NH + k:h * NH + k + BANK], start=(c == 0), stop=(c == CH - 1))
                        last.then_inc(s["bcp"], 1)
                    for h in two:
                        for c in range(CH):
                            pe.wait_ge(s["dtrc"] if c == 0 else s["r1"], h + 1)
                            for k in range(0, NH, BANK):
                                last = pe.matmul(P[h][c][:, k:k + BANK], dtp[:, c * 128:(c + 1) * 128], dtr[h][:, k:k + BANK],
                                                 start=True, stop=True)
                            last.then_inc(s["dtp"], 1)

                @block.scalar
                def _(act):
                    for h in two:
                        act.wait_ge(s["mean"], h + 1)
                        act.activation(tmp[h][:, :], Pa[h][:, :], ACT.Square).then_inc(s["sq"], 1)
                    act.activation(ea[:, :], mat("alog"), ACT.Exp).then_inc(s["ea"], 1)
                    for h in two:
                        act.wait_ge(s["var"], h + 1)
                        act.activation(tmp[h][:, :], Pb[h][:, :], ACT.Ln, bias=eps[:, :]).then_inc(s["lnv"], 1)
                        act.wait_ge(s["lnv"], h + 1)
                        act.activation(rstd[h][:, :], tmp[h][:, :], ACT.Exp, scale=-0.5).then_inc(s["rstd"], 1)
                    act.wait_ge(s["cbh"], CH)
                    for h in two:
                        for c in range(CH):
                            act.wait_ge(s["u"], h * CH + c + 1)
                            act.activation(u[c][:, toks(h)], P[h][c][:, :], ACT.Tanh, bias=cbh[:, c:c + 1]).then_inc(s["tu"], 1)
                    for h in two:
                        for c in range(CH):
                            act.wait_ge(s["zp"], h * CH + c + 1)
                            act.activation(zs[c][:, toks(h)], P[h][c][:, :], ACT.Tanh).then_inc(s["tz"], 1)
                    act.preload_act_table_set(LOG_EXP)
                    for h in two:
                        act.wait_ge(s["dtr"], h + 1)
                        act.activation(dtr[h][:, :], Pa[h][0:RANK, :], ACT.Copy).then_inc(s["dtrc"], 1)
                    for h in two:
                        for c in range(CH):
                            k = h * CH + c + 1
                            act.wait_ge(s["dtp"], k)
                            act.activation(dt[c][:, toks(h)], P[h][c][:, :], ACT.Abs, bias=col(f"dtb_{c}")).then_inc(s["ab"], 1)
                            act.wait_ge(s["ab"], k)
                            act.activation(dt[c][:, toks(h)], dt[c][:, toks(h)], ACT.Exp, scale=-1.0).then_inc(s["eab"], 1)
                            act.wait_ge(s["eab"], k)
                            act.activation(dt[c][:, toks(h)], dt[c][:, toks(h)], ACT.Ln, bias=one[:, :]).then_inc(s["lab"], 1)

                @block.vector
                def _(dve):
                    for c in range(CH):
                        dve.tensor_scalar(cbh[:, c:c + 1], col(f"convb_{c}"), 0.5, None, ALU.mult).then_inc(s["cbh"], 1)
                        dve.tensor_scalar(dskip[:, c * 128:(c + 1) * 128], ident[:, :], col(f"dp_{c}"), None, ALU.mult)
                    dve.tensor_scalar(wz[:, :], mat("inp")[:, DI:2 * DI], 0.5, None, ALU.mult).then_inc(s["ws"], 1)
                    dve.wait_ge(s["wb"], 16)
                    for k in range(TAPS):
                        dve.scalar_tensor_tensor(wconv[:, k * DI:(k + 1) * DI], wb[:, k * DI:(k + 1) * DI], 0.5,
                                                 mat("inp")[:, 0:DI], ALU.mult, ALU.mult).then_inc(s["conv"], 1)
                    dve.wait_ge(s["ea"], 1)
                    dve.tensor_scalar(acoef[:, :], ea[:, :], -1.0, -1e-35, ALU.mult, ALU.min).then_inc(s["ws"], 1)
                    for h in two:
                        dve.wait_ge(s["rstd"], h + 1)
                        dve.tensor_tensor(z[h][:, :], Pa[h][:, :], rstd[h][:, :], ALU.mult).then_inc(s["z"], 1)
                    dve.wait_ge(s["cbh"], CH)
                    for h in two:
                        for c in range(CH):
                            dve.wait_ge(s["tu1"], h * CH + c + 1)
                            dve.scalar_tensor_tensor(u[c][:, toks(h)], P[h][c][:, :], cbh[:, c:c + 1], u[c][:, toks(h)],
                                                     ALU.add, ALU.mult).then_inc(s["us"], 1)
                    for h in two:
                        for c in range(CH):
                            dve.wait_ge(s["tz"], h * CH + c + 1)
                            dve.scalar_tensor_tensor(zs[c][:, toks(h)], zs[c][:, toks(h)], 1.0, P[h][c][:, :], ALU.add,
                                                     ALU.mult).then_inc(s["zs"], 1)
                    for h in two:
                        k = h + 1
                        dve.wait_ge(s["bcp"], k)
                        dve.tensor_copy(bc[:, toks(h)], Pb[h][:, :]).then_inc(s["bc1"], 1)
                        dve.wait_ge(s["bc1"], k)
                        dve.tensor_tensor(tmp[h][64:128, :], Pb[h][64:128, :], bc[64:128, toks(h)], ALU.subtract).then_inc(s["r1"], 1)
                        dve.wait_ge(s["r1"], k)
                        dve.tensor_copy(bc[64:128, toks(h)], tmp[h][64:128, :]).then_inc(s["bc2"], 1)
                        dve.wait_ge(s["bc2"], k)
                        dve.tensor_tensor(tmp[h][96:128, :], tmp[h][96:128, :], bc[96:128, toks(h)], ALU.subtract).then_inc(s["r2"], 1)
                        dve.wait_ge(s["r2"], k)
                        dve.tensor_copy(bc[96:128, toks(h)], tmp[h][96:128, :]).then_inc(s["bc3"], 1)
                    for h in two:
                        for c in range(CH):
                            dve.wait_ge(s["ab"], h * CH + c + 1)
                            dve.tensor_scalar(dtu[c][:, toks(h)], P[h][c][:, :], col(f"dtb_{c}"), 0.0, ALU.add,
                                              ALU.max).then_inc(s["mx"], 1)

        def mamba_scan(u, zs, dt, dtu, bc, sel, acoef, dskip):
            with ExitStack() as on:
                (s_b, s_c, s_dA, s_bu, s_h, s_ccopy, s_hc, s_y, s_ym, s_skip, s_o, s_x) = (
                    sem(f"v_{n}", on) for n in "b c dA bu h ccopy hc y ym skip o x".split())

                def twice(n):
                    return [[sb(f"{n}{p}_{c}", [128, NH], f32, on) for c in range(CH)] for p in range(2)]

                dA, bu, hst, hc = twice("dA"), twice("bu"), twice("hst"), twice("hc")
                cs = [sb(f"cs{p}", [128, NH], f32, on) for p in range(2)]
                ym = u
                Pbb, Pcb = ps("Pbb", [128, NH], f32, on), ps("Pcb", [128, NH], f32, on)
                Py = [ps(f"Py{c}", [128, NH], f32, on) for c in range(CH)]
                two = range(HALVES)

                def toks(h):
                    return slice(h * NH, (h + 1) * NH)

                def steps(eng, h, one):
                    for p in range(2):
                        one(p, h * NS + p, p, h == 0, False, p == 0)
                    with eng.Fori(2, NS - 2, 2) as n:
                        for p in range(2):
                            one(n + p, n + (h * NS + p), p, False, False, False)
                    for p in range(2):
                        one(NS - 2 + p, h * NS + NS - 2 + p, p, False, p == 1, False)

                block = on.enter_context(nc.Block())

                @block.tensor
                def _(pe):
                    def spread(out_, which, n, h, signal):
                        for k in range(0, NH, BANK):
                            last = pe.matmul(out_[:, k:k + BANK], sel[:, bass.ds(n + which * NS, 1), :],
                                             bc[:, h * NH + k:h * NH + k + BANK], start=True, stop=True)
                        last.then_inc(signal, 1)

                    def add_up(at, parity):
                        for c in range(CH):
                            pe.wait_ge(s_hc, at * CH + c + 1)
                            for k in range(0, NH, BANK):
                                last = pe.matmul(Py[c][:, k:k + BANK], ident[:, :], hc[parity][c][:, k:k + BANK], start=False,
                                                 stop=True, skip_group_check=True)
                            last.then_inc(s_y, 1)

                    def reduce(n, at, parity, first, last_of_half, first_of_half):
                        if not last_of_half:
                            pe.wait_ge(s_bu, (at + 1) * CH)
                            spread(Pbb, 0, n + 1, half[0], s_b)
                            pe.wait_ge(s_ccopy, at + 1)
                            spread(Pcb, 1, n + 1, half[0], s_c)
                        if not first_of_half:
                            add_up(at - 1, 1 - parity)

                    half = [0]
                    for h in two:
                        half[0] = h
                        if h:
                            pe.wait_ge(s_bu, h * NS * CH)
                            pe.wait_ge(s_ccopy, h * NS)
                            pe.wait_ge(s_ym, h * CH)
                        spread(Pbb, 0, 0, h, s_b)
                        spread(Pcb, 1, 0, h, s_c)
                        for c in range(CH):
                            for k in range(0, NH, BANK):
                                pe.matmul(Py[c][:, k:k + BANK], dskip[:, c * 128:(c + 1) * 128],
                                          u[c][:, h * NH + k:h * NH + k + BANK], start=True, stop=True, skip_group_check=True)
                        steps(pe, h, reduce)
                        add_up((h + 1) * NS - 1, 1)
                    for h in two:
                        P = (Pbb, Pcb)[h]
                        pe.wait_ge(s_ym, (h + 1) * CH)
                        for k in range(0, NH, BANK):
                            for c in range(CH):
                                last = pe.matmul(P[:, k:k + BANK], mat("outp", c, 128), ym[c][:, h * NH + k:h * NH + k + BANK],
                                                 start=(c == 0), stop=(c == CH - 1))
                        last.then_inc(s_o, 1)

                @block.scalar
                def _(act):
                    def decay(n, at, parity, first, *_):
                        for c in range(CH):
                            if not first:
                                act.wait_ge(s_h, (at - 2) * CH + c + 1)
                            act.activation(dA[parity][c][:, :], dt[c][:, toks(half[0])], ACT.Exp,
                                           scale=acoef[:, bass.ds(n + c * NS, 1)]).then_inc(s_dA, 1)
                        act.wait_ge(s_c, at + 1)
                        if not first:
                            act.wait_ge(s_hc, (at - 1) * CH)
                        act.activation(cs[parity][:, :], Pcb[:, :], ACT.Copy).then_inc(s_ccopy, 1)

                    half = [0]
                    for h in two:
                        half[0] = h
                        steps(act, h, decay)

                @block.vector
                def _(dve):
                    def scan(n, at, parity, first, *_):
                        dve.wait_ge(s_b, at + 1)
                        for c in range(CH):
                            if not first:
                                dve.wait_ge(s_h, (at - 2) * CH + c + 1)
                            dve.tensor_tensor(bu[parity][c][:, :], dtu[c][:, toks(half[0])], Pbb[:, :], ALU.mult).then_inc(s_bu, 1)
                        for c in range(CH):
                            dve.wait_ge(s_dA, at * CH + c + 1)
                            dve.wait_ge(s_bu, at * CH + c + 1)
                            if not first:
                                dve.wait_ge(s_hc, (at - 2) * CH + c + 1)
                            dve.tensor_tensor_scan(hst[parity][c][:, :], dA[parity][c][:, :], bu[parity][c][:, :], 0.0,
                                                   ALU.mult, ALU.add).then_inc(s_h, 1)

                    half = [0]
                    for h in two:
                        half[0] = h
                        steps(dve, h, scan)
                        for c in range(CH):
                            dve.wait_ge(s_y, ((h + 1) * NS - 1) * CH + c + 1)
                            dve.tensor_tensor(ym[c][:, toks(h)], Py[c][:, :], zs[c][:, toks(h)], ALU.mult).then_inc(s_ym, 1)
                    for h in two:
                        dve.wait_ge(s_o, h + 1)
                        for b in range(BH):
                            xb = xT[:, (h * BH + b) * T:(h * BH + b + 1) * T]
                            dve.scalar_tensor_tensor(xb, (Pbb, Pcb)[h][:, b * T:(b + 1) * T],
                                                     gate[:, h * BH + b:h * BH + b + 1], xb, ALU.mult, ALU.add).then_inc(s_x, 1)

                @block.gpsimd
                def _(pool):
                    def times_c(n, at, parity, first, *_):
                        pool.wait_ge(s_ccopy, at + 1)
                        for c in range(CH):
                            pool.wait_ge(s_h, at * CH + c + 1)
                            if not first:
                                pool.wait_ge(s_y, (at - 2) * CH + c + 1)
                            pool.tensor_tensor(hc[parity][c][:, :], hst[parity][c][:, :], cs[parity][:, :],
                                               ALU.mult).then_inc(s_hc, 1)

                    for h in two:
                        steps(pool, h, times_c)

        H3 = HEADS[2]
        W3 = D // H3
        QPARTS, KPARTS = (0, 0, 0, 1, 1, 2), (0, 1, 2, 0, 1, 0)
        MASK_AT, MAX_AT = 64, 96
        KMAX, KEXP = MASK_AT + 3, MAX_AT + 3
        VW = 32

        def softmax_layer():
            with ExitStack() as keep3:
                q_parts = nc.dram_tensor("q_parts", (B, 3, W3, H3, T), bf16, kind="Internal").ap()
                k_parts = nc.dram_tensor("k_parts", (B, 3, W3, H3, T), bf16, kind="Internal").ap()
                vc = sb("vc", [128, N // 128, D], f32, keep3)
                vs = [sb(f"vs{p}", [128, 2, H3, VW], f32, keep3) for p in range(2)]
                qst = [sb(f"qst{p}", [128, H3, T], bf16, keep3) for p in range(2)]
                kst = [sb(f"kst{p}", [128, H3, T], bf16, keep3) for p in range(2)]
                identb = sb("identb", [128, 128], bf16, keep3)
                yT = sb("yT", [D, N], f32, keep3)
                softmax_projections(q_parts, k_parts, vc, vs, qst, kst, identb)
                softmax_attention(q_parts, k_parts, vc, vs, qst, kst, identb, yT)
                softmax_output(yT)

        def softmax_projections(q_parts, k_parts, vc, vs, qst, kst, identb):
            with ExitStack() as on:
                names = ("mean", "sq", "var", "lnv", "rstd", "z", "q", "q1", "q2", "q3", "r1", "k", "k1", "k2", "k3", "kr1",
                         "v", "vk", "w", "zero", "ones", "identb")
                s = {n: sem(f"a_{n}", on) for n in names}
                two = range(HALVES)

                def pair(n, shape, dt_=f32):
                    return [sb(f"a{n}_{h}", shape, dt_, on) for h in two]

                tmp, rstd, z = pair("tmp", [D, NH]), pair("rstd", [D, NH]), pair("z", [D, NH])
                left = {"q": pair("lq", [D, NH]), "k": pair("lk", [D, NH])}
                part = {n: [sb(f"{n}part{j}", [D, N], bf16, on) for j in range(3)] for n in "qk"}
                Pa = [ps(f"aPa_{h}", [128, NH], f32, on) for h in two]
                Pb = [ps(f"aPb_{h}", [128, NH], f32, on) for h in two]

                def toks(h):
                    return slice(h * NH, (h + 1) * NH)

                block = on.enter_context(nc.Block())

                @block.sync
                def _(sp):
                    for h in two:
                        for n, dst in (("q", q_parts), ("k", k_parts)):
                            for j in range(3):
                                sp.wait_ge(s[f"{n}{j + 1}"], h + 1)
                                for b in range(h * BH, (h + 1) * BH):
                                    sp.dma_start(dst[b, j].rearrange("c h t -> h c t"),
                                                 part[n][j][:, b * T:(b + 1) * T]).then_inc(s["w"], 16)
                    sp.wait_ge(s["w"], 16 * 6 * B)

                @block.gpsimd
                def _(pool):
                    pool.tensor_copy(identb[:, :], ident[:, :]).then_inc(s["identb"], 1)
                    for p in range(2):
                        for st in (qst[p], kst[p]):
                            pool.memset(st[:, :, :].bitcast(f32), 0.0).then_inc(s["zero"], 1)
                        pool.memset(vs[p][:, :, :, :], 0.0).then_inc(s["zero"], 1)
                    pool.wait_ge(s["zero"], 6)
                    at = 0
                    for p in range(2):
                        for rows_of_ones in (qst[p][MASK_AT:KMAX, :, :], kst[p][MAX_AT:KEXP, :, :], vs[p][:, :, :, W3:W3 + 1]):
                            if at:
                                pool.wait_ge(s["ones"], at)
                            pool.memset(rows_of_ones, 1.0).then_inc(s["ones"], 1)
                            at += 1

                @block.tensor
                def _(pe):
                    def wide(out_, lhsT, rhs):
                        for c in range(0, NH, BANK):
                            last = pe.matmul(out_[:, c:c + BANK], lhsT, rhs[:, c:c + BANK], start=True, stop=True)
                        return last

                    for h in two:
                        wide(Pa[h], center[:, :], xT[:, toks(h)]).then_inc(s["mean"], 1)
                    for h in two:
                        pe.wait_ge(s["sq"], h + 1)
                        wide(Pb[h], mean[:, :], tmp[h]).then_inc(s["var"], 1)
                    for h in two:
                        pe.wait_ge(s["z"], h + 1)
                        wide(Pa[h], wqkv[2][:, 0:D], z[h]).then_inc(s["q"], 1)
                        pe.wait_ge(s["rstd"], h + 1)
                        wide(Pb[h], wqkv[2][:, D:2 * D], z[h]).then_inc(s["k"], 1)
                    for h in two:
                        pe.wait_ge(s["r1"], h + 1)
                        for t in range(TILES):
                            pe.matmul(Pa[h][:, t * D:(t + 1) * D], z[h][:, t * 128:(t + 1) * 128], wqkv[2][:, 2 * D:3 * D],
                                      start=True, stop=False)
                            last = pe.matmul(Pa[h][:, t * D:(t + 1) * D], ones[:, :], brow[2][:, 2 * D:3 * D],
                                             start=False, stop=True)
                        last.then_inc(s["v"], 1)

                @block.scalar
                def _(act):
                    for h in two:
                        act.wait_ge(s["mean"], h + 1)
                        act.activation(tmp[h][:, :], Pa[h][:, :], ACT.Square).then_inc(s["sq"], 1)
                    for h in two:
                        act.wait_ge(s["var"], h + 1)
                        act.activation(tmp[h][:, :], Pb[h][:, :], ACT.Ln, bias=eps[:, :]).then_inc(s["lnv"], 1)
                        act.wait_ge(s["lnv"], h + 1)
                        act.activation(rstd[h][:, :], tmp[h][:, :], ACT.Exp, scale=-0.5).then_inc(s["rstd"], 1)
                    qk = (("q", Pa, 0, "r1"), ("k", Pb, 1, "kr1"))
                    for h in two:
                        for n, P, bias, _ in qk:
                            act.wait_ge(s[n], h + 1)
                            act.activation(part[n][0][:, toks(h)], P[h][:, :], ACT.Identity,
                                           bias=bfold[2][:, bias:bias + 1]).then_inc(s[n + "1"], 1)
                        for n, _, _, r in qk:
                            act.wait_ge(s[r], h + 1)
                            act.activation(part[n][1][:, toks(h)], left[n][h][:, :], ACT.Copy).then_inc(s[n + "2"], 1)

                @block.vector
                def _(dve):
                    for h in two:
                        dve.wait_ge(s["rstd"], h + 1)
                        dve.tensor_tensor(z[h][:, :], Pa[h][:, :], rstd[h][:, :], ALU.mult).then_inc(s["z"], 1)
                    for h in two:
                        for n, P, bias, r in (("q", Pa, 0, "r1"), ("k", Pb, 1, "kr1")):
                            dve.wait_ge(s[n + "1"], h + 1)
                            dve.scalar_tensor_tensor(left[n][h][:, :], P[h][:, :], bfold[2][:, bias:bias + 1],
                                                     part[n][0][:, toks(h)], ALU.add, ALU.subtract).then_inc(s[r], 1)
                        for n in "qk":
                            dve.wait_ge(s[n + "2"], h + 1)
                            dve.tensor_tensor(part[n][2][:, toks(h)], left[n][h][:, :], part[n][1][:, toks(h)],
                                              ALU.subtract).then_inc(s[n + "3"], 1)
                    for h in two:
                        dve.wait_ge(s["v"], h + 1)
                        dve.tensor_tensor(vc[:, h * TILES:(h + 1) * TILES, :], Pa[h][:, :].rearrange("p (t d) -> p t d", d=D),
                                          keep[2][:, h * TILES:(h + 1) * TILES].unsqueeze(2).to_broadcast([128, TILES, D]),
                                          ALU.mult).then_inc(s["vk"], 1)

        def softmax_attention(q_parts, k_parts, vc, vs, qst, kst, identb, yT):
            PAIRS = H3 // 2
            AHEAD = (3, 3, 3, 3, 2, 2, 0, 0)
            HALF = H3 // 2
            LOADS = 16 * 7
            SETS = H3 // 4
            with ExitStack() as on:
                s_ld = [[sem(f"t_ld{p}_{i}", on) for i in range(2)] for p in range(2)]
                (s_vs, s_s1, s_mx, s_s2, s_e, s_pv, s_ev, s_t1, s_rc, s_t1d, s_t2, s_t2d, s_nm, s_nmc, s_np, s_nz, s_neg) = (
                    sem(f"t_{n}", on) for n in "vs s1 mx s2 e pv ev t1 rc t1d t2 t2d nm nmc np nz neg".split())
                E = [sb(f"E{p}", [128, 4, 2, T], f32, on) for p in range(2)]
                yraw = [sb(f"yraw{p}", [128, 4, T], f32, on) for p in range(2)]
                ytok = [sb(f"ytok{p}", [128, 2, D], f32, on) for p in range(2)]
                rec = [sb(f"rec{p}", [128, 2, H3], f32, on) for p in range(2)]
                mx = sb("mx", [128, H3, 2], f32, on)
                nleft = sb("nleft", [128, 2, H3], f32, on)
                nm = sb("nm", [128, 2, 128 // H3, H3], bf16, on)
                nmT = [sb(f"nmT{p}", [3 * H3, T], bf16, on) for p in range(2)]
                S1 = [ps(f"S1_{i}", [128, 2, T], f32, on) for i in range(2)]
                S2 = [ps(f"S2_{i}", [128, 2, 2, T], f32, on) for i in range(2)]
                PV = ps("PV", [128, 2, T], f32, on)
                Pm = ps("Pm", [128, BANK], f32, on)

                def steps(eng, body):
                    body(0, 0, True, False)
                    body(1, 1, False, False)
                    with eng.Fori(2, B - 3, 2) as b:
                        for p in range(2):
                            body(b + p, p, False, False)
                    body(B - 2, 0, False, False)
                    body(B - 1, 1, False, True)

                block = on.enter_context(nc.Block())

                @block.sync
                def _(sp):
                    def load(b, p, i):
                        heads = slice(i * HALF, (i + 1) * HALF)
                        one = bass.ds(b, 1)
                        at = 0
                        for j, times in ((0, 3), (1, 2), (2, 1)):
                            src = q_parts[one, j, :, heads, :].rearrange("o c h t -> o c (h t)")
                            sp.dma_start(qst[p][at:at + times * W3, heads, :],
                                         src.to_broadcast([times, W3, HALF * T])).then_inc(s_ld[p][i], 16)
                            at += times * W3
                        at = 0
                        for times in (3, 2, 1):
                            src = k_parts[one, 0:times, :, heads, :].rearrange("o j c h t -> (o j c) (h t)")
                            sp.dma_start(kst[p][at:at + times * W3, heads, :], src).then_inc(s_ld[p][i], 16)
                            at += times * W3
                        sp.dma_start(kst[p][MASK_AT:KMAX, heads, :], mrow[:, bass.ds(b * T + 2 * N, T)].unsqueeze(1).to_broadcast(
                            [3, HALF, T])).then_inc(s_ld[p][i], 16)

                    def maxima_rows(b, p):
                        sp.wait_ge(s_nmc, b + 1)
                        for j in range(3):
                            sp.dma_start(qst[p][MAX_AT + j:MAX_AT + j + 1, :, :],
                                         nmT[p][j * H3:(j + 1) * H3, :]).then_inc(s_neg, 16)

                    for p in range(2):
                        load(p, p, 0)
                        load(p, p, 1)
                    maxima_rows(0, 0)
                    with sp.Fori(2, B - 1, 2) as b:
                        for p in range(2):
                            sp.wait_ge(s_s2, (b + p) * PAIRS - 3 * PAIRS // 2)
                            load(b + p, p, 0)
                            maxima_rows(b + (p - 1), 1 - p)
                            sp.wait_ge(s_s2, (b + (p - 1)) * PAIRS)
                            load(b + p, p, 1)
                    maxima_rows(B - 1, 1)
                    for p in range(2):
                        for i in range(2):
                            sp.wait_ge(s_ld[p][i], LOADS * B // 2)
                    sp.wait_ge(s_neg, 3 * 16 * B)

                @block.gpsimd
                def _(pool):
                    def copy_v(b, p):
                        pool.tensor_copy(vs[p][:, :, :, 0:W3], vc[:, bass.ds(b * 2, 2), :].rearrange(
                            "p t (h w) -> p t h w", w=W3)).then_inc(s_vs, 1)

                    for p in range(2):
                        copy_v(p, p)
                    with pool.Fori(2, B - 1, 2) as b:
                        for p in range(2):
                            pool.wait_ge(s_pv, (b + (p - 1)) * SETS)
                            copy_v(b + p, p)

                @block.tensor
                def _(pe):
                    def scores_for_max(at, h, p, wait):
                        if wait:
                            pe.wait_ge(s_mx, at * H3 + (h - 1))
                        for nt in range(2):
                            last = pe.matmul(S1[h % 2][:, nt, :], qst[p][0:KMAX, h, nt * 128:(nt + 1) * 128], kst[p][0:KMAX, h, :],
                                             start=True, stop=True)
                        last.then_inc(s_s1, 1)

                    def maxima_to_rows(at, free, value):
                        pe.wait_ge(s_np, (at + 1) * 4)
                        if free is not None:
                            pe.wait_ge(free, value)
                        for nt in range(2):
                            last = pe.transpose(Pm[:, nt * 64:(nt + 1) * 64].bitcast(bf16),
                                                nm[:, nt, :, :].rearrange("p a h -> p (a h)"), identb[:, :])
                        last.then_inc(s_nm, 1)

                    def times_v(b, st, p, first):
                        pe.wait_ge(s_e, b * PAIRS + (2 * st + 2))
                        if st == 0:
                            pe.wait_ge(s_vs, b + 1)
                            if not first:
                                pe.wait_ge(s_ev, b * 2)
                        if st == SETS // 2:
                            pe.wait_ge(s_ev, b * 2 + 1)
                        for mt in range(2):
                            for g in range(4):
                                last = pe.matmul(PV[32 * g:32 * g + VW, st % 2, :], vs[p][:, mt, 4 * st + g, :],
                                                 E[st % 2][:, g, mt, :], start=(mt == 0), stop=(mt == 1))
                        last.then_inc(s_pv, 1)

                    def to_tokens(b, p, nt, last=False):
                        if nt == 0:
                            pe.wait_ge(s_ev, b * 2 + 2)
                            if last:
                                pe.wait_ge(s_t2d, B - 1)
                            else:
                                pe.wait_ge(s_nmc, b + 2)
                        else:
                            pe.wait_ge(s_t1d, b * 2 + 1)
                        for st in range(4):
                            turned = pe.transpose(Pm[:, st * 128:(st + 1) * 128], yraw[p][:, st, nt * 128:(nt + 1) * 128], ident[:, :])
                        turned.then_inc(s_t1, 1)

                    def to_features(b, p):
                        pe.wait_ge(s_t1d, b * 2 + 2)
                        for nt in range(2):
                            last = pe.transpose(Pm[:, nt * 128:(nt + 1) * 128], ytok[p][:, nt, :], ident[:, :])
                        last.then_inc(s_t2, 1)

                    def body(b, p, first, last_of_all):
                        ahead = 0
                        for j in range(PAIRS):
                            if j == 0:
                                pe.wait_ge(s_neg, (b + 1) * 48)
                            if j >= 2 or not first:
                                pe.wait_ge(s_e, b * PAIRS + (j - 1))
                            for i in range(2):
                                h = 2 * j + i
                                for mt in range(2):
                                    last = pe.matmul(S2[j % 2][:, i, mt, :], kst[p][0:KEXP, h, mt * 128:(mt + 1) * 128],
                                                     qst[p][0:KEXP, h, :], start=True, stop=True)
                            last.then_inc(s_s2, 1)
                            if not last_of_all:
                                for h in range(ahead, ahead + AHEAD[j]):
                                    if h % HALF == 0:
                                        pe.wait_ge(s_ld[1 - p][h // HALF], (b + (2 + p)) * (LOADS // 2))
                                    scores_for_max(b + 1, h, 1 - p, True)
                                ahead += AHEAD[j]
                            if j == 0:
                                if not first:
                                    times_v(b - 1, SETS - 1, 1 - p, False)
                            elif j % 2 == 0:
                                times_v(b, j // 2 - 1, p, first)
                            if not first and j in (2, 3):
                                to_tokens(b - 1, 1 - p, j - 2)
                            if not first and j == 5:
                                to_features(b - 1, 1 - p)
                            if not last_of_all and j == 7:
                                if first:
                                    maxima_to_rows(b + 1, None, 0)
                                else:
                                    maxima_to_rows(b + 1, s_t2d, b)

                    for h in range(H3):
                        if h % HALF == 0:
                            pe.wait_ge(s_ld[0][h // HALF], LOADS)
                        scores_for_max(0, h, 0, h >= 2)
                    maxima_to_rows(0, None, 0)
                    steps(pe, body)
                    times_v(B - 1, SETS - 1, 1, False)
                    for nt in range(2):
                        to_tokens(B - 1, 1, nt, True)
                    to_features(B - 1, 1)

                @block.scalar
                def _(act):
                    def out_of_psum(b, p, half):
                        act.wait_ge(s_pv, b * SETS + (half + 1) * SETS // 2)
                        act.activation(yraw[p][:, 2 * half:2 * half + 2, :], PV[:, :, :], ACT.Copy).then_inc(s_ev, 1)

                    def body(b, p, first, last_of_all):
                        for j in range(PAIRS):
                            act.wait_ge(s_s2, b * PAIRS + (j + 1))
                            st = j // 2
                            if j % 2 == 0 and (st >= 2 or not first):
                                act.wait_ge(s_pv, b * SETS + (st - 1))
                            act.activation(E[st % 2][:, 2 * (j % 2):2 * (j % 2) + 2, :, :], S2[j % 2][:, :, :, :],
                                           ACT.Exp).then_inc(s_e, 1)
                            if j == 0 and not first:
                                out_of_psum(b - 1, 1 - p, 1)
                            if j == 4:
                                out_of_psum(b, p, 0)

                    steps(act, body)
                    out_of_psum(B - 1, 1, 1)

                @block.vector
                def _(dve):
                    def head_max(at, h):
                        dve.wait_ge(s_s1, at * H3 + (h + 1))
                        dve.tensor_reduce(mx[:, h, :], S1[h % 2][:, :, :], AX.X, ALU.max).then_inc(s_mx, 1)

                    def maxima_parts(at):
                        m = mx[:, :, :].rearrange("p h t -> p t h")
                        dve.wait_ge(s_mx, (at + 1) * H3)
                        dve.tensor_scalar(nm[:, :, 0, :], m, -1.0, None, ALU.mult).then_inc(s_np, 1)
                        dve.wait_ge(s_np, at * 4 + 1)
                        dve.scalar_tensor_tensor(nleft[:, :, :], m, -1.0, nm[:, :, 0, :], ALU.mult, ALU.subtract).then_inc(s_np, 1)
                        dve.wait_ge(s_np, at * 4 + 2)
                        dve.tensor_copy(nm[:, :, 1, :], nleft[:, :, :]).then_inc(s_np, 1)
                        dve.wait_ge(s_np, at * 4 + 3)
                        dve.tensor_tensor(nm[:, :, 2, :], nleft[:, :, :], nm[:, :, 1, :], ALU.subtract).then_inc(s_np, 1)

                    def rows_out(at, p):
                        dve.wait_ge(s_nm, at + 1)
                        if not isinstance(at, int) or at >= 2:
                            dve.wait_ge(s_neg, (at - 1) * 48)
                        dve.tensor_copy(nmT[p][:, :], Pm[0:3 * H3, 0:128].bitcast(bf16)).then_inc(s_nmc, 1)

                    def normalise(b, p, nt):
                        dve.wait_ge(s_t1, b * 2 + (nt + 1))
                        v = Pm[:, :].rearrange("p (h w) -> p h w", w=VW)
                        dve.reciprocal(rec[p][:, nt, :], v[:, :, W3]).then_inc(s_rc, 1)
                        dve.wait_ge(s_rc, b * 2 + (nt + 1))
                        dve.tensor_tensor(ytok[p][:, nt, :].rearrange("p (h w) -> p h w", w=W3), v[:, :, 0:W3],
                                          rec[p][:, nt, :].unsqueeze(2).to_broadcast([128, H3, W3]), ALU.mult).then_inc(s_t1d, 1)

                    def features_out(b):
                        dve.wait_ge(s_t2, b + 1)
                        dve.tensor_copy(yT[:, bass.ds(b * T, T)], Pm[:, 0:T]).then_inc(s_t2d, 1)

                    def body(b, p, first, last_of_all):
                        ahead = 0
                        for j in range(PAIRS):
                            if not last_of_all:
                                if j == 0:
                                    dve.wait_ge(s_np, (b + 1) * 4)
                                for h in range(ahead, ahead + AHEAD[j]):
                                    head_max(b + 1, h)
                                ahead += AHEAD[j]
                                if j == 5:
                                    maxima_parts(b + 1)
                            if not first and j in (2, 3):
                                normalise(b - 1, 1 - p, j - 2)
                            if not first and j == 5:
                                features_out(b - 1)
                            if not last_of_all and j == 7:
                                rows_out(b + 1, 1 - p)

                    dve.memset(nm[:, :, :, :], 0.0).then_inc(s_nz, 1)
                    for h in range(H3):
                        head_max(0, h)
                    dve.wait_ge(s_nz, 1)
                    maxima_parts(0)
                    rows_out(0, 0)
                    steps(dve, body)
                    for nt in range(2):
                        normalise(B - 1, 1, nt)
                    features_out(B - 1)

        def softmax_output(yT):
            with ExitStack() as on:
                s = s_layer
                before = 2 * HALVES
                s_stored = sem("s_stored", on)
                two = range(HALVES)

                def pair(n, shape):
                    return [sb(f"o{n}_{h}", shape, f32, on) for h in two]

                tmp, rstd, z, hb, he, hs = (pair(n, [D, NH]) for n in ("tmp", "rstd", "z", "hb", "he", "hs"))
                Pa = [ps(f"oPa_{h}", [128, NH], f32, on) for h in two]
                Pb = [ps(f"oPb_{h}", [128, NH], f32, on) for h in two]

                def toks(h):
                    return slice(h * NH, (h + 1) * NH)

                block = on.enter_context(nc.Block())

                @block.sync
                def _(sp):
                    for h in two:
                        sp.wait_ge(s["x"], before + h + 1)
                        sp.dma_start(out[:, toks(h)], xT[:, toks(h)]).then_inc(s_stored, 16)
                    sp.wait_ge(s_stored, 16 * HALVES)

                @block.tensor
                def _(pe):
                    def wide(out_, lhsT, rhs):
                        for c in range(0, NH, BANK):
                            last = pe.matmul(out_[:, c:c + BANK], lhsT, rhs[:, c:c + BANK], start=True, stop=True)
                        return last

                    for h in two:
                        wide(Pa[h], center[:, :], yT[:, toks(h)]).then_inc(s["mean1"], 1)
                    for h in two:
                        pe.wait_ge(s["sq2"], before + h + 1)
                        wide(Pb[h], mean[:, :], tmp[h]).then_inc(s["var2"], 1)
                    for h in two:
                        pe.wait_ge(s["hs"], before + h + 1)
                        wide(Pb[h], mat("out3"), hs[h]).then_inc(s["o"], 1)

                @block.scalar
                def _(act):
                    for h in two:
                        act.wait_ge(s["mean1"], before + h + 1)
                        act.activation(tmp[h][:, :], Pa[h][:, :], ACT.Square).then_inc(s["sq2"], 1)
                    for h in two:
                        act.wait_ge(s["var2"], before + h + 1)
                        act.activation(tmp[h][:, :], Pb[h][:, :], ACT.Ln, bias=eps[:, :]).then_inc(s["lnv2"], 1)
                        act.wait_ge(s["lnv2"], before + h + 1)
                        act.activation(rstd[h][:, :], tmp[h][:, :], ACT.Exp, scale=-0.5).then_inc(s["rstd2"], 1)
                    for h in two:
                        act.wait_ge(s["h"], BH * (before + h + 1))
                        act.activation(he[h][:, :], hb[h][:, :], ACT.Tanh).then_inc(s["he"], 1)

                @block.vector
                def _(dve):
                    for h in two:
                        dve.wait_ge(s["rstd2"], before + h + 1)
                        dve.tensor_tensor(z[h][:, :], Pa[h][:, :], rstd[h][:, :], ALU.mult).then_inc(s["z2"], 1)
                    for h in two:
                        dve.wait_ge(s["he"], before + h + 1)
                        dve.scalar_tensor_tensor(hs[h][:, :], he[h][:, :], 1.0, hb[h][:, :], ALU.add, ALU.mult).then_inc(s["hs"], 1)
                    for h in two:
                        dve.wait_ge(s["o"], before + h + 1)
                        dve.scalar_tensor_tensor(xT[:, toks(h)], Pb[h][:, :], col("bout3"), xT[:, toks(h)],
                                                 ALU.add, ALU.add).then_inc(s["x"], 1)

                @block.gpsimd
                def _(pool):
                    for h in two:
                        pool.wait_ge(s["z2"], before + h + 1)
                        for b in range(BH):
                            g = h * BH + b
                            pool.tensor_scalar(hb[h][:, b * T:(b + 1) * T], z[h][:, b * T:(b + 1) * T], film_s[2][:, g:g + 1],
                                               film_t[2][:, g:g + 1], ALU.mult, ALU.add).then_inc(s["h"], 1)

        for i in range(2):
            attention_layer(i)
        mamba_layer()
        softmax_layer()


def kernel(**inputs):
    import numpy as np
    import concourse.bacc as bacc
    from concourse import mybir
    from concourse.bass_utils import run_bass_kernel_spmd

    a = {k: np.asarray(v) for k, v in inputs.items()}
    names = {"0": ("L0_cond_", "Wq Wk Wv W_emb W_out ln_w ln_b bq bk bv b_emb ln2_w ln2_b b_out"),
             "1": ("L1_cond_", "Wq Wk Wv film_emb_W film_out_W norm_scale norm_bias bq bk bv film_emb_b "
                               "film_norm_scale film_norm_bias film_out_b"),
             "3": ("L3_cond_", "q_w k_w v_w emb_w out_w norm_w norm_b q_b k_b v_b emb_b sb_norm_w sb_norm_b out_b")}
    keys = ["q", "k", "v", "emb", "out", "lnw", "lnb", "bq", "bk", "bv", "bemb", "ln2w", "ln2b", "bout"]
    m = {}

    def halves(w):
        return np.concatenate([w[i:i + 128] for i in range(0, w.shape[0], 128)], axis=1)

    for n, (prefix, parts) in names.items():
        for key, part in zip(keys, parts.split()):
            m[key + n] = a[prefix + part]
        m["emb" + n] = halves(m["emb" + n])
        m["embs" + n], m["embt" + n] = m["bemb" + n][:D], m["bemb" + n][D:]
    p = "L2_cond_"
    m["ada"] = halves(a[p + "ada_w"].T)
    m["adat"], m["adas"], m["adag"] = a[p + "ada_b"].reshape(3, D)
    m["inp"] = a[p + "in_proj_w"].T
    xp = halves(a[p + "x_proj_w"].T).reshape(128, CH, RANK + 2 * NS)
    m["xdt"] = xp[:, :, :RANK].reshape(128, -1)
    m["xbc"] = xp[:, :, RANK:].reshape(128, -1)
    m["outp"] = halves(a[p + "out_proj_w"].T)
    m["alog"] = halves(a[p + "A_log"])
    m["convw"] = halves(a[p + "conv_w"])
    m["g2"], m["b2"] = a[p + "ln_g"], a[p + "ln_b"]
    for c in range(CH):
        for key, part in (("convb", "conv_b"), ("dtb", "dt_proj_b"), ("dp", "D_param")):
            m[f"{key}_{c}"] = a[p + part][c * 128:(c + 1) * 128]
    arrays = {
        "a_x": a["x"].reshape(N, D).T,
        "a_cond": halves(a["cond_2048"].T),
        "a_w0": np.concatenate([m[n] for n, _ in MATS0], axis=1),
        "a_w1": np.concatenate([m[n] for n, _ in MATS1], axis=1),
        "a_w2": np.concatenate([m[n] for n, _ in MATS2], axis=1),
        "a_dtp": a[p + "dt_proj_w"].T,
        "a_convt": a[p + "conv_w"].T.reshape(1, -1),
        "a_cols": np.stack([m[c] for c in COLS], axis=1),
        "a_rows": np.concatenate([m[r] for r in ROWS]).reshape(1, -1),
        "a_keep0": a["mask_BxSx1_fk1"].reshape(N // 128, 128),
        "a_mask1": a["mask_BxS_ik0"].reshape(N // 128, 128),
        "a_keep3": a["mask_BxS_ff1"].reshape(N // 128, 128),
    }
    nc = bacc.Bacc("TRN2", target_bir_lowering=False, num_devices=1)
    args = []
    for name in arrays:
        arrays[name] = np.ascontiguousarray(arrays[name])
        args.append(nc.dram_tensor(name, arrays[name].shape, mybir.dt.from_np(arrays[name].dtype),
                                   kind="ExternalInput").ap())
    args.append(nc.dram_tensor("out", (D, N), mybir.dt.float32, kind="ExternalOutput").ap())
    cond_seq_kernel(nc, *args)
    got = run_bass_kernel_spmd(nc, [arrays], core_ids=[0]).results[0]["out"]
    return np.ascontiguousarray(got.T).reshape(B, T, D)
```

```python
import concourse.bass as bass
from concourse import mybir
from contextlib import ExitStack

B, T, D, TE = 8, 256, 128, 256
N = B * T
HALVES = 2
NH = N // HALVES
BH = B // HALVES
TILES = NH // 128
BANK = 512
DI, NS, RANK, TAPS = 256, 16, 64, 4
CH = DI // 128
HEADS = (8, 16, 16)
EPS = 1e-5
LOG_EXP = "natural_log_exp_and_others"

MATS0 = [("q0", 128), ("k0", 128), ("v0", 128), ("emb0", 512), ("out0", 128)]
MATS1 = [("q1", 128), ("k1", 128), ("v1", 128), ("emb1", 512), ("out1", 128)]
MATS2 = [("ada", 768), ("inp", 512), ("xdt", 128), ("xbc", 64), ("outp", 256), ("alog", 32), ("convw", 8),
         ("q3", 128), ("k3", 128), ("v3", 128), ("emb3", 512), ("out3", 128)]
LAYER_COLS = ["lnw", "lnb", "bq", "bk", "embs", "embt", "ln2w", "ln2b", "bout"]
COLS = [c + i for i in "013" for c in LAYER_COLS] + [
    "g2", "b2", "adat", "adas", "adag", "convb_0", "convb_1", "dtb_0", "dtb_1", "dp_0", "dp_1"]
ROWS = ["bq0", "bv0", "bq1", "bv1", "bv3"]


def offsets(mats):
    at, out = 0, {}
    for name, width in mats:
        out[name] = (at, width)
        at += width
    return out, at


def cond_seq_kernel(nc, a_x, a_cond, a_w0, a_w1, a_w2, a_dtp, a_cols, a_rows, a_keep0, a_mask1, a_keep3,
                    out):
    f32, bf16, i32 = mybir.dt.float32, mybir.dt.bfloat16, mybir.dt.int32
    ALU, ACT, AX = mybir.AluOpType, mybir.ActivationFunctionType, mybir.AxisListType

    ctx = ExitStack()
    with ctx:
        def sb(name, shape, dt=f32, on=ctx):
            return on.enter_context(nc.sbuf_tensor(name, shape, dt))

        def ps(name, shape, dt=f32, on=ctx):
            return on.enter_context(nc.psum_tensor(name, shape, dt))

        def sem(name, on=ctx):
            return on.enter_context(nc.semaphore(name))

        xT = sb("xT", [D, N])
        off0, n0 = offsets(MATS0)
        off1, n1 = offsets(MATS1)
        off2, n2 = offsets(MATS2)
        w0, w1, w2 = sb("w0", [D, n0]), sb("w1", [D, n1]), sb("w2", [D, n2])
        dtp = sb("dtp", [RANK, DI])
        cols = sb("cols", [D, len(COLS)])
        rows = sb("rows", [1, len(ROWS) * 128])
        cond = sb("cond", [D, 2 * B])

        def mat(name, i=0, n=None):
            for w, off in ((w0, off0), (w1, off1), (w2, off2)):
                if name in off:
                    at, width = off[name]
                    n = n or width
                    return w[:, at + i * n:at + (i + 1) * n]
            raise KeyError(name)

        def col(name):
            c = COLS.index(name)
            return cols[:, c:c + 1]

        def row(name):
            c = ROWS.index(name) * 128
            return rows[0:1, c:c + 128]

        center = sb("center", [D, D])
        mean = sb("mean", [D, D])
        ident = sb("ident", [D, D])
        ones = sb("ones", [3, 128], bf16)
        heads0, heads1 = sb("heads0", [D, D]), sb("heads1", [D, D])
        eps = sb("eps", [D, 1])
        wqkv = [sb(f"wqkv{i}", [D, 3 * D]) for i in range(3)]
        bfold = [sb(f"bfold{i}", [D, 2]) for i in range(3)]
        brow = [sb(f"brow{i}", [3, 3 * D], bf16) for i in range(3)]
        mrow = sb("mrow", [3, 3 * N], bf16)
        film_s = [sb(f"film_s{i}", [D, B]) for i in range(4)]
        film_t = [sb(f"film_t{i}", [D, B]) for i in range(4)]
        gate = sb("gate", [D, B])
        keep = [sb(f"keep{i}", [128, N // 128]) for i in range(3)]
        semb = sb("semb", [D, 2 * B])

        with ExitStack() as on:
            s_cols, s_w0, s_w1, s_w2, s_x = (sem(n, on) for n in ("s_cols", "s_w0", "s_w1", "s_w2", "s_x"))
            s_m = sem("s_m", on)
            s_cst, s_pool, s_dve = sem("s_cst", on), sem("s_pool", on), sem("s_dve", on)
            s_ce, s_semb, s_fold, s_folded = (sem(n, on) for n in ("s_ce", "s_semb", "s_fold", "s_folded"))
            s_keepT = sem("s_keepT", on)
            ce, ce1, cr = (sb(n, [D, 2 * B], f32, on) for n in ("ce", "ce1", "cr"))
            m0, m3 = sb("m0", [N // 128, 128], f32, on), sb("m3", [N // 128, 128], f32, on)
            m1i, m1 = sb("m1i", [N // 128, 128], i32, on), sb("m1", [N // 128, 128], f32, on)
            madd = sb("madd", [N // 128, 3 * 128], f32, on)
            mleft = sb("mleft", [N // 128, 3 * 128], f32, on)
            mpart = [sb(f"mpart{j}", [N // 128, 3 * 128], bf16, on) for j in range(3)]
            brow32, bleft = sb("brow32", [1, 9 * D], f32, on), sb("bleft", [1, 9 * D], f32, on)
            bpart = [sb(f"bpart{j}", [1, 9 * D], bf16, on) for j in range(3)]
            s_mpart, s_bpart, s_rows = sem("s_mpart", on), sem("s_bpart", on), sem("s_rows", on)
            sc1, sh = sb("sc1", [D, 4 * B], f32, on), sb("sh", [D, 4 * B], f32, on)
            Pcol = [ps(f"Pcol{i}", [D, BANK], f32, on) for i in range(4)]
            Pemb = [p[:, 0:3 * B] for p in Pcol]
            Pbias = [p[:, 4 * B:4 * B + 2] for p in Pcol]
            Prow = [ps(f"Prow{i}", [128, BANK], f32, on) for i in range(3)]
            Pkeep = ps("Pkeep", [128, BANK], f32, on)

            block = on.enter_context(nc.Block())

            @block.sync
            def _(sp):
                sp.dma_start(cols[:, :], a_cols).then_inc(s_cols, 16)
                sp.dma_start(cond[:, :], a_cond).then_inc(s_cols, 16)
                sp.dma_start(rows[:, :], a_rows).then_inc(s_cols, 16)
                sp.dma_start(w0[:, :], a_w0).then_inc(s_w0, 16)
                sp.dma_start(xT[:, :], a_x).then_inc(s_x, 16)
                sp.dma_start(w1[:, :], a_w1).then_inc(s_w1, 16)
                sp.dma_start(w2[:, :], a_w2).then_inc(s_w2, 16)
                sp.dma_start(dtp[:, :], a_dtp).then_inc(s_w2, 16)
                sp.wait_ge(s_mpart, 1)
                for j in range(3):
                    for i in range(3):
                        sp.dma_start(mrow[j:j + 1, i * N:(i + 1) * N].rearrange("p (a b) -> p a b", b=128),
                                     mpart[j][:, i * 128:(i + 1) * 128]).then_inc(s_rows, 16)
                for i in range(3):
                    sp.wait_ge(s_bpart, i + 1)
                    for j in range(3):
                        sp.dma_start(brow[i][j:j + 1, :], bpart[j][:, i * 3 * D:(i + 1) * 3 * D]).then_inc(s_rows, 16)
                sp.wait_ge(s_rows, 16 * 18)
                sp.wait_ge(s_x, 16)
                sp.wait_ge(s_w2, 32)

            @block.gpsimd
            def _(pool):
                pool.memset(center[:, :], -1.0 / D).then_inc(s_pool, 1)
                pool.memset(ident[:, :], 0.0).then_inc(s_pool, 1)
                pool.memset(heads0[:, :], 1.0).then_inc(s_pool, 1)
                pool.memset(heads1[:, :], 1.0).then_inc(s_pool, 1)
                pool.memset(mean[:, :], 1.0 / D).then_inc(s_cst, 1)
                pool.memset(ones[:, :], 1.0).then_inc(s_cst, 1)
                pool.memset(eps[:, :], EPS).then_inc(s_cst, 1)
                pool.wait_ge(s_pool, 4)
                pool.affine_select(out=center[:, :], in_=center[:, :], compare_op=ALU.not_equal, fill=1.0 - 1.0 / D,
                                   base=0, pattern=[[-1, D]], channel_multiplier=1).then_inc(s_cst, 1)
                pool.affine_select(out=ident[:, :], in_=ident[:, :], compare_op=ALU.not_equal, fill=1.0,
                                   base=0, pattern=[[-1, D]], channel_multiplier=1).then_inc(s_cst, 1)
                for tile, heads in ((heads0, HEADS[0]), (heads1, HEADS[1])):
                    w = D // heads
                    v = tile[:, :].rearrange("p (h w) -> p h w", w=w)
                    pool.affine_select(out=v, in_=v, compare_op=ALU.is_ge, fill=0.0, base=0,
                                       pattern=[[-w, heads], [0, w]], channel_multiplier=1).then_inc(s_pool, 1)
                pool.wait_ge(s_pool, 6)
                for tile, heads in ((heads0, HEADS[0]), (heads1, HEADS[1])):
                    w = D // heads
                    v = tile[:, :].rearrange("p (h w) -> p h w", w=w)
                    pool.affine_select(out=v, in_=v, compare_op=ALU.is_ge, fill=0.0, base=w - 1,
                                       pattern=[[w, heads], [0, w]], channel_multiplier=-1).then_inc(s_cst, 1)

            @block.scalar
            def _(act):
                act.preload_act_table_set(LOG_EXP)
                act.dma_start(m0[:, :], a_keep0).then_inc(s_m, 16)
                act.dma_start(m1i[:, :], a_mask1).then_inc(s_m, 16)
                act.dma_start(m3[:, :], a_keep3).then_inc(s_m, 16)
                act.wait_ge(s_cols, 48)
                act.activation(ce[:, :], cond[:, :], ACT.Exp, scale=-1.0).then_inc(s_ce, 1)

            layers = (("0", w0, 0), ("1", w1, 1), ("3", w2, 2))

            @block.vector
            def _(dve):
                done = [0]

                def link(ins):
                    done[0] += 1
                    ins.then_inc(s_dve, 1)
                    dve.wait_ge(s_dve, done[0])

                dve.wait_ge(s_ce, 1)
                link(dve.tensor_scalar(ce1[:, :], ce[:, :], 1.0, None, ALU.add))
                link(dve.reciprocal(cr[:, :], ce1[:, :]))
                dve.tensor_tensor(semb[:, :], cond[:, :], cr[:, :], ALU.mult).then_inc(s_semb, 1)
                dve.wait_ge(s_m, 48)
                link(dve.tensor_scalar(m1[:, :], m1i[:, :], 1.0, None, ALU.not_equal))
                link(dve.tensor_scalar(mleft[:, 0:128], m0[:, :], -1.0, 1.0, ALU.mult, ALU.add))
                link(dve.tensor_scalar(mleft[:, 256:384], m3[:, :], -1.0, 1.0, ALU.mult, ALU.add))
                link(dve.tensor_scalar(madd[:, 0:128], mleft[:, 0:128], -1e6, None, ALU.mult))
                link(dve.tensor_scalar(madd[:, 256:384], mleft[:, 256:384], -1e6, None, ALU.mult))
                link(dve.tensor_scalar(madd[:, 128:256], m1i[:, :], 1.0, -1e30, ALU.is_equal, ALU.mult))

                def parts(whole, left, part):
                    link(dve.tensor_copy(part[0], whole))
                    link(dve.tensor_tensor(left, whole, part[0], ALU.subtract))
                    link(dve.tensor_copy(part[1], left))
                    return dve.tensor_tensor(part[2], left, part[1], ALU.subtract)

                parts(madd[:, :], mleft[:, :], [p[:, :] for p in mpart]).then_inc(s_mpart, 1)
                dve.sem_inc(s_keepT, 1)
                dve.wait_ge(s_keepT, 2)
                for i in range(3):
                    link(dve.tensor_copy(keep[i][:, :], Pkeep[:, i * 16:(i + 1) * 16]))
                for name, w, i in layers:
                    dve.wait_ge((s_w0, s_w1, s_w2)[i], 16 if i < 2 else 32)
                    at = {"0": off0, "1": off1, "3": off2}[name]["q" + name][0]
                    link(dve.tensor_scalar(wqkv[i][:, :], w[:, at:at + 3 * D], col("lnw" + name), None, ALU.mult))
                    dve.wait_ge(s_fold, i + 1)
                    link(dve.tensor_tensor(bfold[i][:, 0:1], Pbias[i][:, 0:1], col("bq" + name), ALU.add))
                    link(dve.tensor_tensor(bfold[i][:, 1:2], Pbias[i][:, 1:2], col("bk" + name), ALU.add))
                    at = i * 3 * D
                    link(dve.tensor_copy(brow32[:, at:at + 3 * D], Prow[i][0:1, 0:3 * D]))
                    if name != "3":
                        link(dve.tensor_tensor(brow32[:, at:at + D], brow32[:, at:at + D], row("bq" + name), ALU.add))
                    rv = brow32[:, at + 2 * D:at + 3 * D]
                    link(dve.tensor_tensor(rv, rv, row("bv" + name), ALU.add))
                    r = slice(at, at + 3 * D)
                    parts(brow32[:, r], bleft[:, r], [p[:, r] for p in bpart]).then_inc(s_bpart, 1)
                for i, (s, t, lw, lb) in enumerate((("embs0", "embt0", "ln2w0", "ln2b0"), ("embs1", "embt1", "ln2w1", "ln2b1"),
                                                    ("embs3", "embt3", "ln2w3", "ln2b3"), ("adas", "adat", "g2", "b2"))):
                    dve.wait_ge(s_fold, min(i + 1, 3))
                    link(dve.tensor_scalar(sc1[:, i * B:(i + 1) * B], Pemb[i][:, 0:B], col(s), 1.0, ALU.add, ALU.add))
                    link(dve.tensor_scalar(sh[:, i * B:(i + 1) * B], Pemb[i][:, B:2 * B], col(t), None, ALU.add))
                    sci, shi = sc1[:, i * B:(i + 1) * B], sh[:, i * B:(i + 1) * B]
                    link(dve.tensor_scalar(film_s[i][:, :], sci, col(lw), None, ALU.mult))
                    link(dve.scalar_tensor_tensor(film_t[i][:, :], sci, col(lb), shi, ALU.mult, ALU.add))
                link(dve.tensor_scalar(gate[:, :], Pemb[3][:, 2 * B:3 * B], col("adag"), None, ALU.add))

            @block.tensor
            def _(pe):
                pe.wait_ge(s_cst, 7)
                pe.wait_ge(s_m, 48)
                pe.wait_ge(s_keepT, 1)
                pe.transpose(Pkeep[:, 0:16], m0[:, :], ident[0:16, 0:16])
                pe.transpose(Pkeep[:, 16:32], m1[:, :], ident[0:16, 0:16])
                pe.transpose(Pkeep[:, 32:48], m3[:, :], ident[0:16, 0:16]).then_inc(s_keepT, 1)
                pe.wait_ge(s_semb, 1)
                pe.wait_ge(s_cols, 48)
                for name, w, i in layers:
                    pe.wait_ge((s_w0, s_w1, s_w2)[i], 16 if i < 2 else 32)
                    for j, n in enumerate("qk"):
                        pe.matmul(Pbias[i][:, j:j + 1], mat(n + name), col("lnb" + name), start=True, stop=True)
                    at = {"0": off0, "1": off1, "3": off2}[name]["q" + name][0]
                    pe.matmul(Prow[i][0:1, 0:3 * D], col("lnb" + name), w[:, at:at + 3 * D], start=True, stop=True)
                    for part in range(2):
                        for c in range(2):
                            last = pe.matmul(Pemb[i][:, part * B:(part + 1) * B],
                                             mat("emb" + name, c, 256)[:, part * 128:(part + 1) * 128],
                                             semb[:, c * B:(c + 1) * B], start=(c == 0), stop=(c == 1))
                    if i == 2:
                        for part, src in ((0, 1), (1, 0), (2, 2)):
                            for c in range(2):
                                last = pe.matmul(Pemb[3][:, part * B:(part + 1) * B],
                                                 mat("ada", c, 384)[:, src * 128:(src + 1) * 128],
                                                 semb[:, c * B:(c + 1) * B], start=(c == 0), stop=(c == 1))
                    last.then_inc(s_fold, 1)

        attention_steps = ("mean1", "sq1", "var1", "lnv1", "rstd1", "z", "k", "kmax", "kbias", "knb", "ek", "rk", "ekt", "ektc",
                 "q", "qmax", "qs", "eq", "qsum", "rq", "qn", "qnt", "qtc", "v", "vk", "att", "attm", "attc",
                 "attcr", "y", "sq2", "var2", "lnv2", "rstd2", "z2", "hs", "o", "x")
        s_layer = {n: sem(f"l_{n}") for n in attention_steps}

        def attention_layer(i):
            heads = HEADS[i]
            hw = D // heads
            blockmask = (heads0, heads1)[i]
            name = "01"[i]
            with ExitStack() as on:
                s = s_layer
                before = i * HALVES
                two = range(HALVES)

                def pair(n, shape, dt=f32):
                    return [sb(f"{n}{i}_{h}", shape, dt, on) for h in two]

                tmp, rstd, z = pair("tmp", [D, NH]), pair("rstd", [D, NH]), pair("z", [D, NH])
                kmax, knb, ksum, rk, kbias = (pair(n, [D, BH]) for n in ("kmax", "knb", "ksum", "rk", "kbias"))
                ek, ekT = pair("ek", [D, NH]), pair("ekT", [128, NH])
                qmax, qsum, rq = (pair(n, [128, TILES * heads]) for n in ("qmax", "qsum", "rq"))
                qs, qT, vk = pair("qs", [128, NH]), pair("qT", [D, NH]), pair("vk", [128, NH])
                attm, attc = pair("attm", [D, BH * D]), pair("attc", [D, BH * D])
                hs = pair("hs", [D, NH])
                Pa = [ps(f"Pa{i}_{h}", [128, NH], f32, on) for h in two]
                Pb = [ps(f"Pb{i}_{h}", [128, NH], f32, on) for h in two]
                mask = mrow[:, i * N:(i + 1) * N]

                def toks(h):
                    return slice(h * NH, (h + 1) * NH)

                block = on.enter_context(nc.Block())

                @block.tensor
                def _(pe):
                    def wide(out_, lhsT, rhs, signal, stop=True):
                        for c in range(0, NH, BANK):
                            last = pe.matmul(out_[:, c:c + BANK], lhsT, rhs[:, c:c + BANK], start=True, stop=stop)
                        last.then_inc(signal, 1)

                    for h in two:
                        wide(Pa[h], center[:, :], xT[:, toks(h)], s["mean1"])
                    for h in two:
                        pe.wait_ge(s["sq1"], before + h + 1)
                        wide(Pb[h], mean[:, :], tmp[h], s["var1"])
                    for h in two:
                        pe.wait_ge(s["z"], before + h + 1)
                        for c in range(0, NH, BANK):
                            pe.matmul(Pa[h][:, c:c + BANK], wqkv[i][:, D:2 * D], z[h][:, c:c + BANK], start=True, stop=False)
                            last = pe.matmul(Pa[h][:, c:c + BANK], ones[:, :], mask[:, h * NH + c:h * NH + c + BANK],
                                             start=False, stop=True)
                        last.then_inc(s["k"], 1)
                    for h in two:
                        pe.wait_ge(s["rstd1"], before + h + 1)
                        for t in range(TILES):
                            pe.matmul(Pb[h][:, t * D:(t + 1) * D], z[h][:, t * 128:(t + 1) * 128], wqkv[i][:, 0:D],
                                      start=True, stop=False)
                            last = pe.matmul(Pb[h][:, t * D:(t + 1) * D], ones[:, :], brow[i][:, 0:D], start=False, stop=True)
                        last.then_inc(s["q"], 1)
                    for h in two:
                        pe.wait_ge(s["ek"], BH * (before + h + 1))
                        for t in range(TILES):
                            last = pe.transpose(Pa[h][:, t * 128:(t + 1) * 128], ek[h][:, t * 128:(t + 1) * 128], ident[:, :])
                        last.then_inc(s["ekt"], 1)
                    for h in two:
                        pe.wait_ge(s["ektc"], before + h + 1)
                        for t in range(TILES):
                            pe.matmul(Pa[h][:, t * D:(t + 1) * D], z[h][:, t * 128:(t + 1) * 128], wqkv[i][:, 2 * D:3 * D],
                                      start=True, stop=False)
                            last = pe.matmul(Pa[h][:, t * D:(t + 1) * D], ones[:, :], brow[i][:, 2 * D:3 * D],
                                             start=False, stop=True)
                        last.then_inc(s["v"], 1)
                    for h in two:
                        pe.wait_ge(s["qn"], before + h + 1)
                        for t in range(TILES):
                            last = pe.transpose(Pb[h][:, t * 128:(t + 1) * 128], qs[h][:, t * 128:(t + 1) * 128], ident[:, :])
                        last.then_inc(s["qnt"], 1)
                    for h in two:
                        pe.wait_ge(s["vk"], before + h + 1)
                        for b in range(BH):
                            for t in (2 * b, 2 * b + 1):
                                one, other = (vk[h], ekT[h]) if i == 0 else (ekT[h], vk[h])
                                last = pe.matmul(Pa[h][:, b * D:(b + 1) * D], one[:, t * D:(t + 1) * D],
                                                 other[:, t * D:(t + 1) * D], start=(t == 2 * b), stop=(t == 2 * b + 1))
                        last.then_inc(s["att"], 1)
                    for h in two:
                        pe.wait_ge(s["attm"], before + h + 1)
                        for b in range(BH):
                            last = pe.matmul(Pa[h][:, BANK + b * D:BANK + (b + 1) * D], attm[h][:, b * D:(b + 1) * D],
                                             center[:, :], start=True, stop=True)
                        last.then_inc(s["attc"], 1)
                    for h in two:
                        pe.wait_ge(s["attcr"], before + h + 1)
                        pe.wait_ge(s["qtc"], before + h + 1)
                        for b in range(BH):
                            last = pe.matmul(Pa[h][:, b * T:(b + 1) * T], attc[h][:, b * D:(b + 1) * D],
                                             qT[h][:, b * T:(b + 1) * T], start=True, stop=True)
                        last.then_inc(s["y"], 1)
                    for h in two:
                        pe.wait_ge(s["sq2"], before + h + 1)
                        wide(Pb[h], mean[:, :], tmp[h], s["var2"])
                    for h in two:
                        pe.wait_ge(s["hs"], before + h + 1)
                        wide(Pb[h], mat("out" + name), hs[h], s["o"])

                @block.scalar
                def _(act):
                    for h in two:
                        act.wait_ge(s["mean1"], before + h + 1)
                        act.activation(tmp[h][:, :], Pa[h][:, :], ACT.Square).then_inc(s["sq1"], 1)
                    for h in two:
                        act.wait_ge(s["var1"], before + h + 1)
                        act.activation(tmp[h][:, :], Pb[h][:, :], ACT.Ln, bias=eps[:, :]).then_inc(s["lnv1"], 1)
                        act.wait_ge(s["lnv1"], before + h + 1)
                        act.activation(rstd[h][:, :], tmp[h][:, :], ACT.Exp, scale=-0.5).then_inc(s["rstd1"], 1)
                    for h in two:
                        act.wait_ge(s["knb"], before + h + 1)
                        for b in range(BH):
                            act.activation(ek[h][:, b * T:(b + 1) * T], Pa[h][:, b * T:(b + 1) * T], ACT.Exp,
                                           bias=knb[h][:, b:b + 1], accum_out=ksum[h][:, b:b + 1]).then_inc(s["ek"], 1)
                    for h in two:
                        act.wait_ge(s["qs"], before + h + 1)
                        act.activation(qs[h][:, :], qs[h][:, :], ACT.Exp).then_inc(s["eq"], 1)
                    for h in two:
                        act.wait_ge(s["ekt"], before + h + 1)
                        act.activation(ekT[h][:, :], Pa[h][:, :], ACT.Copy).then_inc(s["ektc"], 1)
                    for h in two:
                        act.wait_ge(s["qnt"], before + h + 1)
                        act.activation(qT[h][:, :], Pb[h][:, :], ACT.Copy).then_inc(s["qtc"], 1)
                    for h in two:
                        act.wait_ge(s["y"], before + h + 1)
                        act.activation(tmp[h][:, :], Pa[h][:, :], ACT.Square).then_inc(s["sq2"], 1)
                    for h in two:
                        act.wait_ge(s["var2"], before + h + 1)
                        act.activation(tmp[h][:, :], Pb[h][:, :], ACT.Ln, bias=eps[:, :]).then_inc(s["lnv2"], 1)
                        act.wait_ge(s["lnv2"], before + h + 1)
                        act.activation(rstd[h][:, :], tmp[h][:, :], ACT.Exp, scale=-0.5).then_inc(s["rstd2"], 1)
                    for h in two:
                        act.wait_ge(s["z2"], before + h + 1)
                        for b in range(BH):
                            g = h * BH + b
                            last = act.activation(hs[h][:, b * T:(b + 1) * T], z[h][:, b * T:(b + 1) * T], ACT.Silu,
                                                  bias=film_t[i][:, g:g + 1], scale=film_s[i][:, g:g + 1])
                        last.then_inc(s["hs"], 1)
                    act.preload_act_table_set(LOG_EXP)

                @block.vector
                def _(dve):
                    for h in two:
                        dve.wait_ge(s["rstd1"], before + h + 1)
                        dve.tensor_tensor(z[h][:, :], Pa[h][:, :], rstd[h][:, :], ALU.mult).then_inc(s["z"], 1)
                    for h in two:
                        dve.wait_ge(s["k"], before + h + 1)
                        dve.tensor_reduce(kmax[h][:, :], Pa[h][:, :].rearrange("p (b t) -> p b t", t=T), AX.X,
                                          ALU.max).then_inc(s["kmax"], 1)
                        dve.wait_ge(s["kmax"], before + h + 1)
                        dve.tensor_scalar(kbias[h][:, :], kmax[h][:, :], bfold[i][:, 1:2], None, ALU.add).then_inc(s["kbias"], 1)
                        dve.wait_ge(s["kbias"], before + h + 1)
                        dve.tensor_scalar(knb[h][:, :], kbias[h][:, :], -1.0, bfold[i][:, 1:2], ALU.mult,
                                          ALU.add).then_inc(s["knb"], 1)
                    for h in two:
                        dve.wait_ge(s["q"], before + h + 1)
                        qv = Pb[h][:, :].rearrange("p (g w) -> p g w", w=hw)
                        dve.tensor_reduce(qmax[h][:, :], qv, AX.X, ALU.max).then_inc(s["qmax"], 1)
                        dve.wait_ge(s["qmax"], before + h + 1)
                        dve.tensor_tensor(qs[h][:, :].rearrange("p (g w) -> p g w", w=hw), qv,
                                          qmax[h][:, :].unsqueeze(2).to_broadcast([128, TILES * heads, hw]),
                                          ALU.subtract).then_inc(s["qs"], 1)
                    for h in two:
                        dve.wait_ge(s["eq"], before + h + 1)
                        dve.tensor_reduce(qsum[h][:, :], qs[h][:, :].rearrange("p (g w) -> p g w", w=hw), AX.X,
                                          ALU.add).then_inc(s["qsum"], 1)
                        dve.wait_ge(s["qsum"], before + h + 1)
                        dve.reciprocal(rq[h][:, :], qsum[h][:, :]).then_inc(s["rq"], 1)
                    for h in two:
                        dve.wait_ge(s["v"], before + h + 1)
                        dve.tensor_tensor(vk[h][:, :].rearrange("p (t d) -> p t d", d=D),
                                          Pa[h][:, :].rearrange("p (t d) -> p t d", d=D),
                                          keep[i][:, h * TILES:(h + 1) * TILES].unsqueeze(2).to_broadcast([128, TILES, D]),
                                          ALU.mult).then_inc(s["vk"], 1)
                        dve.wait_ge(s["ek"], BH * (before + h + 1))
                        dve.reciprocal(rk[h][:, :], ksum[h][:, :]).then_inc(s["rk"], 1)
                    for h in two:
                        dve.wait_ge(s["att"], before + h + 1)
                        if i == 0:
                            dve.tensor_tensor(attm[h][:, :].rearrange("p (b d) -> p b d", d=D),
                                              Pa[h][:, 0:BH * D].rearrange("p (b d) -> p b d", d=D),
                                              blockmask[:, :].unsqueeze(1).to_broadcast([D, BH, D]),
                                              ALU.mult).then_inc(s["attm"], 1)
                        else:
                            dve.wait_ge(s["rk"], before + h + 1)
                            for b in range(BH):
                                last = dve.scalar_tensor_tensor(attm[h][:, b * D:(b + 1) * D], Pa[h][:, b * D:(b + 1) * D],
                                                                rk[h][:, b:b + 1], blockmask[:, :], ALU.mult, ALU.mult)
                            last.then_inc(s["attm"], 1)
                    for h in two:
                        dve.wait_ge(s["attc"], before + h + 1)
                        if i == 0:
                            dve.wait_ge(s["rk"], before + h + 1)
                            dve.tensor_tensor(attc[h][:, :].rearrange("p (b d) -> p b d", d=D),
                                              Pa[h][:, BANK:BANK + BH * D].rearrange("p (b d) -> p b d", d=D),
                                              rk[h][:, :].unsqueeze(2).to_broadcast([D, BH, D]),
                                              ALU.mult).then_inc(s["attcr"], 1)
                        else:
                            dve.tensor_copy(attc[h][:, :], Pa[h][:, BANK:BANK + BH * D]).then_inc(s["attcr"], 1)
                    for h in two:
                        dve.wait_ge(s["rstd2"], before + h + 1)
                        dve.tensor_tensor(z[h][:, :], Pa[h][:, :], rstd[h][:, :], ALU.mult).then_inc(s["z2"], 1)
                    for h in two:
                        dve.wait_ge(s["o"], before + h + 1)
                        dve.scalar_tensor_tensor(xT[:, toks(h)], Pb[h][:, :], col("bout" + name), xT[:, toks(h)],
                                                 ALU.add, ALU.add).then_inc(s["x"], 1)

                @block.gpsimd
                def _(pool):
                    for h in two:
                        pool.wait_ge(s["rq"], before + h + 1)
                        v = qs[h][:, :].rearrange("p (g w) -> p g w", w=hw)
                        pool.tensor_tensor(v, v, rq[h][:, :].unsqueeze(2).to_broadcast([128, TILES * heads, hw]),
                                           ALU.mult).then_inc(s["qn"], 1)

        def mamba_layer():
            with ExitStack() as keep2:
                u = [sb(f"u{c}", [128, N], f32, keep2) for c in range(CH)]
                zs = [sb(f"zs{c}", [128, N], f32, keep2) for c in range(CH)]
                dt = [sb(f"dt{c}", [128, N], f32, keep2) for c in range(CH)]
                dtu = [sb(f"dtu{c}", [128, N], f32, keep2) for c in range(CH)]
                bc = sb("bc", [128, N], bf16, keep2)
                sel = sb("sel", [128, 2 * NS, 128], bf16, keep2)
                acoef = sb("acoef", [128, CH * NS], f32, keep2)
                dskip = sb("dskip", [128, CH * 128], f32, keep2)
                mamba_projections(u, zs, dt, dtu, bc, sel, acoef, dskip)
                mamba_scan(u, zs, dt, dtu, bc, sel, acoef, dskip)

        def mamba_projections(u, zs, dt, dtu, bc, sel, acoef, dskip):
            with ExitStack() as on:
                names = ("mean", "sq", "var", "lnv", "rstd", "z", "xn", "u", "tap", "taps", "us", "zp", "zs", "bcp",
                         "bc1", "r1", "bc2", "bc3", "dtr", "dtrc", "dtp", "ab", "eab", "lab", "mx", "dtA",
                         "sel", "pad", "acoef", "ea", "xbc")
                s = {n: sem(f"m_{n}", on) for n in names}
                s_dt, s_dtu = ([sem(f"m_{n}{c}", on) for c in range(CH)] for n in ("dt", "dtu"))
                two = range(HALVES)

                def pair(n, shape, dt_=f32):
                    return [sb(f"m{n}_{h}", shape, dt_, on) for h in two]

                xbc3 = sb("xbc3", [D, CH * 128], f32, on)
                one = sb("one", [128, 1], f32, on)
                ea = sb("ea", [128, CH * NS], f32, on)
                tmp, rstd, z = pair("tmp", [D, NH]), pair("rstd", [D, NH]), pair("z", [D, NH])
                xn = pair("xn", [D, NH])
                dtr = pair("dtr", [RANK, NH])
                Pa = [ps(f"mPa_{h}", [128, NH], f32, on) for h in two]
                Pb = [ps(f"mPb_{h}", [128, NH], f32, on) for h in two]
                P = [[Pa[h], Pb[h]] for h in two]

                def toks(h):
                    return slice(h * NH, (h + 1) * NH)

                def batches(tile_of_half):
                    return tile_of_half.rearrange("p (b t) -> p b t", t=T)

                block = on.enter_context(nc.Block())

                def finish_dt(eng, h, c):
                    eng.wait_ge(s["lab"], h * CH + c + 1)
                    eng.wait_ge(s["mx"], h * CH + c + 1)
                    eng.tensor_tensor(dt[c][:, toks(h)], dt[c][:, toks(h)], dtu[c][:, toks(h)], ALU.add).then_inc(s_dt[c], 1)
                    eng.wait_ge(s_dt[c], h + 1)
                    eng.tensor_tensor(dtu[c][:, toks(h)], dt[c][:, toks(h)], u[c][:, toks(h)], ALU.mult).then_inc(s_dtu[c], 1)
                    eng.wait_ge(s_dtu[c], h + 1)
                    eng.memset(batches(dt[c][:, toks(h)])[:, :, 0:1], 1e37).then_inc(s["dtA"], 1)

                @block.gpsimd
                def _(pool):
                    pool.memset(one[:, :], 1.0).then_inc(s["pad"], 1)
                    pool.memset(xbc3[:, :], 0.0).then_inc(s["pad"], 1)
                    pool.wait_ge(s["pad"], 2)
                    for c in range(CH):
                        for at in (0, 64, 96):
                            pool.tensor_copy(xbc3[:, c * 128 + at:c * 128 + at + 2 * NS], mat("xbc", c, 2 * NS)).then_inc(s["xbc"], 1)
                    for h in two:
                        pool.wait_ge(s["z"], h + 1)
                        for b in range(BH):
                            g = h * BH + b
                            pool.tensor_scalar(xn[h][:, b * T:(b + 1) * T], z[h][:, b * T:(b + 1) * T], film_s[3][:, g:g + 1],
                                               film_t[3][:, g:g + 1], ALU.mult, ALU.add).then_inc(s["xn"], 1)
                    pool.memset(sel[:, :, :], 0.0).then_inc(s["sel"], 1)
                    for j, at in enumerate((0, 64, 96)):
                        pool.wait_ge(s["sel"], j + 1)
                        pool.affine_select(out=sel[:, :, :], in_=sel[:, :, :], compare_op=ALU.not_equal, fill=1.0, base=-at,
                                           pattern=[[-1, 2 * NS], [0, 128]], channel_multiplier=1).then_inc(s["sel"], 1)
                    for h in two:
                        finish_dt(pool, h, 1)

                @block.tensor
                def _(pe):
                    def wide(out_, lhsT, rhs, start=True, stop=True):
                        for c in range(0, NH, BANK):
                            last = pe.matmul(out_[:, c:c + BANK], lhsT, rhs[:, c:c + BANK], start=start, stop=stop)
                        return last

                    for h in two:
                        wide(Pa[h], center[:, :], xT[:, toks(h)]).then_inc(s["mean"], 1)
                    for h in two:
                        pe.wait_ge(s["sq"], h + 1)
                        wide(Pb[h], mean[:, :], tmp[h]).then_inc(s["var"], 1)
                    for h in two:
                        pe.wait_ge(s["xn"], BH * (h + 1))
                        for c in range(CH):
                            wide(P[h][c], mat("inp", c, 128), xn[h]).then_inc(s["u"], 1)
                    for h in two:
                        for c in range(CH):
                            pe.wait_ge(s["taps"], (h * CH + c + 1) * (TAPS - 1))
                            wide(P[h][c], mat("inp", CH + c, 128), xn[h]).then_inc(s["zp"], 1)
                    pe.wait_ge(s["xbc"], 3 * CH)
                    for h in two:
                        pe.wait_ge(s["us"], CH * h + 2)
                        pe.wait_ge(s["zs"], CH * h + 1)
                        for k in range(0, NH, BANK):
                            for c in range(CH):
                                last = pe.matmul(Pa[h][0:RANK, k:k + BANK], mat("xdt", c, RANK),
                                                 u[c][:, h * NH + k:h * NH + k + BANK], start=(c == 0), stop=(c == CH - 1))
                        last.then_inc(s["dtr"], 1)
                        pe.wait_ge(s["zs"], CH * h + 2)
                        for k in range(0, NH, BANK):
                            for c in range(CH):
                                last = pe.matmul(Pb[h][:, k:k + BANK], xbc3[:, c * 128:(c + 1) * 128],
                                                 u[c][:, h * NH + k:h * NH + k + BANK], start=(c == 0), stop=(c == CH - 1))
                        last.then_inc(s["bcp"], 1)
                    for h in two:
                        for c in range(CH):
                            pe.wait_ge(s["dtrc"] if c == 0 else s["r1"], h + 1)
                            for k in range(0, NH, BANK):
                                last = pe.matmul(P[h][c][:, k:k + BANK], dtp[:, c * 128:(c + 1) * 128], dtr[h][:, k:k + BANK],
                                                 start=True, stop=True)
                            last.then_inc(s["dtp"], 1)

                @block.scalar
                def _(act):
                    for h in two:
                        act.wait_ge(s["mean"], h + 1)
                        act.activation(tmp[h][:, :], Pa[h][:, :], ACT.Square).then_inc(s["sq"], 1)
                    act.activation(ea[:, :], mat("alog"), ACT.Exp).then_inc(s["ea"], 1)
                    for h in two:
                        act.wait_ge(s["var"], h + 1)
                        act.activation(tmp[h][:, :], Pb[h][:, :], ACT.Ln, bias=eps[:, :]).then_inc(s["lnv"], 1)
                        act.wait_ge(s["lnv"], h + 1)
                        act.activation(rstd[h][:, :], tmp[h][:, :], ACT.Exp, scale=-0.5).then_inc(s["rstd"], 1)
                    def last_tap(i):
                        h, c = divmod(i, CH)
                        act.wait_ge(s["u"], i + 1)
                        act.activation(u[c][:, toks(h)], P[h][c][:, :], ACT.Identity, bias=col(f"convb_{c}"),
                                       scale=mat("convw", (c + 1) * TAPS - 1, 1)).then_inc(s["tap"], 1)

                    def silu_u(i):
                        h, c = divmod(i, CH)
                        act.wait_ge(s["taps"], (i + 1) * (TAPS - 1))
                        act.activation(u[c][:, toks(h)], u[c][:, toks(h)], ACT.Silu).then_inc(s["us"], 1)

                    def silu_z(i):
                        h, c = divmod(i, CH)
                        act.wait_ge(s["zp"], i + 1)
                        act.activation(zs[c][:, toks(h)], P[h][c][:, :], ACT.Silu).then_inc(s["zs"], 1)

                    last_tap(0)
                    last_tap(1)
                    last_tap(2)
                    silu_u(0)
                    last_tap(3)
                    silu_u(1)
                    silu_z(0)
                    silu_z(1)
                    silu_u(2)
                    silu_u(3)
                    silu_z(2)
                    silu_z(3)
                    act.preload_act_table_set(LOG_EXP)
                    for h in two:
                        act.wait_ge(s["dtr"], h + 1)
                        act.activation(dtr[h][:, :], Pa[h][0:RANK, :], ACT.Copy).then_inc(s["dtrc"], 1)
                    for h in two:
                        for c in range(CH):
                            k = h * CH + c + 1
                            act.wait_ge(s["dtp"], k)
                            act.activation(dt[c][:, toks(h)], P[h][c][:, :], ACT.Abs, bias=col(f"dtb_{c}")).then_inc(s["ab"], 1)
                            act.wait_ge(s["ab"], k)
                            act.activation(dt[c][:, toks(h)], dt[c][:, toks(h)], ACT.Exp, scale=-1.0).then_inc(s["eab"], 1)
                            act.wait_ge(s["eab"], k)
                            act.activation(dt[c][:, toks(h)], dt[c][:, toks(h)], ACT.Ln, bias=one[:, :]).then_inc(s["lab"], 1)

                @block.vector
                def _(dve):
                    for c in range(CH):
                        dve.tensor_scalar(dskip[:, c * 128:(c + 1) * 128], ident[:, :], col(f"dp_{c}"), None, ALU.mult)
                    dve.wait_ge(s["ea"], 1)
                    dve.tensor_scalar(acoef[:, :], ea[:, :], -1.0, -1e-35, ALU.mult, ALU.min).then_inc(s["acoef"], 1)
                    for h in two:
                        dve.wait_ge(s["rstd"], h + 1)
                        dve.tensor_tensor(z[h][:, :], Pa[h][:, :], rstd[h][:, :], ALU.mult).then_inc(s["z"], 1)

                    def other_taps(i):
                        h, c = divmod(i, CH)
                        dve.wait_ge(s["tap"], i + 1)
                        for k in range(1, TAPS):
                            if k > 1:
                                dve.wait_ge(s["taps"], i * (TAPS - 1) + k - 1)
                            tap = mat("convw", (c + 1) * TAPS - 1 - k, 1)
                            later = batches(u[c][:, toks(h)])[:, :, k:]
                            dve.scalar_tensor_tensor(later, batches(P[h][c][:, :])[:, :, 0:T - k], tap, later,
                                                     ALU.mult, ALU.add).then_inc(s["taps"], 1)

                    def bc_parts(h):
                        k = h + 1
                        dve.wait_ge(s["bcp"], k)
                        dve.tensor_copy(bc[:, toks(h)], Pb[h][:, :]).then_inc(s["bc1"], 1)
                        dve.wait_ge(s["bc1"], k)
                        dve.tensor_tensor(tmp[h][64:128, :], Pb[h][64:128, :], bc[64:128, toks(h)], ALU.subtract).then_inc(s["r1"], 1)
                        dve.wait_ge(s["r1"], k)
                        dve.tensor_copy(bc[64:128, toks(h)], tmp[h][64:128, :]).then_inc(s["bc2"], 1)
                        dve.wait_ge(s["bc2"], k)
                        dve.tensor_tensor(bc[96:128, toks(h)], tmp[h][96:128, :], bc[96:128, toks(h)], ALU.subtract).then_inc(s["bc3"], 1)

                    def above_zero(h, c):
                        dve.wait_ge(s["ab"], h * CH + c + 1)
                        dve.tensor_scalar(dtu[c][:, toks(h)], P[h][c][:, :], col(f"dtb_{c}"), 0.0, ALU.add,
                                          ALU.max).then_inc(s["mx"], 1)

                    for i in range(HALVES * CH):
                        other_taps(i)
                    for h in two:
                        bc_parts(h)
                    for h in two:
                        for c in range(CH):
                            above_zero(h, c)
                        finish_dt(dve, h, 0)

        def mamba_scan(u, zs, dt, dtu, bc, sel, acoef, dskip):
            with ExitStack() as on:
                (s_b, s_c, s_dA, s_bu, s_h, s_ccopy, s_hc, s_y, s_ym, s_skip, s_o, s_x) = (
                    sem(f"v_{n}", on) for n in "b c dA bu h ccopy hc y ym skip o x".split())

                def twice(n):
                    return [[sb(f"{n}{p}_{c}", [128, NH], f32, on) for c in range(CH)] for p in range(2)]

                dA, bu, hst, hc = twice("dA"), twice("bu"), twice("hst"), twice("hc")
                cs = [sb(f"cs{p}", [128, NH], f32, on) for p in range(2)]
                ym = u
                Pbb, Pcb = ps("Pbb", [128, NH], f32, on), ps("Pcb", [128, NH], f32, on)
                Py = [ps(f"Py{c}", [128, NH], f32, on) for c in range(CH)]
                two = range(HALVES)

                def toks(h):
                    return slice(h * NH, (h + 1) * NH)

                def steps(eng, h, one):
                    for p in range(2):
                        one(p, h * NS + p, p, h == 0, False, p == 0)
                    with eng.Fori(2, NS - 2, 2) as n:
                        for p in range(2):
                            one(n + p, n + (h * NS + p), p, False, False, False)
                    for p in range(2):
                        one(NS - 2 + p, h * NS + NS - 2 + p, p, False, p == 1, False)

                block = on.enter_context(nc.Block())

                @block.tensor
                def _(pe):
                    def spread(out_, which, n, h, signal):
                        for k in range(0, NH, BANK):
                            last = pe.matmul(out_[:, k:k + BANK], sel[:, bass.ds(n + which * NS, 1), :],
                                             bc[:, h * NH + k:h * NH + k + BANK], start=True, stop=True)
                        last.then_inc(signal, 1)

                    def add_up(at, parity):
                        for c in range(CH):
                            pe.wait_ge(s_hc, at * CH + c + 1)
                            for k in range(0, NH, BANK):
                                last = pe.matmul(Py[c][:, k:k + BANK], ident[:, :], hc[parity][c][:, k:k + BANK], start=False,
                                                 stop=True, skip_group_check=True)
                            last.then_inc(s_y, 1)

                    def reduce(n, at, parity, first, last_of_half, first_of_half):
                        if not last_of_half:
                            pe.wait_ge(s_bu, (at + 1) * CH)
                            spread(Pbb, 0, n + 1, half[0], s_b)
                            pe.wait_ge(s_ccopy, at + 1)
                            spread(Pcb, 1, n + 1, half[0], s_c)
                        if not first_of_half:
                            add_up(at - 1, 1 - parity)

                    half = [0]
                    for h in two:
                        half[0] = h
                        if h:
                            pe.wait_ge(s_bu, h * NS * CH)
                            pe.wait_ge(s_ccopy, h * NS)
                            pe.wait_ge(s_ym, h * CH)
                        spread(Pbb, 0, 0, h, s_b)
                        spread(Pcb, 1, 0, h, s_c)
                        for c in range(CH):
                            for k in range(0, NH, BANK):
                                pe.matmul(Py[c][:, k:k + BANK], dskip[:, c * 128:(c + 1) * 128],
                                          u[c][:, h * NH + k:h * NH + k + BANK], start=True, stop=True, skip_group_check=True)
                        steps(pe, h, reduce)
                        add_up((h + 1) * NS - 1, 1)
                    for h in two:
                        P = (Pbb, Pcb)[h]
                        pe.wait_ge(s_ym, (h + 1) * CH)
                        for k in range(0, NH, BANK):
                            for c in range(CH):
                                last = pe.matmul(P[:, k:k + BANK], mat("outp", c, 128), ym[c][:, h * NH + k:h * NH + k + BANK],
                                                 start=(c == 0), stop=(c == CH - 1))
                        last.then_inc(s_o, 1)

                @block.scalar
                def _(act):
                    def decay(n, at, parity, first, *_):
                        for c in range(CH):
                            if not first:
                                act.wait_ge(s_h, (at - 2) * CH + c + 1)
                            act.activation(dA[parity][c][:, :], dt[c][:, toks(half[0])], ACT.Exp,
                                           scale=acoef[:, bass.ds(n + c * NS, 1)]).then_inc(s_dA, 1)
                        act.wait_ge(s_c, at + 1)
                        if not first:
                            act.wait_ge(s_hc, (at - 1) * CH)
                        act.activation(cs[parity][:, :], Pcb[:, :], ACT.Copy).then_inc(s_ccopy, 1)

                    half = [0]
                    for h in two:
                        half[0] = h
                        steps(act, h, decay)

                @block.vector
                def _(dve):
                    def scan(n, at, parity, first, *_):
                        dve.wait_ge(s_b, at + 1)
                        for c in range(CH):
                            if not first:
                                dve.wait_ge(s_h, (at - 2) * CH + c + 1)
                            dve.tensor_tensor(bu[parity][c][:, :], dtu[c][:, toks(half[0])], Pbb[:, :], ALU.mult).then_inc(s_bu, 1)
                        for c in range(CH):
                            dve.wait_ge(s_dA, at * CH + c + 1)
                            dve.wait_ge(s_bu, at * CH + c + 1)
                            if not first:
                                dve.wait_ge(s_hc, (at - 2) * CH + c + 1)
                            dve.tensor_tensor_scan(hst[parity][c][:, :], dA[parity][c][:, :], bu[parity][c][:, :], 0.0,
                                                   ALU.mult, ALU.add).then_inc(s_h, 1)

                    half = [0]
                    for h in two:
                        half[0] = h
                        steps(dve, h, scan)
                        for c in range(CH):
                            dve.wait_ge(s_y, ((h + 1) * NS - 1) * CH + c + 1)
                            dve.tensor_tensor(ym[c][:, toks(h)], Py[c][:, :], zs[c][:, toks(h)], ALU.mult).then_inc(s_ym, 1)
                    for h in two:
                        dve.wait_ge(s_o, h + 1)
                        for b in range(BH):
                            xb = xT[:, (h * BH + b) * T:(h * BH + b + 1) * T]
                            dve.scalar_tensor_tensor(xb, (Pbb, Pcb)[h][:, b * T:(b + 1) * T],
                                                     gate[:, h * BH + b:h * BH + b + 1], xb, ALU.mult, ALU.add).then_inc(s_x, 1)

                @block.gpsimd
                def _(pool):
                    def times_c(n, at, parity, first, *_):
                        pool.wait_ge(s_ccopy, at + 1)
                        for c in range(CH):
                            pool.wait_ge(s_h, at * CH + c + 1)
                            if not first:
                                pool.wait_ge(s_y, (at - 2) * CH + c + 1)
                            pool.tensor_tensor(hc[parity][c][:, :], hst[parity][c][:, :], cs[parity][:, :],
                                               ALU.mult).then_inc(s_hc, 1)

                    for h in two:
                        steps(pool, h, times_c)

        H3 = HEADS[2]
        W3 = D // H3
        QPARTS, KPARTS = (0, 0, 0, 1, 1, 2), (0, 1, 2, 0, 1, 0)
        MASK_AT, MAX_AT = 64, 96
        KMAX, KEXP = MASK_AT + 3, MAX_AT + 3
        VW = 32

        def softmax_layer():
            with ExitStack() as keep3:
                q_parts = nc.dram_tensor("q_parts", (B, 3, W3, H3, T), bf16, kind="Internal").ap()
                k_parts = nc.dram_tensor("k_parts", (B, 3, W3, H3, T), bf16, kind="Internal").ap()
                s_written = [sem(f"s_written{h}", keep3) for h in range(HALVES)]
                vc = sb("vc", [128, N // 128, D], f32, keep3)
                vs = [sb(f"vs{p}", [128, 2, H3, VW], f32, keep3) for p in range(2)]
                qst = [sb(f"qst{p}", [128, H3, T], bf16, keep3) for p in range(2)]
                kst = [sb(f"kst{p}", [128, H3, T], bf16, keep3) for p in range(2)]
                identb = sb("identb", [128, 128], bf16, keep3)
                yT = sb("yT", [D, N], f32, keep3)
                part = {n: [sb(f"{n}part{j}", [D, N], bf16, keep3) for j in range(3)] for n in "qk"}
                softmax_projections(q_parts, k_parts, vc, vs, qst, kst, identb, part, s_written)
                softmax_attention(q_parts, k_parts, vc, vs, qst, kst, identb, yT, s_written)
                softmax_output(yT)

        def softmax_projections(q_parts, k_parts, vc, vs, qst, kst, identb, part, s_written):
            with ExitStack() as on:
                names = ("mean", "sq", "var", "lnv", "rstd", "z", "q", "q1", "q2", "q3", "r1", "k", "k1", "k2", "k3", "kr1",
                         "v", "vk", "zero", "ones", "identb")
                s = {n: sem(f"a_{n}", on) for n in names}
                two = range(HALVES)

                def pair(n, shape, dt_=f32):
                    return [sb(f"a{n}_{h}", shape, dt_, on) for h in two]

                tmp, rstd, z = pair("tmp", [D, NH]), pair("rstd", [D, NH]), pair("z", [D, NH])
                left = {"q": pair("lq", [D, NH]), "k": pair("lk", [D, NH])}
                Pa = [ps(f"aPa_{h}", [128, NH], f32, on) for h in two]
                Pb = [ps(f"aPb_{h}", [128, NH], f32, on) for h in two]

                def toks(h):
                    return slice(h * NH, (h + 1) * NH)

                block = on.enter_context(nc.Block())

                @block.sync
                def _(sp):
                    for h in two:
                        for n, dst in (("q", q_parts), ("k", k_parts)):
                            for j in range(3):
                                sp.wait_ge(s[f"{n}{j + 1}"], h + 1)
                                sp.dma_start(dst[h * BH:(h + 1) * BH, j].rearrange("b c h t -> (c h) b t"),
                                             part[n][j][:, toks(h)].rearrange("p (b t) -> p b t", t=T)).then_inc(s_written[h], 16)

                @block.gpsimd
                def _(pool):
                    pool.tensor_copy(identb[:, :], ident[:, :]).then_inc(s["identb"], 1)
                    for p in range(2):
                        for st in (qst[p], kst[p]):
                            pool.memset(st[:, :, :].bitcast(f32), 0.0).then_inc(s["zero"], 1)
                        pool.memset(vs[p][:, :, :, :], 0.0).then_inc(s["zero"], 1)
                    pool.wait_ge(s["zero"], 6)
                    at = 0
                    for p in range(2):
                        for rows_of_ones in (qst[p][MASK_AT:KMAX, :, :], kst[p][MAX_AT:KEXP, :, :], vs[p][:, :, :, W3:W3 + 1]):
                            if at:
                                pool.wait_ge(s["ones"], at)
                            pool.memset(rows_of_ones, 1.0).then_inc(s["ones"], 1)
                            at += 1

                @block.tensor
                def _(pe):
                    def wide(out_, lhsT, rhs):
                        for c in range(0, NH, BANK):
                            last = pe.matmul(out_[:, c:c + BANK], lhsT, rhs[:, c:c + BANK], start=True, stop=True)
                        return last

                    for h in two:
                        wide(Pa[h], center[:, :], xT[:, toks(h)]).then_inc(s["mean"], 1)
                    for h in two:
                        pe.wait_ge(s["sq"], h + 1)
                        wide(Pb[h], mean[:, :], tmp[h]).then_inc(s["var"], 1)
                    for h in two:
                        pe.wait_ge(s["z"], h + 1)
                        wide(Pa[h], wqkv[2][:, 0:D], z[h]).then_inc(s["q"], 1)
                        pe.wait_ge(s["rstd"], h + 1)
                        wide(Pb[h], wqkv[2][:, D:2 * D], z[h]).then_inc(s["k"], 1)
                    for h in two:
                        pe.wait_ge(s["r1"], h + 1)
                        for t in range(TILES):
                            pe.matmul(Pa[h][:, t * D:(t + 1) * D], z[h][:, t * 128:(t + 1) * 128], wqkv[2][:, 2 * D:3 * D],
                                      start=True, stop=False)
                            last = pe.matmul(Pa[h][:, t * D:(t + 1) * D], ones[:, :], brow[2][:, 2 * D:3 * D],
                                             start=False, stop=True)
                        last.then_inc(s["v"], 1)

                @block.scalar
                def _(act):
                    for h in two:
                        act.wait_ge(s["mean"], h + 1)
                        act.activation(tmp[h][:, :], Pa[h][:, :], ACT.Square).then_inc(s["sq"], 1)
                    for h in two:
                        act.wait_ge(s["var"], h + 1)
                        act.activation(tmp[h][:, :], Pb[h][:, :], ACT.Ln, bias=eps[:, :]).then_inc(s["lnv"], 1)
                        act.wait_ge(s["lnv"], h + 1)
                        act.activation(rstd[h][:, :], tmp[h][:, :], ACT.Exp, scale=-0.5).then_inc(s["rstd"], 1)
                    qk = (("q", Pa, 0, "r1"), ("k", Pb, 1, "kr1"))
                    for h in two:
                        for n, P, bias, _ in qk:
                            act.wait_ge(s[n], h + 1)
                            act.activation(part[n][0][:, toks(h)], P[h][:, :], ACT.Identity,
                                           bias=bfold[2][:, bias:bias + 1]).then_inc(s[n + "1"], 1)
                        for n, _, _, r in qk:
                            act.wait_ge(s[r], h + 1)
                            act.activation(part[n][1][:, toks(h)], left[n][h][:, :], ACT.Copy).then_inc(s[n + "2"], 1)

                @block.vector
                def _(dve):
                    for h in two:
                        dve.wait_ge(s["rstd"], h + 1)
                        dve.tensor_tensor(z[h][:, :], Pa[h][:, :], rstd[h][:, :], ALU.mult).then_inc(s["z"], 1)
                    for h in two:
                        for n, P, bias, r in (("q", Pa, 0, "r1"), ("k", Pb, 1, "kr1")):
                            dve.wait_ge(s[n + "1"], h + 1)
                            dve.scalar_tensor_tensor(left[n][h][:, :], P[h][:, :], bfold[2][:, bias:bias + 1],
                                                     part[n][0][:, toks(h)], ALU.add, ALU.subtract).then_inc(s[r], 1)
                        for n in "qk":
                            dve.wait_ge(s[n + "2"], h + 1)
                            dve.tensor_tensor(part[n][2][:, toks(h)], left[n][h][:, :], part[n][1][:, toks(h)],
                                              ALU.subtract).then_inc(s[n + "3"], 1)
                    for h in two:
                        dve.wait_ge(s["v"], h + 1)
                        dve.tensor_tensor(vc[:, h * TILES:(h + 1) * TILES, :], Pa[h][:, :].rearrange("p (t d) -> p t d", d=D),
                                          keep[2][:, h * TILES:(h + 1) * TILES].unsqueeze(2).to_broadcast([128, TILES, D]),
                                          ALU.mult).then_inc(s["vk"], 1)

        def softmax_attention(q_parts, k_parts, vc, vs, qst, kst, identb, yT, s_written):
            PAIRS = H3 // 2
            HALF = H3 // 2
            LOADS = 16 * 7
            SETS = H3 // 4
            with ExitStack() as on:
                s_ld = [[sem(f"t_ld{p}_{i}", on) for i in range(2)] for p in range(2)]
                (s_vs, s_s1, s_mx, s_s2, s_e, s_pv, s_ev, s_t1, s_rc, s_t1d, s_t2, s_t2d, s_nm, s_nmc, s_np, s_nz, s_neg) = (
                    sem(f"t_{n}", on) for n in "vs s1 mx s2 e pv ev t1 rc t1d t2 t2d nm nmc np nz neg".split())
                E = [sb(f"E{p}", [128, 4, 2, T], f32, on) for p in range(2)]
                yraw = [sb(f"yraw{p}", [128, 4, T], f32, on) for p in range(2)]
                ytok = [sb(f"ytok{p}", [128, 2, D], f32, on) for p in range(2)]
                rec = [sb(f"rec{p}", [128, 2, H3], f32, on) for p in range(2)]
                mx = sb("mx", [128, H3, 2], f32, on)
                nleft = sb("nleft", [128, 2, HALF], f32, on)
                nm = sb("nm", [128, 2, 2, 128 // HALF, HALF], bf16, on)
                nmT = [sb(f"nmT{i}", [3 * HALF, T], bf16, on) for i in range(2)]
                S1 = [ps(f"S1_{i}", [128, 2, T], f32, on) for i in range(2)]
                S2 = [ps(f"S2_{i}", [128, 2, 2, T], f32, on) for i in range(2)]
                PV = ps("PV", [128, 2, T], f32, on)
                Pm = ps("Pm", [128, BANK], f32, on)

                def steps(eng, body):
                    body(0, 0, True, False)
                    body(1, 1, False, False)
                    with eng.Fori(2, B - 3, 2) as b:
                        for p in range(2):
                            body(b + p, p, False, False)
                    body(B - 2, 0, False, False)
                    body(B - 1, 1, False, True)

                block = on.enter_context(nc.Block())

                @block.sync
                def _(sp):
                    def load(b, p, i):
                        heads = slice(i * HALF, (i + 1) * HALF)
                        one = bass.ds(b, 1)
                        at = 0
                        for j, times in ((0, 3), (1, 2), (2, 1)):
                            src = q_parts[one, j, :, heads, :].rearrange("o c h t -> o c (h t)")
                            sp.dma_start(qst[p][at:at + times * W3, heads, :],
                                         src.to_broadcast([times, W3, HALF * T])).then_inc(s_ld[p][i], 16)
                            at += times * W3
                        at = 0
                        for times in (3, 2, 1):
                            src = k_parts[one, 0:times, :, heads, :].rearrange("o j c h t -> (o j c) (h t)")
                            sp.dma_start(kst[p][at:at + times * W3, heads, :], src).then_inc(s_ld[p][i], 16)
                            at += times * W3
                        sp.dma_start(kst[p][MASK_AT:KMAX, heads, :], mrow[:, bass.ds(b * T + 2 * N, T)].unsqueeze(1).to_broadcast(
                            [3, HALF, T])).then_inc(s_ld[p][i], 16)

                    def maxima_rows(b, p, i):
                        sp.wait_ge(s_nmc, b * 2 + (i + 1))
                        for j in range(3):
                            sp.dma_start(qst[p][MAX_AT + j:MAX_AT + j + 1, i * HALF:(i + 1) * HALF, :],
                                         nmT[i][j * HALF:(j + 1) * HALF, :]).then_inc(s_neg, 16)

                    sp.wait_ge(s_written[0], 16 * 6)
                    for p in range(2):
                        load(p, p, 0)
                        load(p, p, 1)
                    maxima_rows(0, 0, 0)
                    sp.wait_ge(s_written[1], 16 * 6)
                    with sp.Fori(0, B - 3, 2) as b:
                        for p in range(2):
                            maxima_rows(b + p, p, 1)
                            sp.wait_ge(s_s2, (b + p) * PAIRS + PAIRS // 2)
                            load(b + (p + 2), p, 0)
                            maxima_rows(b + (p + 1), 1 - p, 0)
                            sp.wait_ge(s_s2, (b + p) * PAIRS + PAIRS)
                            load(b + (p + 2), p, 1)
                    maxima_rows(B - 2, 0, 1)
                    maxima_rows(B - 1, 1, 0)
                    maxima_rows(B - 1, 1, 1)
                    for p in range(2):
                        for i in range(2):
                            sp.wait_ge(s_ld[p][i], LOADS * B // 2)
                    sp.wait_ge(s_neg, 3 * 16 * 2 * B)

                @block.gpsimd
                def _(pool):
                    def copy_v(b, p):
                        pool.tensor_copy(vs[p][:, :, :, 0:W3], vc[:, bass.ds(b * 2, 2), :].rearrange(
                            "p t (h w) -> p t h w", w=W3)).then_inc(s_vs, 1)

                    for p in range(2):
                        copy_v(p, p)
                    with pool.Fori(2, B - 1, 2) as b:
                        for p in range(2):
                            pool.wait_ge(s_pv, (b + (p - 1)) * SETS)
                            copy_v(b + p, p)

                @block.tensor
                def _(pe):
                    def scores_for_max(at, h, p, wait):
                        if wait:
                            pe.wait_ge(s_mx, at * H3 + (h - 1))
                        for nt in range(2):
                            last = pe.matmul(S1[h % 2][:, nt, :], qst[p][0:KMAX, h, nt * 128:(nt + 1) * 128], kst[p][0:KMAX, h, :],
                                             start=True, stop=True)
                        last.then_inc(s_s1, 1)

                    def maxima_to_rows(at, i, free, value):
                        pe.wait_ge(s_np, at * 8 + (i + 1) * 4)
                        if free is not None:
                            pe.wait_ge(free, value)
                        for nt in range(2):
                            last = pe.transpose(Pm[:, nt * 64:(nt + 1) * 64].bitcast(bf16),
                                                nm[:, i, nt, :, :].rearrange("p a h -> p (a h)"), identb[:, :])
                        last.then_inc(s_nm, 1)

                    def times_v(b, st, p, first):
                        pe.wait_ge(s_e, b * PAIRS + (2 * st + 2))
                        if st == 0:
                            pe.wait_ge(s_vs, b + 1)
                            if not first:
                                pe.wait_ge(s_ev, b * 2)
                        if st == SETS // 2:
                            pe.wait_ge(s_ev, b * 2 + 1)
                        for mt in range(2):
                            for g in range(4):
                                last = pe.matmul(PV[32 * g:32 * g + VW, st % 2, :], vs[p][:, mt, 4 * st + g, :],
                                                 E[st % 2][:, g, mt, :], start=(mt == 0), stop=(mt == 1))
                        last.then_inc(s_pv, 1)

                    def to_tokens(b, p, nt, last=False):
                        if nt == 0:
                            pe.wait_ge(s_ev, b * 2 + 2)
                            if last:
                                pe.wait_ge(s_t2d, B - 1)
                            else:
                                pe.wait_ge(s_nmc, b * 2 + 4)
                        else:
                            pe.wait_ge(s_t1d, b * 2 + 1)
                        for st in range(4):
                            turned = pe.transpose(Pm[:, st * 128:(st + 1) * 128], yraw[p][:, st, nt * 128:(nt + 1) * 128], ident[:, :])
                        turned.then_inc(s_t1, 1)

                    def to_features(b, p, last_of_all):
                        pe.wait_ge(s_t1d, b * 2 + 2)
                        if not last_of_all:
                            pe.wait_ge(s_nmc, b * 2 + 5)
                        for nt in range(2):
                            last = pe.transpose(Pm[:, nt * 128:(nt + 1) * 128], ytok[p][:, nt, :], ident[:, :])
                        last.then_inc(s_t2, 1)

                    def body(b, p, first, last_of_all):
                        for j in range(PAIRS):
                            if j % (PAIRS // 2) == 0:
                                pe.wait_ge(s_neg, (b * 2 + (1 + j // (PAIRS // 2))) * 48)
                            if j >= 2 or not first:
                                pe.wait_ge(s_e, b * PAIRS + (j - 1))
                            for i in range(2):
                                h = 2 * j + i
                                for mt in range(2):
                                    last = pe.matmul(S2[j % 2][:, i, mt, :], kst[p][0:KEXP, h, mt * 128:(mt + 1) * 128],
                                                     qst[p][0:KEXP, h, :], start=True, stop=True)
                                if i == 1:
                                    last.then_inc(s_s2, 1)
                                if not last_of_all:
                                    if h % HALF == 0:
                                        pe.wait_ge(s_ld[1 - p][h // HALF], (b + (2 + p)) * (LOADS // 2))
                                    scores_for_max(b + 1, h, 1 - p, True)
                            if j == 0:
                                if not first:
                                    times_v(b - 1, SETS - 1, 1 - p, False)
                                if isinstance(b, int) and b < 2:
                                    maxima_to_rows(b, 1, s_nmc, b * 2 + 1)
                                else:
                                    maxima_to_rows(b, 1, s_t2d, b - 1)
                            elif j % 2 == 0:
                                times_v(b, j // 2 - 1, p, first)
                            if not first and j in (2, 3):
                                to_tokens(b - 1, 1 - p, j - 2)
                            if not last_of_all and j == 4:
                                if first:
                                    maxima_to_rows(b + 1, 0, s_nmc, 2)
                                else:
                                    maxima_to_rows(b + 1, 0, s_t1d, b * 2)
                            if not first and j == 6:
                                to_features(b - 1, 1 - p, last_of_all)

                    for i in range(2):
                        pe.wait_ge(s_ld[0][i], LOADS)
                        for h in range(i * HALF, (i + 1) * HALF):
                            scores_for_max(0, h, 0, h >= 2)
                        if i == 0:
                            maxima_to_rows(0, 0, None, 0)
                    steps(pe, body)
                    times_v(B - 1, SETS - 1, 1, False)
                    for nt in range(2):
                        to_tokens(B - 1, 1, nt, True)
                    to_features(B - 1, 1, True)

                @block.scalar
                def _(act):
                    def out_of_psum(b, p, half):
                        act.wait_ge(s_pv, b * SETS + (half + 1) * SETS // 2)
                        act.activation(yraw[p][:, 2 * half:2 * half + 2, :], PV[:, :, :], ACT.Copy).then_inc(s_ev, 1)

                    def body(b, p, first, last_of_all):
                        for j in range(PAIRS):
                            act.wait_ge(s_s2, b * PAIRS + (j + 1))
                            st = j // 2
                            if j % 2 == 0 and (st >= 2 or not first):
                                act.wait_ge(s_pv, b * SETS + (st - 1))
                            act.activation(E[st % 2][:, 2 * (j % 2):2 * (j % 2) + 2, :, :], S2[j % 2][:, :, :, :],
                                           ACT.Exp).then_inc(s_e, 1)
                            if j == 0 and not first:
                                out_of_psum(b - 1, 1 - p, 1)
                            if j == 4:
                                out_of_psum(b, p, 0)

                    steps(act, body)
                    out_of_psum(B - 1, 1, 1)

                @block.vector
                def _(dve):
                    def head_max(at, h):
                        dve.wait_ge(s_s1, at * H3 + (h + 1))
                        dve.tensor_reduce(mx[:, h, :], S1[h % 2][:, :, :], AX.X, ALU.max).then_inc(s_mx, 1)

                    def maxima_parts(at, i):
                        m = mx[:, i * HALF:(i + 1) * HALF, :].rearrange("p h t -> p t h")
                        before = at * 8 + i * 4
                        dve.wait_ge(s_mx, at * H3 + (i + 1) * HALF)
                        dve.tensor_scalar(nm[:, i, :, 0, :], m, -1.0, None, ALU.mult).then_inc(s_np, 1)
                        dve.wait_ge(s_np, before + 1)
                        dve.scalar_tensor_tensor(nleft[:, :, :], m, -1.0, nm[:, i, :, 0, :], ALU.mult, ALU.subtract).then_inc(s_np, 1)
                        dve.wait_ge(s_np, before + 2)
                        dve.tensor_copy(nm[:, i, :, 1, :], nleft[:, :, :]).then_inc(s_np, 1)
                        dve.wait_ge(s_np, before + 3)
                        dve.tensor_tensor(nm[:, i, :, 2, :], nleft[:, :, :], nm[:, i, :, 1, :], ALU.subtract).then_inc(s_np, 1)

                    def rows_out(at, i, any_before=True):
                        dve.wait_ge(s_nm, at * 2 + (i + 1))
                        if any_before:
                            dve.wait_ge(s_neg, at * 96 + i * 48)
                        dve.tensor_copy(nmT[i][:, :], Pm[0:3 * HALF, 0:128].bitcast(bf16)).then_inc(s_nmc, 1)

                    def normalise(b, p, nt):
                        dve.wait_ge(s_t1, b * 2 + (nt + 1))
                        v = Pm[:, :].rearrange("p (h w) -> p h w", w=VW)
                        dve.reciprocal(rec[p][:, nt, :], v[:, :, W3]).then_inc(s_rc, 1)
                        dve.wait_ge(s_rc, b * 2 + (nt + 1))
                        dve.tensor_tensor(ytok[p][:, nt, :].rearrange("p (h w) -> p h w", w=W3), v[:, :, 0:W3],
                                          rec[p][:, nt, :].unsqueeze(2).to_broadcast([128, H3, W3]), ALU.mult).then_inc(s_t1d, 1)

                    def features_out(b):
                        dve.wait_ge(s_t2, b + 1)
                        dve.tensor_copy(yT[:, bass.ds(b * T, T)], Pm[:, 0:T]).then_inc(s_t2d, 1)

                    def body(b, p, first, last_of_all):
                        for j in range(PAIRS):
                            if not last_of_all:
                                if j % (PAIRS // 2) == 0:
                                    dve.wait_ge(s_np, b * 8 + (1 + j // (PAIRS // 2)) * 4)
                                for h in range(2 * j, 2 * j + 2):
                                    head_max(b + 1, h)
                                if j % (PAIRS // 2) == PAIRS // 2 - 1:
                                    maxima_parts(b + 1, j // (PAIRS // 2))
                            if j == 0:
                                rows_out(b, 1, True)
                            if not first and j in (2, 3):
                                normalise(b - 1, 1 - p, j - 2)
                            if not last_of_all and j == 4:
                                rows_out(b + 1, 0)
                            if not first and j == 6:
                                features_out(b - 1)

                    dve.memset(nm[:, :, :, :, :], 0.0).then_inc(s_nz, 1)
                    dve.wait_ge(s_nz, 1)
                    for i in range(2):
                        for h in range(i * HALF, (i + 1) * HALF):
                            head_max(0, h)
                        maxima_parts(0, i)
                        if i == 0:
                            rows_out(0, 0, False)
                    steps(dve, body)
                    for nt in range(2):
                        normalise(B - 1, 1, nt)
                    features_out(B - 1)

        def softmax_output(yT):
            with ExitStack() as on:
                s = s_layer
                before = 2 * HALVES
                s_stored = sem("s_stored", on)
                two = range(HALVES)

                def pair(n, shape):
                    return [sb(f"o{n}_{h}", shape, f32, on) for h in two]

                tmp, rstd, z, hs = (pair(n, [D, NH]) for n in ("tmp", "rstd", "z", "hs"))
                Pa = [ps(f"oPa_{h}", [128, NH], f32, on) for h in two]
                Pb = [ps(f"oPb_{h}", [128, NH], f32, on) for h in two]

                def toks(h):
                    return slice(h * NH, (h + 1) * NH)

                block = on.enter_context(nc.Block())

                @block.sync
                def _(sp):
                    for h in two:
                        sp.wait_ge(s["x"], before + h + 1)
                        sp.dma_start(out[:, toks(h)], xT[:, toks(h)]).then_inc(s_stored, 16)
                    sp.wait_ge(s_stored, 16 * HALVES)

                @block.tensor
                def _(pe):
                    def wide(out_, lhsT, rhs):
                        for c in range(0, NH, BANK):
                            last = pe.matmul(out_[:, c:c + BANK], lhsT, rhs[:, c:c + BANK], start=True, stop=True)
                        return last

                    for h in two:
                        wide(Pa[h], center[:, :], yT[:, toks(h)]).then_inc(s["mean1"], 1)
                    for h in two:
                        pe.wait_ge(s["sq2"], before + h + 1)
                        wide(Pb[h], mean[:, :], tmp[h]).then_inc(s["var2"], 1)
                    for h in two:
                        pe.wait_ge(s["hs"], before + h + 1)
                        wide(Pb[h], mat("out3"), hs[h]).then_inc(s["o"], 1)

                @block.scalar
                def _(act):
                    for h in two:
                        act.wait_ge(s["mean1"], before + h + 1)
                        act.activation(tmp[h][:, :], Pa[h][:, :], ACT.Square).then_inc(s["sq2"], 1)
                    for h in two:
                        act.wait_ge(s["var2"], before + h + 1)
                        act.activation(tmp[h][:, :], Pb[h][:, :], ACT.Ln, bias=eps[:, :]).then_inc(s["lnv2"], 1)
                        act.wait_ge(s["lnv2"], before + h + 1)
                        act.activation(rstd[h][:, :], tmp[h][:, :], ACT.Exp, scale=-0.5).then_inc(s["rstd2"], 1)
                    for h in two:
                        act.wait_ge(s["z2"], before + h + 1)
                        for b in range(BH):
                            g = h * BH + b
                            last = act.activation(hs[h][:, b * T:(b + 1) * T], z[h][:, b * T:(b + 1) * T], ACT.Silu,
                                                  bias=film_t[2][:, g:g + 1], scale=film_s[2][:, g:g + 1])
                        last.then_inc(s["hs"], 1)

                @block.vector
                def _(dve):
                    for h in two:
                        dve.wait_ge(s["rstd2"], before + h + 1)
                        dve.tensor_tensor(z[h][:, :], Pa[h][:, :], rstd[h][:, :], ALU.mult).then_inc(s["z2"], 1)
                    for h in two:
                        dve.wait_ge(s["o"], before + h + 1)
                        dve.scalar_tensor_tensor(xT[:, toks(h)], Pb[h][:, :], col("bout3"), xT[:, toks(h)],
                                                 ALU.add, ALU.add).then_inc(s["x"], 1)

        for i in range(2):
            attention_layer(i)
        mamba_layer()
        softmax_layer()


def kernel(**inputs):
    import numpy as np
    import concourse.bacc as bacc
    from concourse import mybir
    from concourse.bass_utils import run_bass_kernel_spmd

    a = {k: np.asarray(v) for k, v in inputs.items()}
    names = {"0": ("L0_cond_", "Wq Wk Wv W_emb W_out ln_w ln_b bq bk bv b_emb ln2_w ln2_b b_out"),
             "1": ("L1_cond_", "Wq Wk Wv film_emb_W film_out_W norm_scale norm_bias bq bk bv film_emb_b "
                               "film_norm_scale film_norm_bias film_out_b"),
             "3": ("L3_cond_", "q_w k_w v_w emb_w out_w norm_w norm_b q_b k_b v_b emb_b sb_norm_w sb_norm_b out_b")}
    keys = ["q", "k", "v", "emb", "out", "lnw", "lnb", "bq", "bk", "bv", "bemb", "ln2w", "ln2b", "bout"]
    m = {}

    def halves(w):
        return np.concatenate([w[i:i + 128] for i in range(0, w.shape[0], 128)], axis=1)

    for n, (prefix, parts) in names.items():
        for key, part in zip(keys, parts.split()):
            m[key + n] = a[prefix + part]
        m["emb" + n] = halves(m["emb" + n])
        if n == "3":
            for key in ("q3", "k3", "bq3", "bk3"):
                m[key] = m[key].reshape(-1, HEADS[2], D // HEADS[2]).swapaxes(1, 2).reshape(m[key].shape)
        m["embs" + n], m["embt" + n] = m["bemb" + n][:D], m["bemb" + n][D:]
    p = "L2_cond_"
    m["ada"] = halves(a[p + "ada_w"].T)
    m["adat"], m["adas"], m["adag"] = a[p + "ada_b"].reshape(3, D)
    m["inp"] = a[p + "in_proj_w"].T
    xp = halves(a[p + "x_proj_w"].T).reshape(128, CH, RANK + 2 * NS)
    m["xdt"] = xp[:, :, :RANK].reshape(128, -1)
    m["xbc"] = xp[:, :, RANK:].reshape(128, -1)
    m["outp"] = halves(a[p + "out_proj_w"].T)
    m["alog"] = halves(a[p + "A_log"])
    m["convw"] = halves(a[p + "conv_w"])
    m["g2"], m["b2"] = a[p + "ln_g"], a[p + "ln_b"]
    for c in range(CH):
        for key, part in (("convb", "conv_b"), ("dtb", "dt_proj_b"), ("dp", "D_param")):
            m[f"{key}_{c}"] = a[p + part][c * 128:(c + 1) * 128]
    arrays = {
        "a_x": a["x"].reshape(N, D).T,
        "a_cond": halves(a["cond_2048"].T),
        "a_w0": np.concatenate([m[n] for n, _ in MATS0], axis=1),
        "a_w1": np.concatenate([m[n] for n, _ in MATS1], axis=1),
        "a_w2": np.concatenate([m[n] for n, _ in MATS2], axis=1),
        "a_dtp": a[p + "dt_proj_w"].T,
        "a_cols": np.stack([m[c] for c in COLS], axis=1),
        "a_rows": np.concatenate([m[r] for r in ROWS]).reshape(1, -1),
        "a_keep0": a["mask_BxSx1_fk1"].reshape(N // 128, 128),
        "a_mask1": a["mask_BxS_ik0"].reshape(N // 128, 128),
        "a_keep3": a["mask_BxS_ff1"].reshape(N // 128, 128),
    }
    nc = bacc.Bacc("TRN2", target_bir_lowering=False, num_devices=1)
    args = []
    for name in arrays:
        arrays[name] = np.ascontiguousarray(arrays[name])
        args.append(nc.dram_tensor(name, arrays[name].shape, mybir.dt.from_np(arrays[name].dtype),
                                   kind="ExternalInput").ap())
    args.append(nc.dram_tensor("out", (D, N), mybir.dt.float32, kind="ExternalOutput").ap())
    cond_seq_kernel(nc, *args)
    got = run_bass_kernel_spmd(nc, [arrays], core_ids=[0]).results[0]["out"]
    return np.ascontiguousarray(got.T).reshape(B, T, D)
```

```python
import concourse.bass as bass
from concourse import mybir
from contextlib import ExitStack

B, T, D, TE = 8, 256, 128, 256
N = B * T
HALVES = 2
NH = N // HALVES
BH = B // HALVES
TILES = NH // 128
BANK = 512
DI, NS, RANK, TAPS = 256, 16, 64, 4
CH = DI // 128
HEADS = (8, 16, 16)
EPS = 1e-5
LOG_EXP = "natural_log_exp_and_others"

MATS0 = [("q0", 128), ("k0", 128), ("v0", 128), ("emb0", 512), ("out0", 128)]
MATS1 = [("q1", 128), ("k1", 128), ("v1", 128), ("emb1", 512), ("out1", 128)]
MATS2 = [("ada", 768), ("inp", 512), ("xdt", 128), ("xbc", 64), ("outp", 256), ("alog", 32), ("convw", 8),
         ("q3", 128), ("k3", 128), ("v3", 128), ("emb3", 512), ("out3", 128)]
LAYER_COLS = ["lnw", "lnb", "bq", "bk", "embs", "embt", "ln2w", "ln2b", "bout"]
COLS = [c + i for i in "013" for c in LAYER_COLS] + [
    "g2", "b2", "adat", "adas", "adag", "convb_0", "convb_1", "dtb_0", "dtb_1", "dp_0", "dp_1"]
ROWS = ["bq0", "bv0", "bq1", "bv1", "bv3"]


def offsets(mats):
    at, out = 0, {}
    for name, width in mats:
        out[name] = (at, width)
        at += width
    return out, at


def cond_seq_kernel(nc, a_x, a_cond, a_w0, a_w1, a_w2, a_dtp, a_cols, a_rows, a_keep0, a_mask1, a_keep3,
                    out):
    f32, bf16, i32 = mybir.dt.float32, mybir.dt.bfloat16, mybir.dt.int32
    ALU, ACT, AX = mybir.AluOpType, mybir.ActivationFunctionType, mybir.AxisListType

    ctx = ExitStack()
    with ctx:
        def sb(name, shape, dt=f32, on=ctx):
            return on.enter_context(nc.sbuf_tensor(name, shape, dt))

        def ps(name, shape, dt=f32, on=ctx):
            return on.enter_context(nc.psum_tensor(name, shape, dt))

        def sem(name, on=ctx):
            return on.enter_context(nc.semaphore(name))

        xT = sb("xT", [D, N])
        off0, n0 = offsets(MATS0)
        off1, n1 = offsets(MATS1)
        off2, n2 = offsets(MATS2)
        w0, w1, w2 = sb("w0", [D, n0]), sb("w1", [D, n1]), sb("w2", [D, n2])
        dtp = sb("dtp", [RANK, DI])
        cols = sb("cols", [D, len(COLS)])
        rows = sb("rows", [1, len(ROWS) * 128])
        cond = sb("cond", [D, 2 * B])

        def mat(name, i=0, n=None):
            for w, off in ((w0, off0), (w1, off1), (w2, off2)):
                if name in off:
                    at, width = off[name]
                    n = n or width
                    return w[:, at + i * n:at + (i + 1) * n]
            raise KeyError(name)

        def col(name):
            c = COLS.index(name)
            return cols[:, c:c + 1]

        def row(name):
            c = ROWS.index(name) * 128
            return rows[0:1, c:c + 128]

        center = sb("center", [D, D])
        mean = sb("mean", [D, D])
        ident = sb("ident", [D, D])
        ones = sb("ones", [3, 128], bf16)
        heads0, heads1 = sb("heads0", [D, D]), sb("heads1", [D, D])
        eps = sb("eps", [D, 1])
        wqkv = [sb(f"wqkv{i}", [D, 3 * D]) for i in range(3)]
        bfold = [sb(f"bfold{i}", [D, 2]) for i in range(3)]
        brow = [sb(f"brow{i}", [3, 2 * D], bf16) for i in range(3)]
        mrow = sb("mrow", [3, 3 * N], bf16)
        film_s = [sb(f"film_s{i}", [D, B]) for i in range(4)]
        film_t = [sb(f"film_t{i}", [D, B]) for i in range(4)]
        gate = sb("gate", [D, B])
        keep = [sb(f"keep{i}", [128, N // 128]) for i in range(3)]
        semb = sb("semb", [D, 2 * B])

        attention_steps = ("mean1", "sq1", "var1", "lnv1", "rstd1", "z", "k", "kmax", "kbias", "knb", "ek", "rk", "ekt", "ektc",
                 "q", "qmax", "qs", "eq", "qsum", "rq", "qn", "qnt", "qtc", "v", "vk", "att", "attm", "attc",
                 "attcr", "y", "sq2", "var2", "lnv2", "rstd2", "z2", "hs", "o", "x")
        s_layer = {n: sem(f"l_{n}") for n in attention_steps}

        keep2, front = ExitStack(), ExitStack()
        u = [sb(f"u{c}", [128, N], f32, keep2) for c in range(CH)]
        zs = [sb(f"zs{c}", [128, N], f32, keep2) for c in range(CH)]
        dt = [sb(f"dt{c}", [128, N], f32, keep2) for c in range(CH)]
        dtu = [sb(f"dtu{c}", [128, N], f32, keep2) for c in range(CH)]
        bc = sb("bc", [128, N], bf16, keep2)
        sel = sb("sel", [128, 2 * NS, 128], bf16, keep2)
        acoef = sb("acoef", [128, CH * NS], f32, keep2)

        s_cols, s_w0, s_w1, s_w2, s_m = (sem(n, front) for n in ("s_cols", "s_w0", "s_w1", "s_w2", "s_m"))
        s_x = [sem(f"s_x{h}", front) for h in range(HALVES)]
        s_cst, s_pool, s_dve, s_folding = (sem(n, front) for n in ("s_cst", "s_pool", "s_dve", "s_folding"))
        s_semb, s_fold, s_keepT, s_read, s_raw, s_films = (
            sem(n, front) for n in ("s_semb", "s_fold", "s_keepT", "s_read", "s_raw", "s_films"))
        s_mpart, s_mrow, s_bpart = (sem(n, front) for n in ("s_mpart", "s_mrow", "s_bpart"))
        s_brow = [sem(f"s_brow{i}", front) for i in range(3)]
        m0, m3 = sb("m0", [N // 128, 128], f32, front), sb("m3", [N // 128, 128], f32, front)
        m1i, m1 = sb("m1i", [N // 128, 128], i32, front), sb("m1", [N // 128, 128], f32, front)
        madd = sb("madd", [N // 128, 3 * 128], f32, front)
        mleft = sb("mleft", [N // 128, 3 * 128], f32, front)
        mpart = [sb(f"mpart{j}", [N // 128, 3 * 128], bf16, front) for j in range(3)]
        brow32, bleft = ([sb(f"{n}{i}", [1, 2 * D], f32, front) for i in range(3)] for n in ("brow32", "bleft"))
        bpart = [[sb(f"bpart{i}_{j}", [1, 2 * D], bf16, front) for j in range(3)] for i in range(3)]
        fsc, fsh, flb = ([sb(f"{n}{i}", [D, B], f32, front) for i in range(4)] for n in ("fsc", "fsh", "flb"))
        raw = [sb(f"raw{i}", [D, BANK], f32, front) for i in range(4)]

        two = range(HALVES)

        def pair(n, shape, dt_=f32):
            return [sb(f"{n}_{h}", shape, dt_, front) for h in two]

        tmp, rstd, z = pair("tmp", [D, NH]), pair("rstd", [D, NH]), pair("z", [D, NH])
        kmax, knb, ksum, rk, kbias = (pair(n, [D, BH]) for n in ("kmax", "knb", "ksum", "rk", "kbias"))
        ek, ekT, qs, qT, vk, hs = ([t[:, h * NH:(h + 1) * NH] for h in two] for t in (u[0], u[1], zs[0], zs[1], dt[0], dt[1]))
        attm, attc = ([dtu[0][:, (2 * k + h) * BH * D:(2 * k + h + 1) * BH * D] for h in two] for k in range(2))
        qmax, qsum, rq = (pair(n, [128, TILES * max(HEADS)]) for n in ("qmax", "qsum", "rq"))
        mamba_steps = ("mean", "sq", "var", "lnv", "rstd", "z", "xn", "xna", "u", "tap", "taps", "us", "zp", "zs", "bcp",
                 "bc1", "r1", "bc2", "bc3", "dtr", "dtrc", "dtp", "clamp", "eab", "lab", "fresh",
                 "sel0", "sel1", "sel", "pad", "acoef", "ea", "xbc")
        s_mamba = {n: sem(f"m_{n}", front) for n in mamba_steps}
        s_dt, s_dtu = sem("m_dt", front), sem("m_dtu", front)
        xbc3 = sb("xbc3", [D, CH * 128], f32, front)
        sel0, sel1 = sb("sel0", [128, 2 * NS], f32, front), sb("sel1", [128, 2 * NS], f32, front)
        one = sb("one", [128, 1], f32, front)
        ea = sb("ea", [128, CH * NS], f32, front)
        xn = pair("xn", [D, NH])
        dtr = pair("dtr", [RANK, NH])
        Pa = [ps(f"Pa_{h}", [128, NH], f32, front) for h in two]
        Pb = [ps(f"Pb_{h}", [128, NH], f32, front) for h in two]
        P = [[Pa[h], Pb[h]] for h in two]

        def toks(h):
            return slice(h * NH, (h + 1) * NH)

        QUARTERS = N // BANK
        four = range(QUARTERS)

        NORM_ORDER = ((True, 0), (True, 1), (False, 0), (True, 2), (False, 1), (True, 3), (False, 2), (False, 3))

        def quarter(q):
            h, c = divmod(q * BANK, NH)
            return h, slice(c, c + BANK), slice(q * BANK, (q + 1) * BANK)

        def batches(tile_of_half):
            return tile_of_half.rearrange("p (b t) -> p b t", t=T)

        def tiles_and_bias(pe, out_, zh, w, bias):
            per_bank = BANK // D
            for t in range(TILES):
                if t % per_bank == 0:
                    pe.matmul(out_[:, t * D:(t + per_bank) * D].rearrange("p (a d) -> p a d", d=D), ones[:, :],
                              bias.unsqueeze(1).to_broadcast([3, per_bank, D]), start=True, stop=True, skip_group_check=True)
                last = pe.matmul(out_[:, t * D:(t + 1) * D], zh[:, t * 128:(t + 1) * 128], w, start=False, stop=True,
                                 skip_group_check=True)
            return last

        Pkeep = Pb[1][:, BANK:2 * BANK]
        ROW_AT = 128
        layers = (("0", w0, off0, s_w0, 16), ("1", w1, off1, s_w1, 16), ("3", w2, off2, s_w2, 32))

        def condition_product(pe, out_, weights, chunks):
            for part, src in enumerate(chunks):
                for c in range(2):
                    last = pe.matmul(out_[:, part * B:(part + 1) * B], weights[c][:, src * 128:(src + 1) * 128],
                                     semb[:, c * B:(c + 1) * B], start=(c == 0), stop=(c == 1))
            return last

        def layer_products(pe, i, bank):
            name, _, _, s_w, loaded = layers[i]
            pe.wait_ge(s_w, loaded)
            for j, n in enumerate("qk"):
                pe.matmul(bank[:, 2 * B + j:2 * B + j + 1], mat(n + name), col("lnb" + name), start=True, stop=True)
            for j, n in enumerate("qv"):
                pe.matmul(bank[0:1, ROW_AT + j * D:ROW_AT + (j + 1) * D], col("lnb" + name), mat(n + name), start=True, stop=True)
            condition_product(pe, bank, [mat("emb" + name, c, 256) for c in range(2)], (0, 1)).then_inc(s_fold, 1)

        def setup_products(pe):
            pe.wait_ge(s_semb, 1)
            pe.wait_ge(s_cols, 48)
            layer_products(pe, 0, Pb[1][:, 0:BANK])
            pe.wait_ge(s_m, 48)
            pe.wait_ge(s_keepT, 1)
            pe.transpose(Pkeep[:, 0:16], m0[:, :], ident[0:16, 0:16])
            pe.transpose(Pkeep[:, 16:32], m1[:, :], ident[0:16, 0:16])
            pe.transpose(Pkeep[:, 32:48], m3[:, :], ident[0:16, 0:16]).then_inc(s_keepT, 1)

        PLACE = {0: 0, 1: 1, 3: 2, 2: 3}
        AT_END_OF = {0: ((1, Pb[0][:, 0:BANK]),), 1: ((3, Pb[0][:, 0:BANK]), (2, Pb[0][:, BANK:2 * BANK]))}

        def fold_products(pe, i):
            for q, (k, bank) in enumerate(AT_END_OF[i]):
                pe.wait_ge(s_layer["lnv2"], i * QUARTERS + q + 1)
                if k < 3:
                    layer_products(pe, k, bank)
                else:
                    pe.wait_ge(s_w2, 32)
                    condition_product(pe, bank, [mat("ada", c, 384) for c in range(2)], (1, 0, 2)).then_inc(s_fold, 1)

        def raw_out(dve, k, bank):
            dve.wait_ge(s_fold, PLACE[k] + 1)
            if k < 3:
                dve.tensor_copy(raw[k][:, 0:2 * B + 2], bank[:, 0:2 * B + 2])
                dve.tensor_copy(raw[k][0:1, ROW_AT:ROW_AT + 2 * D], bank[0:1, ROW_AT:ROW_AT + 2 * D]).then_inc(s_raw, 1)
            else:
                dve.tensor_copy(raw[k][:, 0:3 * B], bank[:, 0:3 * B]).then_inc(s_raw, 1)

        def linker(eng, signal):
            done = [0]

            def link(ins):
                done[0] += 1
                ins.then_inc(signal, 1)
                eng.wait_ge(signal, done[0])

            return link

        def parts(eng, link, whole, left, part):
            link(eng.tensor_copy(part[0], whole))
            link(eng.tensor_tensor(left, whole, part[0], ALU.subtract))
            link(eng.tensor_copy(part[1], left))
            return eng.tensor_tensor(part[2], left, part[1], ALU.subtract)

        def film_factors(eng, link, i, bank, s_, t_, lw, lb):
            link(eng.tensor_scalar(fsc[i][:, :], bank[:, 0:B], col(s_), 1.0, ALU.add, ALU.add))
            link(eng.tensor_scalar(fsh[i][:, :], bank[:, B:2 * B], col(t_), 0.0, ALU.add, ALU.add))
            link(eng.tensor_scalar(film_s[i][:, :], fsc[i][:, :], col(lw), 1.0, ALU.mult, ALU.mult))
            link(eng.tensor_scalar(flb[i][:, :], fsc[i][:, :], col(lb), 1.0, ALU.mult, ALU.mult))
            link(eng.tensor_tensor(film_t[i][:, :], flb[i][:, :], fsh[i][:, :], ALU.add))

        def fold_weights(eng, link, i):
            name, w, off, s_w, loaded = layers[i]
            eng.wait_ge(s_w, loaded)
            at = off["q" + name][0]
            link(eng.tensor_scalar(wqkv[i][:, :], w[:, at:at + 3 * D], col("lnw" + name), 1.0, ALU.mult, ALU.mult))

        def fold_biases(eng, link, i, bank):
            name = layers[i][0]
            link(eng.tensor_tensor(bfold[i][:, 0:1], bank[:, 2 * B:2 * B + 1], col("bq" + name), ALU.add))
            link(eng.tensor_tensor(bfold[i][:, 1:2], bank[:, 2 * B + 1:2 * B + 2], col("bk" + name), ALU.add))
            r = slice(0, 2 * D) if name != "3" else slice(D, 2 * D)
            c = ROWS.index("bq" + name if name != "3" else "bv3") * 128
            link(eng.tensor_tensor(brow32[i][:, r], bank[0:1, ROW_AT + r.start:ROW_AT + r.stop],
                                   rows[0:1, c:c + r.stop - r.start], ALU.add))
            parts(eng, link, brow32[i][:, r], bleft[i][:, r], [p[:, r] for p in bpart[i]]).then_inc(s_bpart, 1)

        def setup_vector(dve):
            link = linker(dve, s_dve)
            dve.wait_ge(s_m, 48)
            link(dve.tensor_scalar(m1[:, :], m1i[:, :], 1.0, None, ALU.not_equal))
            dve.sem_inc(s_keepT, 1)
            link(dve.tensor_scalar(mleft[:, 0:128], m0[:, :], -1.0, 1.0, ALU.mult, ALU.add))
            link(dve.tensor_scalar(mleft[:, 256:384], m3[:, :], -1.0, 1.0, ALU.mult, ALU.add))
            link(dve.tensor_scalar(madd[:, 0:128], mleft[:, 0:128], -1e6, None, ALU.mult))
            link(dve.tensor_scalar(madd[:, 256:384], mleft[:, 256:384], -1e6, None, ALU.mult))
            link(dve.tensor_scalar(madd[:, 128:256], m1i[:, :], 1.0, -1e30, ALU.is_equal, ALU.mult))
            parts(dve, link, madd[:, :], mleft[:, :], [p[:, :] for p in mpart]).then_inc(s_mpart, 1)
            dve.wait_ge(s_cols, 48)
            fold_weights(dve, link, 0)

        def setup_results(dve):
            raw_out(dve, 0, Pb[1][:, 0:BANK])
            dve.wait_ge(s_keepT, 2)
            for i in range(3):
                last = dve.tensor_copy(keep[i][:, :], Pkeep[:, i * 16:(i + 1) * 16])
            last.then_inc(s_read, 1)

        def setup_scalar(act):
            act.dma_start(w0[:, :], a_w0).then_inc(s_w0, 16)
            act.dma_start(m0[:, :], a_keep0).then_inc(s_m, 16)
            act.dma_start(m1i[:, :], a_mask1).then_inc(s_m, 16)
            act.dma_start(m3[:, :], a_keep3).then_inc(s_m, 16)
            act.wait_ge(s_cols, 48)
            act.activation(semb[:, :], cond[:, :], ACT.Silu).then_inc(s_semb, 1)
            act.preload_act_table_set(LOG_EXP)

        def setup_gpsimd(pool):
            pool.memset(center[:, :], -1.0 / D).then_inc(s_pool, 1)
            pool.memset(ident[:, :], 0.0).then_inc(s_pool, 1)
            pool.memset(heads0[:, :], 1.0).then_inc(s_pool, 1)
            pool.memset(heads1[:, :], 1.0).then_inc(s_pool, 1)
            pool.memset(mean[:, :], 1.0 / D).then_inc(s_cst, 1)
            pool.memset(ones[:, :], 1.0).then_inc(s_cst, 1)
            pool.memset(eps[:, :], EPS).then_inc(s_cst, 1)
            pool.wait_ge(s_pool, 4)
            pool.affine_select(out=center[:, :], in_=center[:, :], compare_op=ALU.not_equal, fill=1.0 - 1.0 / D,
                               base=0, pattern=[[-1, D]], channel_multiplier=1).then_inc(s_cst, 1)
            pool.affine_select(out=ident[:, :], in_=ident[:, :], compare_op=ALU.not_equal, fill=1.0,
                               base=0, pattern=[[-1, D]], channel_multiplier=1).then_inc(s_cst, 1)
            for tile, heads in ((heads0, HEADS[0]), (heads1, HEADS[1])):
                w = D // heads
                v = tile[:, :].rearrange("p (h w) -> p h w", w=w)
                pool.affine_select(out=v, in_=v, compare_op=ALU.is_ge, fill=0.0, base=0,
                                   pattern=[[-w, heads], [0, w]], channel_multiplier=1).then_inc(s_pool, 1)
            pool.wait_ge(s_pool, 6)
            for tile, heads in ((heads0, HEADS[0]), (heads1, HEADS[1])):
                w = D // heads
                v = tile[:, :].rearrange("p (h w) -> p h w", w=w)
                pool.affine_select(out=v, in_=v, compare_op=ALU.is_ge, fill=0.0, base=w - 1,
                                   pattern=[[w, heads], [0, w]], channel_multiplier=-1).then_inc(s_cst, 1)

        def fold_gpsimd(pool, link, i):
            pool.wait_ge(s_cols, 48)
            if 0 < i < 3:
                fold_weights(pool, link, i)
            pool.wait_ge(s_raw, PLACE[i] + 1)
            if i < 3:
                n = layers[i][0]
                fold_biases(pool, link, i, raw[i])
                film_factors(pool, link, i, raw[i], "embs" + n, "embt" + n, "ln2w" + n, "ln2b" + n)
            else:
                film_factors(pool, link, 3, raw[3], "adas", "adat", "g2", "b2")
                link(pool.tensor_scalar(gate[:, :], raw[3][:, 2 * B:3 * B], col("adag"), 0.0, ALU.add, ALU.add))
            pool.sem_inc(s_films, 1)

        def attention_tensor(pe, i):
            s, name, before = s_layer, "01"[i], i * HALVES
            before4 = i * QUARTERS
            mask = mrow[:, i * N:(i + 1) * N]

            def wide(out_, lhsT, rhs, signal, stop=True):
                for c in range(0, NH, BANK):
                    last = pe.matmul(out_[:, c:c + BANK], lhsT, rhs[:, c:c + BANK], start=True, stop=stop)
                last.then_inc(signal, 1)

            for first, q in NORM_ORDER:
                h, c, n = quarter(q)
                if first:
                    if i == 0:
                        pe.wait_ge(s_x[h], 16)
                    else:
                        pe.wait_ge(s["x"], before4 - QUARTERS + q + 1)
                    pe.matmul(Pa[h][:, c], center[:, :], xT[:, n], start=True, stop=True).then_inc(s["mean1"], 1)
                    if i == 0 and q == QUARTERS - 1:
                        setup_products(pe)
                else:
                    pe.wait_ge(s["sq1"], before4 + q + 1)
                    if i == 0 and h == 1:
                        pe.wait_ge(s_read, 1)
                    pe.matmul(Pb[h][:, c], mean[:, :], tmp[h][:, c], start=True, stop=True).then_inc(s["var1"], 1)
            for h in two:
                pe.wait_ge(s["z"], 2 * (before + h + 1))
                if i == 0:
                    pe.wait_ge(s_mrow, 16 * 9)
                else:
                    pe.wait_ge(s_films, 2)
                for c in range(0, NH, BANK):
                    pe.matmul(Pa[h][:, c:c + BANK], wqkv[i][:, D:2 * D], z[h][:, c:c + BANK], start=True, stop=False)
                    last = pe.matmul(Pa[h][:, c:c + BANK], ones[:, :], mask[:, h * NH + c:h * NH + c + BANK],
                                     start=False, stop=True)
                last.then_inc(s["k"], 1)
            for h in two:
                pe.wait_ge(s["rstd1"], 2 * (before + h + 1))
                pe.wait_ge(s_brow[i], 16 * 3)
                last = tiles_and_bias(pe, Pb[h], z[h], wqkv[i][:, 0:D], brow[i][:, 0:D])
                last.then_inc(s["q"], 1)
            for h in two:
                pe.wait_ge(s["ek"], BH * (before + h + 1))
                for t in range(TILES):
                    last = pe.transpose(Pa[h][:, t * 128:(t + 1) * 128], ek[h][:, t * 128:(t + 1) * 128], ident[:, :])
                last.then_inc(s["ekt"], 1)
            for h in two:
                pe.wait_ge(s["ektc"], before + h + 1)
                last = tiles_and_bias(pe, Pa[h], z[h], wqkv[i][:, 2 * D:3 * D], brow[i][:, D:2 * D])
                last.then_inc(s["v"], 1)
            for h in two:
                pe.wait_ge(s["qn"], before + h + 1)
                for t in range(TILES):
                    last = pe.transpose(Pb[h][:, t * 128:(t + 1) * 128], qs[h][:, t * 128:(t + 1) * 128], ident[:, :])
                last.then_inc(s["qnt"], 1)
            for h in two:
                pe.wait_ge(s["vk"], before + h + 1)
                for b in range(BH):
                    for t in (2 * b, 2 * b + 1):
                        one, other = (vk[h], ekT[h]) if i == 0 else (ekT[h], vk[h])
                        last = pe.matmul(Pa[h][:, b * D:(b + 1) * D], one[:, t * D:(t + 1) * D],
                                         other[:, t * D:(t + 1) * D], start=(t == 2 * b), stop=(t == 2 * b + 1))
                last.then_inc(s["att"], 1)
            for h in two:
                pe.wait_ge(s["attm"], before + h + 1)
                for b in range(BH):
                    last = pe.matmul(Pa[h][:, BANK + b * D:BANK + (b + 1) * D], attm[h][:, b * D:(b + 1) * D],
                                     center[:, :], start=True, stop=True)
                last.then_inc(s["attc"], 1)
            for first, q in NORM_ORDER:
                h, c, _ = quarter(q)
                if first:
                    pe.wait_ge(s["attcr"], before + h + 1)
                    pe.wait_ge(s["qtc"], before + h + 1)
                    for g in (2 * q, 2 * q + 1):
                        b = g % BH
                        last = pe.matmul(Pa[h][:, b * T:(b + 1) * T], attc[h][:, b * D:(b + 1) * D],
                                         qT[h][:, b * T:(b + 1) * T], start=True, stop=True)
                    last.then_inc(s["y"], 1)
                else:
                    pe.wait_ge(s["sq2"], before4 + q + 1)
                    pe.matmul(Pb[h][:, c], mean[:, :], tmp[h][:, c], start=True, stop=True).then_inc(s["var2"], 1)
            fold_products(pe, i)
            for q in four:
                h, c, _ = quarter(q)
                pe.wait_ge(s["hs"], before4 + q + 1)
                if q < len(AT_END_OF[i]):
                    pe.wait_ge(s_raw, PLACE[AT_END_OF[i][q][0]] + 1)
                pe.matmul(Pb[h][:, c], mat("out" + name), hs[h][:, c], start=True, stop=True).then_inc(s["o"], 1)

        def attention_scalar(act, i):
            s, before, before4 = s_layer, i * HALVES, i * QUARTERS
            for first, q in NORM_ORDER:
                h, c, _ = quarter(q)
                if first:
                    act.wait_ge(s["mean1"], before4 + q + 1)
                    act.activation(tmp[h][:, c], Pa[h][:, c], ACT.Square).then_inc(s["sq1"], 1)
                else:
                    act.wait_ge(s["var1"], before4 + q + 1)
                    if i == 0 and q == 0:
                        act.wait_ge(s_cst, 7)
                    act.activation(tmp[h][:, c], Pb[h][:, c], ACT.Ln, bias=eps[:, :]).then_inc(s["lnv1"], 1)
                    act.wait_ge(s["lnv1"], before4 + q + 1)
                    act.activation(rstd[h][:, c], tmp[h][:, c], ACT.Exp, scale=-0.5).then_inc(s["rstd1"], 1)
            for h in two:
                act.wait_ge(s["knb"], before + h + 1)
                for b in range(BH):
                    act.activation(ek[h][:, b * T:(b + 1) * T], Pa[h][:, b * T:(b + 1) * T], ACT.Exp,
                                   bias=knb[h][:, b:b + 1], accum_out=ksum[h][:, b:b + 1]).then_inc(s["ek"], 1)
            for h in two:
                act.wait_ge(s["qs"], before + h + 1)
                act.activation(qs[h][:, :], qs[h][:, :], ACT.Exp).then_inc(s["eq"], 1)
                if h == 0:
                    for h2 in two:
                        act.wait_ge(s["ekt"], before + h2 + 1)
                        act.activation(ekT[h2][:, :], Pa[h2][:, :], ACT.Copy).then_inc(s["ektc"], 1)
            for h in two:
                act.wait_ge(s["qnt"], before + h + 1)
                act.activation(qT[h][:, :], Pb[h][:, :], ACT.Copy).then_inc(s["qtc"], 1)
            for first, q in NORM_ORDER:
                h, c, _ = quarter(q)
                if first:
                    act.wait_ge(s["y"], before4 + q + 1)
                    act.activation(tmp[h][:, c], Pa[h][:, c], ACT.Square).then_inc(s["sq2"], 1)
                else:
                    act.wait_ge(s["var2"], before4 + q + 1)
                    act.activation(tmp[h][:, c], Pb[h][:, c], ACT.Ln, bias=eps[:, :]).then_inc(s["lnv2"], 1)
                    act.wait_ge(s["lnv2"], before4 + q + 1)
                    act.activation(rstd[h][:, c], tmp[h][:, c], ACT.Exp, scale=-0.5).then_inc(s["rstd2"], 1)
            for q in four:
                h, c, _ = quarter(q)
                act.wait_ge(s["z2"], before4 + q + 1)
                act.wait_ge(s_films, i + 1)
                for g in (2 * q, 2 * q + 1):
                    b = g % BH
                    last = act.activation(hs[h][:, b * T:(b + 1) * T], z[h][:, b * T:(b + 1) * T], ACT.Silu,
                                          bias=film_t[i][:, g:g + 1], scale=film_s[i][:, g:g + 1])
                last.then_inc(s["hs"], 1)
            act.preload_act_table_set(LOG_EXP)

        def attention_vector(dve, i):
            s, name, before = s_layer, "01"[i], i * HALVES
            before4 = i * QUARTERS
            heads, hw, blockmask = HEADS[i], D // HEADS[i], (heads0, heads1)[i]
            for q in four:
                if i == 0 and q == 2:
                    setup_results(dve)
                h, c, _ = quarter(q)
                dve.wait_ge(s["rstd1"], before4 + q + 1)
                dve.tensor_tensor(z[h][:, c], Pa[h][:, c], rstd[h][:, c], ALU.mult).then_inc(s["z"], 1)
            for h in two:
                dve.wait_ge(s["k"], before + h + 1)
                dve.wait_ge(s_films, i + 1)
                dve.tensor_reduce(kmax[h][:, :], Pa[h][:, :].rearrange("p (b t) -> p b t", t=T), AX.X,
                                  ALU.max).then_inc(s["kmax"], 1)
                dve.wait_ge(s["kmax"], before + h + 1)
                dve.tensor_scalar(kbias[h][:, :], kmax[h][:, :], bfold[i][:, 1:2], None, ALU.add).then_inc(s["kbias"], 1)
                dve.wait_ge(s["kbias"], before + h + 1)
                dve.tensor_scalar(knb[h][:, :], kbias[h][:, :], -1.0, bfold[i][:, 1:2], ALU.mult,
                                  ALU.add).then_inc(s["knb"], 1)
            for h in two:
                dve.wait_ge(s["q"], before + h + 1)
                qv = Pb[h][:, :].rearrange("p (g w) -> p g w", w=hw)
                dve.tensor_reduce(qmax[h][:, 0:TILES * heads], qv, AX.X, ALU.max).then_inc(s["qmax"], 1)
                dve.wait_ge(s["qmax"], before + h + 1)
                dve.tensor_tensor(qs[h][:, :].rearrange("p (g w) -> p g w", w=hw), qv,
                                  qmax[h][:, 0:TILES * heads].unsqueeze(2).to_broadcast([128, TILES * heads, hw]),
                                  ALU.subtract).then_inc(s["qs"], 1)
            for h in two:
                dve.wait_ge(s["eq"], before + h + 1)
                dve.tensor_reduce(qsum[h][:, 0:TILES * heads], qs[h][:, :].rearrange("p (g w) -> p g w", w=hw), AX.X,
                                  ALU.add).then_inc(s["qsum"], 1)
                dve.wait_ge(s["qsum"], before + h + 1)
                dve.reciprocal(rq[h][:, 0:TILES * heads], qsum[h][:, 0:TILES * heads]).then_inc(s["rq"], 1)
            for h in two:
                dve.wait_ge(s["v"], before + h + 1)
                dve.tensor_tensor(vk[h][:, :].rearrange("p (t d) -> p t d", d=D),
                                  Pa[h][:, :].rearrange("p (t d) -> p t d", d=D),
                                  keep[i][:, h * TILES:(h + 1) * TILES].unsqueeze(2).to_broadcast([128, TILES, D]),
                                  ALU.mult).then_inc(s["vk"], 1)
                dve.wait_ge(s["ek"], BH * (before + h + 1))
                dve.reciprocal(rk[h][:, :], ksum[h][:, :]).then_inc(s["rk"], 1)
            for h in two:
                dve.wait_ge(s["att"], before + h + 1)
                if i == 0:
                    dve.tensor_tensor(attm[h][:, :].rearrange("p (b d) -> p b d", d=D),
                                      Pa[h][:, 0:BH * D].rearrange("p (b d) -> p b d", d=D),
                                      blockmask[:, :].unsqueeze(1).to_broadcast([D, BH, D]),
                                      ALU.mult).then_inc(s["attm"], 1)
                else:
                    dve.wait_ge(s["rk"], before + h + 1)
                    for b in range(BH):
                        last = dve.scalar_tensor_tensor(attm[h][:, b * D:(b + 1) * D], Pa[h][:, b * D:(b + 1) * D],
                                                        rk[h][:, b:b + 1], blockmask[:, :], ALU.mult, ALU.mult)
                    last.then_inc(s["attm"], 1)
            for h in two:
                dve.wait_ge(s["attc"], before + h + 1)
                if i == 0:
                    dve.wait_ge(s["rk"], before + h + 1)
                    dve.tensor_tensor(attc[h][:, :].rearrange("p (b d) -> p b d", d=D),
                                      Pa[h][:, BANK:BANK + BH * D].rearrange("p (b d) -> p b d", d=D),
                                      rk[h][:, :].unsqueeze(2).to_broadcast([D, BH, D]),
                                      ALU.mult).then_inc(s["attcr"], 1)
                else:
                    dve.tensor_copy(attc[h][:, :], Pa[h][:, BANK:BANK + BH * D]).then_inc(s["attcr"], 1)
            for q in four:
                h, c, _ = quarter(q)
                dve.wait_ge(s["rstd2"], before4 + q + 1)
                dve.tensor_tensor(z[h][:, c], Pa[h][:, c], rstd[h][:, c], ALU.mult).then_inc(s["z2"], 1)
            for k, bank in AT_END_OF[i]:
                raw_out(dve, k, bank)
            for q in four:
                h, c, n = quarter(q)
                dve.wait_ge(s["o"], before4 + q + 1)
                dve.scalar_tensor_tensor(xT[:, n], Pb[h][:, c], col("bout" + name), xT[:, n],
                                         ALU.add, ALU.add).then_inc(s["x"], 1)

        def attention_gpsimd(pool, i):
            s, before, heads, hw = s_layer, i * HALVES, HEADS[i], D // HEADS[i]
            for h in two:
                pool.wait_ge(s["rq"], before + h + 1)
                v = qs[h][:, :].rearrange("p (g w) -> p g w", w=hw)
                pool.tensor_tensor(v, v, rq[h][:, 0:TILES * heads].unsqueeze(2).to_broadcast([128, TILES * heads, hw]),
                                   ALU.mult).then_inc(s["qn"], 1)

        def times_u(pool, h, c, s_dtu, s_fresh):
            pool.tensor_tensor(dtu[c][:, toks(h)], dt[c][:, toks(h)], u[c][:, toks(h)], ALU.mult).then_inc(s_dtu, 1)
            pool.wait_ge(s_dtu, c + 1)
            pool.memset(batches(dt[c][:, toks(h)])[:, :, 0:1], 1e37).then_inc(s_fresh, 1)

        FILM_ON_ACT = (4, 5)
        FILM_ON_POOL = tuple(g for g in range(B) if g not in FILM_ON_ACT)

        def mamba_tensor(pe):
            s = s_mamba

            def wide(out_, lhsT, rhs, start=True, stop=True):
                for c in range(0, NH, BANK):
                    last = pe.matmul(out_[:, c:c + BANK], lhsT, rhs[:, c:c + BANK], start=start, stop=stop)
                return last

            for first, q in NORM_ORDER:
                h, c, n = quarter(q)
                if first:
                    pe.wait_ge(s_layer["x"], QUARTERS + q + 1)
                    pe.matmul(Pa[h][:, c], center[:, :], xT[:, n], start=True, stop=True).then_inc(s["mean"], 1)
                else:
                    pe.wait_ge(s["sq"], q + 1)
                    pe.matmul(Pb[h][:, c], mean[:, :], tmp[h][:, c], start=True, stop=True).then_inc(s["var"], 1)
            for h in two:
                for c in range(CH):
                    for k in range(0, NH, BANK):
                        last_batch = h * BH + (k + BANK) // T - 1
                        for signal, batches_of in ((s["xn"], FILM_ON_POOL), (s["xna"], FILM_ON_ACT)):
                            count = sum(g <= last_batch for g in batches_of)
                            if count:
                                pe.wait_ge(signal, count)
                        last = pe.matmul(P[h][c][:, k:k + BANK], mat("inp", c, 128), xn[h][:, k:k + BANK], start=True, stop=True)
                    last.then_inc(s["u"], 1)

            def z_projection(h, c):
                pe.wait_ge(s["taps"], (h * CH + c + 1) * (TAPS - 1))
                wide(P[h][c], mat("inp", CH + c, 128), xn[h]).then_inc(s["zp"], 1)

            def from_u(h, c):
                pe.wait_ge(s["us"], CH * h + 2)
                pe.wait_ge(s["zs"], CH * h + c + 1)
                for k in range(0, NH, BANK):
                    for c2 in range(CH):
                        uk = u[c2][:, h * NH + k:h * NH + k + BANK]
                        if c == 0:
                            last = pe.matmul(Pa[h][0:RANK, k:k + BANK], mat("xdt", c2, RANK), uk,
                                             start=(c2 == 0), stop=(c2 == CH - 1))
                        else:
                            last = pe.matmul(Pb[h][:, k:k + BANK], xbc3[:, c2 * 128:(c2 + 1) * 128], uk,
                                             start=(c2 == 0), stop=(c2 == CH - 1))
                last.then_inc(s["dtr" if c == 0 else "bcp"], 1)

            def dt_projection(h, c):
                if c == 0:
                    pe.wait_ge(s["dtrc"], h + 1)
                else:
                    pe.wait_ge(s["r1"], h + 1)
                wide(P[h][c], dtp[:, c * 128:(c + 1) * 128], dtr[h]).then_inc(s["dtp"], 1)

            pe.wait_ge(s["xbc"], 3 * CH)
            z_projection(0, 0)
            z_projection(0, 1)
            z_projection(1, 0)
            from_u(0, 0)
            z_projection(1, 1)
            from_u(0, 1)
            from_u(1, 0)
            dt_projection(0, 0)
            dt_projection(0, 1)
            from_u(1, 1)
            dt_projection(1, 0)
            dt_projection(1, 1)

        def mamba_scalar(act):
            s = s_mamba
            act.activation(ea[:, :], mat("alog"), ACT.Exp).then_inc(s["ea"], 1)
            for first, q in NORM_ORDER:
                h, c, _ = quarter(q)
                if first:
                    act.wait_ge(s["mean"], q + 1)
                    act.activation(tmp[h][:, c], Pa[h][:, c], ACT.Square).then_inc(s["sq"], 1)
                else:
                    act.wait_ge(s["var"], q + 1)
                    act.activation(tmp[h][:, c], Pb[h][:, c], ACT.Ln, bias=eps[:, :]).then_inc(s["lnv"], 1)
                    act.wait_ge(s["lnv"], q + 1)
                    act.activation(rstd[h][:, c], tmp[h][:, c], ACT.Exp, scale=-0.5).then_inc(s["rstd"], 1)
            act.wait_ge(s_films, 3)
            for g in FILM_ON_ACT:
                h, b = divmod(g, BH)
                act.wait_ge(s["z"], g // 2 + 1)
                act.activation(xn[h][:, b * T:(b + 1) * T], z[h][:, b * T:(b + 1) * T], ACT.Identity,
                               bias=film_t[3][:, g:g + 1], scale=film_s[3][:, g:g + 1]).then_inc(s["xna"], 1)

            def last_tap(i):
                h, c = divmod(i, CH)
                act.wait_ge(s["u"], i + 1)
                act.activation(u[c][:, toks(h)], P[h][c][:, :], ACT.Identity, bias=col(f"convb_{c}"),
                               scale=mat("convw", (c + 1) * TAPS - 1, 1)).then_inc(s["tap"], 1)

            def silu_u(i):
                h, c = divmod(i, CH)
                act.wait_ge(s["taps"], (i + 1) * (TAPS - 1))
                act.activation(u[c][:, toks(h)], u[c][:, toks(h)], ACT.Silu).then_inc(s["us"], 1)

            def silu_z(i):
                h, c = divmod(i, CH)
                act.wait_ge(s["zp"], i + 1)
                act.activation(zs[c][:, toks(h)], P[h][c][:, :], ACT.Silu).then_inc(s["zs"], 1)

            def leading_parts(h):
                act.wait_ge(s["bcp"], h + 1)
                act.activation(bc[:, toks(h)], Pb[h][:, :], ACT.Copy).then_inc(s["bc1"], 1)

            def rank_rows(h):
                act.wait_ge(s["dtr"], h + 1)
                act.activation(dtr[h][:, :], Pa[h][0:RANK, :], ACT.Copy).then_inc(s["dtrc"], 1)

            last_tap(0)
            last_tap(1)
            last_tap(2)
            silu_u(0)
            last_tap(3)
            silu_u(1)
            silu_z(0)
            silu_z(1)
            silu_u(2)
            rank_rows(0)
            silu_z(2)
            silu_u(3)
            silu_z(3)
            act.preload_act_table_set(LOG_EXP)
            leading_parts(0)
            rank_rows(1)
            def log_of_one_and_exp(h, c):
                k = h * CH + c + 1
                act.wait_ge(s["clamp"], k)
                act.activation(dt[c][:, toks(h)], dt[c][:, toks(h)], ACT.Exp).then_inc(s["eab"], 1)
                act.wait_ge(s["eab"], k)
                act.activation(dt[c][:, toks(h)], dt[c][:, toks(h)], ACT.Ln, bias=one[:, :]).then_inc(s["lab"], 1)

            log_of_one_and_exp(0, 0)
            log_of_one_and_exp(0, 1)
            leading_parts(1)
            log_of_one_and_exp(1, 0)
            log_of_one_and_exp(1, 1)

        def mamba_vector(dve):
            s = s_mamba
            dve.tensor_tensor(sel0[:, :], ident[:, 0:2 * NS], ident[:, 64:64 + 2 * NS], ALU.add).then_inc(s["sel0"], 1)
            dve.wait_ge(s["sel0"], 1)
            dve.tensor_tensor(sel1[:, :], sel0[:, :], ident[:, 96:96 + 2 * NS], ALU.add).then_inc(s["sel1"], 1)
            dve.wait_ge(s["ea"], 1)
            dve.tensor_scalar(acoef[:, :], ea[:, :], -1.0, -1e-35, ALU.mult, ALU.min).then_inc(s["acoef"], 1)
            for q in four:
                h, c, _ = quarter(q)
                dve.wait_ge(s["rstd"], q + 1)
                dve.tensor_tensor(z[h][:, c], Pa[h][:, c], rstd[h][:, c], ALU.mult).then_inc(s["z"], 1)

            def other_taps(i):
                h, c = divmod(i, CH)
                dve.wait_ge(s["tap"], i + 1)
                for k in range(1, TAPS):
                    if k > 1:
                        dve.wait_ge(s["taps"], i * (TAPS - 1) + k - 1)
                    tap = mat("convw", (c + 1) * TAPS - 1 - k, 1)
                    later = batches(u[c][:, toks(h)])[:, :, k:]
                    dve.scalar_tensor_tensor(later, batches(P[h][c][:, :])[:, :, 0:T - k], tap, later,
                                             ALU.mult, ALU.add).then_inc(s["taps"], 1)

            def below_leading(h):
                k = h + 1
                dve.wait_ge(s["bc1"], k)
                dve.tensor_tensor(tmp[h][64:128, :], Pb[h][64:128, :], bc[64:128, toks(h)], ALU.subtract).then_inc(s["r1"], 1)

            def other_parts(h):
                k = h + 1
                dve.wait_ge(s["r1"], k)
                dve.tensor_copy(bc[64:128, toks(h)], tmp[h][64:128, :]).then_inc(s["bc2"], 1)
                dve.wait_ge(s["bc2"], k)
                dve.tensor_tensor(bc[96:128, toks(h)], tmp[h][96:128, :], bc[96:128, toks(h)], ALU.subtract).then_inc(s["bc3"], 1)

            def clamp(h, c):
                dve.wait_ge(s["dtp"], h * CH + c + 1)
                dve.tensor_scalar(dt[c][:, toks(h)], P[h][c][:, :], col(f"dtb_{c}"), 30.0, ALU.add, ALU.min).then_inc(s["clamp"], 1)

            def softplus(h, c):
                dve.wait_ge(s["lab"], h * CH + c + 1)
                dve.scalar_tensor_tensor(dt[c][:, toks(h)], P[h][c][:, :], col(f"dtb_{c}"), dt[c][:, toks(h)],
                                         ALU.add, ALU.max).then_inc(s_dt, 1)

            for i in range(HALVES * CH):
                other_taps(i)
            below_leading(0)
            other_parts(0)
            clamp(0, 0)
            clamp(0, 1)
            softplus(0, 0)
            below_leading(1)
            clamp(1, 0)
            softplus(0, 1)
            clamp(1, 1)
            other_parts(1)
            softplus(1, 0)
            softplus(1, 1)

        def mamba_gpsimd(pool):
            s = s_mamba
            pool.memset(one[:, :], 1.0).then_inc(s["pad"], 1)
            pool.memset(xbc3[:, :], 0.0).then_inc(s["pad"], 1)
            pool.wait_ge(s["pad"], 2)
            for c in range(CH):
                for at in (0, 64, 96):
                    pool.tensor_copy(xbc3[:, c * 128 + at:c * 128 + at + 2 * NS], mat("xbc", c, 2 * NS)).then_inc(s["xbc"], 1)
            for g in FILM_ON_POOL:
                h, b = divmod(g, BH)
                pool.wait_ge(s["z"], g // 2 + 1)
                pool.tensor_scalar(xn[h][:, b * T:(b + 1) * T], z[h][:, b * T:(b + 1) * T], film_s[3][:, g:g + 1],
                                   film_t[3][:, g:g + 1], ALU.mult, ALU.add).then_inc(s["xn"], 1)
            pool.wait_ge(s["sel1"], 1)
            pool.tensor_copy(sel[:, :, :], sel1[:, :].unsqueeze(2).to_broadcast([128, 2 * NS, 128])).then_inc(s["sel"], 1)
            for c in range(CH):
                pool.wait_ge(s_dt, c + 1)
                times_u(pool, 0, c, s_dtu, s["fresh"])

        def mamba_scan(u, zs, dt, dtu, bc, sel, acoef):
            with ExitStack() as on:
                (s_dtu, s_fresh, s_b, s_c, s_dA, s_bu, s_h, s_ccopy, s_hc, s_y, s_ym, s_ym0, s_skip, s_o, s_x) = (
                    sem(f"v_{n}", on) for n in "dtu fresh b c dA bu h ccopy hc y ym ym0 skip o x".split())

                def twice(n):
                    return [[sb(f"{n}{p}_{c}", [128, NH], f32, on) for c in range(CH)] for p in range(2)]

                dA, bu, hst, hc = twice("dA"), twice("bu"), twice("hst"), twice("hc")
                cs = [sb(f"cs{p}", [128, NH], f32, on) for p in range(2)]
                ym = u
                Pbb, Pcb = ps("Pbb", [128, NH], f32, on), ps("Pcb", [128, NH], f32, on)
                Py = [ps(f"Py{c}", [128, NH], f32, on) for c in range(CH)]
                two = range(HALVES)

                def toks(h):
                    return slice(h * NH, (h + 1) * NH)

                def steps(eng, h, one):
                    for p in range(2):
                        one(p, h * NS + p, p, h == 0, False, p)
                    with eng.Fori(2, NS - 2, 2) as n:
                        for p in range(2):
                            one(n + p, n + (h * NS + p), p, False, False, None)
                    for p in range(2):
                        one(NS - 2 + p, h * NS + NS - 2 + p, p, False, p == 1, None)

                block = on.enter_context(nc.Block())

                @block.tensor
                def _(pe):
                    def spread(out_, which, n, h, signal):
                        for k in range(0, NH, BANK):
                            last = pe.matmul(out_[:, k:k + BANK], sel[:, bass.ds(n + which * NS, 1), :],
                                             bc[:, h * NH + k:h * NH + k + BANK], start=True, stop=True)
                        last.then_inc(signal, 1)

                    def add_up(at, parity, opens=False):
                        for c in range(CH):
                            pe.wait_ge(s_hc, at * CH + c + 1)
                            for k in range(0, NH, BANK):
                                last = pe.matmul(Py[c][:, k:k + BANK], ident[:, :], hc[parity][c][:, k:k + BANK], start=opens,
                                                 stop=True, skip_group_check=True)
                            last.then_inc(s_y, 1)

                    def reduce(n, at, parity, first, last_of_half, place):
                        if not last_of_half:
                            pe.wait_ge(s_bu, (at + 1) * CH)
                            spread(Pbb, 0, n + 1, half[0], s_b)
                            pe.wait_ge(s_ccopy, at + 1)
                            spread(Pcb, 1, n + 1, half[0], s_c)
                        elif half[0] + 1 < HALVES:
                            first_spread(half[0] + 1)
                        else:
                            pe.wait_ge(s_bu, HALVES * NS * CH)
                            output_projection(0)
                        if place == 1 and half[0]:
                            pe.wait_ge(s_skip, half[0] * CH)
                        if place != 0:
                            add_up(at - 1, 1 - parity, opens=place == 1)

                    def output_projection(h):
                        P = (Pbb, Pcb)[h]
                        if h == 0:
                            pe.wait_ge(s_ym, CH)
                        for k in range(0, NH, BANK):
                            if h:
                                pe.wait_ge(s_ym0, k // BANK + 1)
                                pe.wait_ge(s_ym, CH + k // BANK + 1)
                            for c in range(CH):
                                last = pe.matmul(P[:, k:k + BANK], mat("outp", c, 128), ym[c][:, h * NH + k:h * NH + k + BANK],
                                                 start=(c == 0), stop=(c == CH - 1))
                            last.then_inc(s_o, 1)

                    def first_spread(h):
                        if h:
                            pe.wait_ge(s_bu, h * NS * CH)
                        spread(Pbb, 0, 0, h, s_b)
                        if h:
                            pe.wait_ge(s_ccopy, h * NS)
                        spread(Pcb, 1, 0, h, s_c)

                    half = [0]
                    first_spread(0)
                    for h in two:
                        half[0] = h
                        steps(pe, h, reduce)
                        add_up((h + 1) * NS - 1, 1)
                    output_projection(1)

                @block.scalar
                def _(act):
                    def decay(n, at, parity, first, last_of_half, place):
                        if place == 0 and half[0]:
                            act.wait_ge(s_fresh, CH)
                        for c in range(CH):
                            if not first:
                                act.wait_ge(s_h, (at - 2) * CH + c + 1)
                            act.activation(dA[parity][c][:, :], dt[c][:, toks(half[0])], ACT.Exp,
                                           scale=acoef[:, bass.ds(n + c * NS, 1)]).then_inc(s_dA, 1)
                        act.wait_ge(s_c, at + 1)
                        if not first:
                            act.wait_ge(s_hc, (at - 1) * CH)
                        act.activation(cs[parity][:, :], Pcb[:, :], ACT.Copy).then_inc(s_ccopy, 1)

                    half = [0]
                    for h in two:
                        half[0] = h
                        steps(act, h, decay)

                @block.vector
                def _(dve):
                    def add_skip(h, c):
                        dve.wait_ge(s_y, ((h + 1) * NS - 1) * CH + c + 1)
                        dve.scalar_tensor_tensor(ym[c][:, toks(h)], u[c][:, toks(h)], col(f"dp_{c}"), Py[c][:, :],
                                                 ALU.mult, ALU.add).then_inc(s_skip, 1)

                    def times_silu_z(h, c, n):
                        dve.wait_ge(s_skip, h * CH + c + 1)
                        dve.tensor_tensor(ym[c][:, n], ym[c][:, n], zs[c][:, n], ALU.mult).then_inc(s_ym, 1)

                    def scan(n, at, parity, first, last_of_half, place):
                        dve.wait_ge(s_b, at + 1)
                        if place == 0 and half[0]:
                            dve.wait_ge(s_dtu, CH)
                        for c in range(CH):
                            if not first:
                                dve.wait_ge(s_h, (at - 2) * CH + c + 1)
                            dve.tensor_tensor(bu[parity][c][:, :], dtu[c][:, toks(half[0])], Pbb[:, :], ALU.mult).then_inc(s_bu, 1)
                        for c in range(CH):
                            dve.wait_ge(s_dA, at * CH + c + 1)
                            dve.wait_ge(s_bu, at * CH + c + 1)
                            if not first:
                                dve.wait_ge(s_hc, (at - 2) * CH + c + 1)
                            dve.tensor_tensor_scan(hst[parity][c][:, :], dA[parity][c][:, :], bu[parity][c][:, :], 0.0,
                                                   ALU.mult, ALU.add).then_inc(s_h, 1)

                        if half[0] and place is not None:
                            for c in range(CH):
                                if place == 0:
                                    add_skip(half[0] - 1, c)
                                else:
                                    times_silu_z(half[0] - 1, c, toks(half[0] - 1))

                    half = [0]
                    for h in two:
                        half[0] = h
                        steps(dve, h, scan)
                    for c in range(CH):
                        add_skip(1, c)
                    for q in (2, 3):
                        times_silu_z(1, CH - 1, quarter(q)[2])
                    for q in four:
                        h, at, _ = quarter(q)
                        dve.wait_ge(s_o, q + 1)
                        for b in range(at.start // T, at.stop // T):
                            xb = xT[:, (h * BH + b) * T:(h * BH + b + 1) * T]
                            dve.scalar_tensor_tensor(xb, (Pbb, Pcb)[h][:, b * T:(b + 1) * T],
                                                     gate[:, h * BH + b:h * BH + b + 1], xb, ALU.mult, ALU.add).then_inc(s_x, 1)

                @block.gpsimd
                def _(pool):
                    def times_c(n, at, parity, first, *_):
                        pool.wait_ge(s_ccopy, at + 1)
                        for c in range(CH):
                            pool.wait_ge(s_h, at * CH + c + 1)
                            if not first:
                                pool.wait_ge(s_y, (at - 2) * CH + c + 1)
                            pool.tensor_tensor(hc[parity][c][:, :], hst[parity][c][:, :], cs[parity][:, :],
                                               ALU.mult).then_inc(s_hc, 1)

                    for c in range(CH):
                        times_u(pool, 1, c, s_dtu, s_fresh)
                    for h in two:
                        steps(pool, h, times_c)
                    pool.wait_ge(s_skip, CH + 1)
                    for q in (2, 3):
                        n = quarter(q)[2]
                        pool.tensor_tensor(ym[0][:, n], ym[0][:, n], zs[0][:, n], ALU.mult).then_inc(s_ym0, 1)

        H3 = HEADS[2]
        W3 = D // H3
        QPARTS, KPARTS = (0, 0, 0, 1, 1, 2), (0, 1, 2, 0, 1, 0)
        MASK_AT, MAX_AT = 64, 96
        KMAX, KEXP = MASK_AT + 3, MAX_AT + 3
        VW = 32
        HALF = H3 // 2
        LOADS = 16 * 7

        def softmax_layer():
            with ExitStack() as keep3:
                q_parts = nc.dram_tensor("q_parts", (B, 3, W3, H3, T), bf16, kind="Internal").ap()
                k_parts = nc.dram_tensor("k_parts", (B, 3, W3, H3, T), bf16, kind="Internal").ap()
                s_ld = [[sem(f"t_ld{p}_{i}", keep3) for i in range(2)] for p in range(2)]
                s_written = [{n: sem(f"s_written_{n}{h}", keep3) for n in "qk"} for h in range(HALVES)]
                vc = sb("vc", [128, N // 128, D], f32, keep3)
                vs = [sb(f"vs{p}", [128, 2, H3, VW], f32, keep3) for p in range(2)]
                qst = [sb(f"qst{p}", [128, H3, T], bf16, keep3) for p in range(2)]
                kst = [sb(f"kst{p}", [128, H3, T], bf16, keep3) for p in range(2)]
                identb = sb("identb", [128, 128], bf16, keep3)
                yT = sb("yT", [D, N], f32, keep3)
                part = {n: [sb(f"{n}part{j}", [D, N], bf16, keep3) for j in range(3)] for n in "qk"}

                def write(eng, h, n, j):
                    dst = {"q": q_parts, "k": k_parts}[n]
                    eng.dma_start(dst[h * BH:(h + 1) * BH, j].rearrange("b c h t -> (c h) b t"),
                                  part[n][j][:, h * NH:(h + 1) * NH].rearrange("p (b t) -> p b t", t=T)).then_inc(
                                      s_written[h][n], 16)

                def load(eng, b, p, i, written=None):
                    heads = slice(i * HALF, (i + 1) * HALF)
                    one = bass.ds(b, 1)
                    eng.dma_start(kst[p][MASK_AT:KMAX, heads, :], mrow[:, bass.ds(b * T + 2 * N, T)].unsqueeze(1).to_broadcast(
                        [3, HALF, T])).then_inc(s_ld[p][i], 16)
                    if written:
                        eng.wait_ge(written["q"], 16 * 3)
                    at = 0
                    for j, times in ((0, 3), (1, 2), (2, 1)):
                        src = q_parts[one, j, :, heads, :].rearrange("o c h t -> o c (h t)")
                        eng.dma_start(qst[p][at:at + times * W3, heads, :],
                                     src.to_broadcast([times, W3, HALF * T])).then_inc(s_ld[p][i], 16)
                        at += times * W3
                    if written:
                        eng.wait_ge(written["k"], 16 * 3)
                    at = 0
                    for times in (3, 2, 1):
                        src = k_parts[one, 0:times, :, heads, :].rearrange("o j c h t -> (o j c) (h t)")
                        eng.dma_start(kst[p][at:at + times * W3, heads, :], src).then_inc(s_ld[p][i], 16)
                        at += times * W3

                softmax_projections(vc, vs, qst, kst, identb, part, s_written, write, load)
                softmax_attention(vc, vs, qst, kst, identb, yT, s_written, s_ld, write, load)
                softmax_output(yT)

        def softmax_projections(vc, vs, qst, kst, identb, part, s_written, write, load):
            with ExitStack() as on:
                names = ("mean", "z", "q", "q1", "q2", "q3", "r1", "k", "k1", "k2", "k3", "kr1",
                         "v", "vk", "zero", "kst_zero", "ones", "identb")
                s = {n: sem(f"a_{n}", on) for n in names}
                before = 2 * QUARTERS
                two = range(HALVES)

                def pair(n, shape, dt_=f32):
                    return [sb(f"a{n}_{h}", shape, dt_, on) for h in two]

                tmp, rstd, z = pair("tmp", [D, NH]), pair("rstd", [D, NH]), pair("z", [D, NH])
                left = {"q": pair("lq", [D, NH]), "k": pair("lk", [D, NH])}
                Pa = [ps(f"aPa_{h}", [128, NH], f32, on) for h in two]
                Pb = [ps(f"aPb_{h}", [128, NH], f32, on) for h in two]

                def toks(h):
                    return slice(h * NH, (h + 1) * NH)

                block = on.enter_context(nc.Block())

                @block.sync
                def _(sp):
                    for j in range(3):
                        for n in "qk":
                            sp.wait_ge(s[f"{n}{j + 1}"], 1)
                            write(sp, 0, n, j)
                    sp.wait_ge(s["ones"], 2)
                    load(sp, 0, 0, 0, s_written[0])

                @block.gpsimd
                def _(pool):
                    pool.tensor_copy(identb[:, :], ident[:, :]).then_inc(s["identb"], 1)
                    at = 0
                    for p in range(2):
                        for zeros in (qst[p][:, :, :].bitcast(f32), vs[p][:, :, :, :]):
                            pool.memset(zeros, 0.0).then_inc(s["zero"], 1)
                        if p == 0:
                            pool.memset(kst[p][:, :, :].bitcast(f32), 0.0).then_inc(s["zero"], 1)
                        else:
                            pool.wait_ge(s["kst_zero"], 1)
                        pool.wait_ge(s["zero"], 2 * p + 3)
                        if p == 0:
                            pool.wait_ge(s["identb"], 1)
                        for rows_of_ones in (qst[p][MASK_AT:KMAX, :, :], kst[p][MAX_AT:KEXP, :, :], vs[p][:, :, :, W3:W3 + 1]):
                            if at:
                                pool.wait_ge(s["ones"], at)
                            pool.memset(rows_of_ones, 1.0).then_inc(s["ones"], 1)
                            at += 1
                        pool.wait_ge(s["ones"], at)

                @block.tensor
                def _(pe):
                    def wide(out_, lhsT, rhs):
                        for c in range(0, NH, BANK):
                            last = pe.matmul(out_[:, c:c + BANK], lhsT, rhs[:, c:c + BANK], start=True, stop=True)
                        return last

                    for first, q in NORM_ORDER:
                        h, c, n = quarter(q)
                        if first:
                            pe.matmul(Pa[h][:, c], center[:, :], xT[:, n], start=True, stop=True).then_inc(s["mean"], 1)
                        else:
                            pe.wait_ge(s_layer["sq1"], before + q + 1)
                            pe.matmul(Pb[h][:, c], mean[:, :], tmp[h][:, c], start=True, stop=True).then_inc(s_layer["var1"], 1)
                    for h in two:
                        pe.wait_ge(s["z"], 2 * (h + 1))
                        wide(Pa[h], wqkv[2][:, 0:D], z[h]).then_inc(s["q"], 1)
                        pe.wait_ge(s_layer["rstd1"], before + 2 * (h + 1))
                        wide(Pb[h], wqkv[2][:, D:2 * D], z[h]).then_inc(s["k"], 1)
                    for h in two:
                        pe.wait_ge(s["r1"], h + 1)
                        last = tiles_and_bias(pe, Pa[h], z[h], wqkv[2][:, 2 * D:3 * D], brow[2][:, D:2 * D])
                        last.then_inc(s["v"], 1)

                @block.scalar
                def _(act):
                    for first, q in NORM_ORDER:
                        h, c, _ = quarter(q)
                        if first:
                            act.wait_ge(s["mean"], q + 1)
                            act.activation(tmp[h][:, c], Pa[h][:, c], ACT.Square).then_inc(s_layer["sq1"], 1)
                        else:
                            act.wait_ge(s_layer["var1"], before + q + 1)
                            act.activation(tmp[h][:, c], Pb[h][:, c], ACT.Ln, bias=eps[:, :]).then_inc(s_layer["lnv1"], 1)
                            act.wait_ge(s_layer["lnv1"], before + q + 1)
                            act.activation(rstd[h][:, c], tmp[h][:, c], ACT.Exp, scale=-0.5).then_inc(s_layer["rstd1"], 1)
                    qk = (("q", Pa, 0, "r1"), ("k", Pb, 1, "kr1"))
                    for h in two:
                        for n, P, bias, _ in qk:
                            act.wait_ge(s[n], h + 1)
                            act.activation(part[n][0][:, toks(h)], P[h][:, :], ACT.Identity,
                                           bias=bfold[2][:, bias:bias + 1]).then_inc(s[n + "1"], 1)
                        for n, _, _, r in qk:
                            act.wait_ge(s[r], h + 1)
                            act.activation(part[n][1][:, toks(h)], left[n][h][:, :], ACT.Copy).then_inc(s[n + "2"], 1)
                    act.wait_ge(s["v"], HALVES)
                    for t in range(TILES):
                        act.activation(vc[:, TILES + t, :], Pa[1][:, t * D:(t + 1) * D], ACT.Copy,
                                       scale=keep[2][:, TILES + t:TILES + t + 1]).then_inc(s["vk"], 1)

                @block.vector
                def _(dve):
                    dve.memset(kst[1][:, :, :].bitcast(f32), 0.0).then_inc(s["kst_zero"], 1)
                    for q in four:
                        h, c, _ = quarter(q)
                        dve.wait_ge(s_layer["rstd1"], before + q + 1)
                        dve.tensor_tensor(z[h][:, c], Pa[h][:, c], rstd[h][:, c], ALU.mult).then_inc(s["z"], 1)
                    for h in two:
                        for n, P, bias, r in (("q", Pa, 0, "r1"), ("k", Pb, 1, "kr1")):
                            dve.wait_ge(s[n + "1"], h + 1)
                            dve.scalar_tensor_tensor(left[n][h][:, :], P[h][:, :], bfold[2][:, bias:bias + 1],
                                                     part[n][0][:, toks(h)], ALU.add, ALU.subtract).then_inc(s[r], 1)
                        for n in "qk":
                            dve.wait_ge(s[n + "2"], h + 1)
                            dve.tensor_tensor(part[n][2][:, toks(h)], left[n][h][:, :], part[n][1][:, toks(h)],
                                              ALU.subtract).then_inc(s[n + "3"], 1)
                    dve.wait_ge(s["v"], 1)
                    dve.tensor_tensor(vc[:, 0:TILES, :], Pa[0][:, :].rearrange("p (t d) -> p t d", d=D),
                                      keep[2][:, 0:TILES].unsqueeze(2).to_broadcast([128, TILES, D]),
                                      ALU.mult).then_inc(s["vk"], 1)

        def softmax_attention(vc, vs, qst, kst, identb, yT, s_written, s_ld, write, load):
            PAIRS = H3 // 2
            SETS = H3 // 4
            with ExitStack() as on:
                (s_vs, s_s1, s_mx, s_s2, s_e, s_pv, s_ev, s_t1, s_rc, s_t1d, s_t2, s_t2d, s_nm, s_nmc, s_np, s_nz, s_neg) = (
                    sem(f"t_{n}", on) for n in "vs s1 mx s2 e pv ev t1 rc t1d t2 t2d nm nmc np nz neg".split())
                E = [sb(f"E{p}", [128, 4, 2, T], f32, on) for p in range(2)]
                yraw = [sb(f"yraw{p}", [128, 4, T], f32, on) for p in range(2)]
                ytok = [sb(f"ytok{p}", [128, 2, D], f32, on) for p in range(2)]
                rec = [sb(f"rec{p}", [128, 2, H3], f32, on) for p in range(2)]
                mx = sb("mx", [128, H3, 2], f32, on)
                nleft = sb("nleft", [128, 2, HALF], f32, on)
                nm = sb("nm", [128, 2, 2, 128 // HALF, HALF], bf16, on)
                nmT = [sb(f"nmT{i}", [3 * HALF, T], bf16, on) for i in range(2)]
                S1 = [ps(f"S1_{i}", [128, 2, T], f32, on) for i in range(2)]
                S2 = [ps(f"S2_{i}", [128, 2, 2, T], f32, on) for i in range(2)]
                PV = ps("PV", [128, 2, T], f32, on)
                Pm = ps("Pm", [128, BANK], f32, on)

                def steps(eng, body):
                    body(0, 0, True, False)
                    body(1, 1, False, False)
                    with eng.Fori(2, B - 3, 2) as b:
                        for p in range(2):
                            body(b + p, p, False, False)
                    body(B - 2, 0, False, False)
                    body(B - 1, 1, False, True)

                block = on.enter_context(nc.Block())

                @block.sync
                def _(sp):
                    def maxima_rows(b, p, i):
                        sp.wait_ge(s_nmc, b * 2 + (i + 1))
                        for j in range(3):
                            sp.dma_start(qst[p][MAX_AT + j:MAX_AT + j + 1, i * HALF:(i + 1) * HALF, :],
                                         nmT[i][j * HALF:(j + 1) * HALF, :]).then_inc(s_neg, 16)

                    load(sp, 0, 0, 1)
                    maxima_rows(0, 0, 0)
                    for n in "qk":
                        sp.wait_ge(s_written[1][n], 16 * 3)
                    with sp.Fori(0, B - 3, 2) as b:
                        for p in range(2):
                            maxima_rows(b + p, p, 1)
                            sp.wait_ge(s_s2, (b + p) * PAIRS + PAIRS // 2)
                            load(sp, b + (p + 2), p, 0)
                            maxima_rows(b + (p + 1), 1 - p, 0)
                            sp.wait_ge(s_s2, (b + p) * PAIRS + PAIRS)
                            load(sp, b + (p + 2), p, 1)
                    maxima_rows(B - 2, 0, 1)
                    maxima_rows(B - 1, 1, 0)
                    maxima_rows(B - 1, 1, 1)
                    for p in range(2):
                        for i in range(2):
                            sp.wait_ge(s_ld[p][i], LOADS * B // 2)
                    sp.wait_ge(s_neg, 3 * 16 * 2 * B)

                @block.gpsimd
                def _(pool):
                    def copy_v(b, p):
                        pool.tensor_copy(vs[p][:, :, :, 0:W3], vc[:, bass.ds(b * 2, 2), :].rearrange(
                            "p t (h w) -> p t h w", w=W3)).then_inc(s_vs, 1)

                    for p in range(2):
                        copy_v(p, p)
                    with pool.Fori(2, B - 1, 2) as b:
                        for p in range(2):
                            pool.wait_ge(s_pv, (b + (p - 1)) * SETS)
                            copy_v(b + p, p)

                @block.tensor
                def _(pe):
                    def scores_for_max(at, h, p, wait):
                        if wait:
                            pe.wait_ge(s_mx, at * H3 + (h - 1))
                        for nt in range(2):
                            last = pe.matmul(S1[h % 2][:, nt, :], qst[p][0:KMAX, h, nt * 128:(nt + 1) * 128], kst[p][0:KMAX, h, :],
                                             start=True, stop=True)
                        last.then_inc(s_s1, 1)

                    def maxima_to_rows(at, i, free, value):
                        pe.wait_ge(s_np, at * 8 + (i + 1) * 4)
                        if free is not None:
                            pe.wait_ge(free, value)
                        for nt in range(2):
                            last = pe.transpose(Pm[:, nt * 64:(nt + 1) * 64].bitcast(bf16),
                                                nm[:, i, nt, :, :].rearrange("p a h -> p (a h)"), identb[:, :])
                        last.then_inc(s_nm, 1)

                    def times_v(b, st, p, first, mt):
                        if mt == 0:
                            pe.wait_ge(s_e, b * PAIRS + (2 * st + 2))
                            if st == 0:
                                pe.wait_ge(s_vs, b + 1)
                                if not first:
                                    pe.wait_ge(s_ev, b * 2)
                            if st == SETS // 2:
                                pe.wait_ge(s_ev, b * 2 + 1)
                        for g in range(4):
                            last = pe.matmul(PV[32 * g:32 * g + VW, st % 2, :], vs[p][:, mt, 4 * st + g, :],
                                             E[st % 2][:, g, mt, :], start=(mt == 0), stop=(mt == 1))
                        if mt == 1:
                            last.then_inc(s_pv, 1)

                    def to_tokens(b, p, nt, last=False):
                        if nt == 0:
                            pe.wait_ge(s_ev, b * 2 + 2)
                            if last:
                                pe.wait_ge(s_t2d, B - 1)
                            else:
                                pe.wait_ge(s_nmc, b * 2 + 4)
                        else:
                            pe.wait_ge(s_t1d, b * 2 + 1)
                        for st in range(4):
                            turned = pe.transpose(Pm[:, st * 128:(st + 1) * 128], yraw[p][:, st, nt * 128:(nt + 1) * 128], ident[:, :])
                        turned.then_inc(s_t1, 1)

                    def to_features(b, p, last_of_all):
                        pe.wait_ge(s_t1d, b * 2 + 2)
                        if not last_of_all:
                            pe.wait_ge(s_nmc, b * 2 + 5)
                        for nt in range(2):
                            last = pe.transpose(Pm[:, nt * 128:(nt + 1) * 128], ytok[p][:, nt, :], ident[:, :])
                        last.then_inc(s_t2, 1)

                    def previous_set(b, j, p, first, mt):
                        if j == 0 and not first:
                            times_v(b - 1, SETS - 1, 1 - p, False, mt)
                        elif j > 0 and j % 2 == 0:
                            times_v(b, j // 2 - 1, p, first, mt)

                    def body(b, p, first, last_of_all):
                        for j in range(PAIRS):
                            if j % (PAIRS // 2) == 0:
                                pe.wait_ge(s_neg, (b * 2 + (1 + j // (PAIRS // 2))) * 48)
                            if j >= 2 or not first:
                                pe.wait_ge(s_e, b * PAIRS + (j - 1))
                            for i in range(2):
                                h = 2 * j + i
                                for mt in range(2):
                                    last = pe.matmul(S2[j % 2][:, i, mt, :], kst[p][0:KEXP, h, mt * 128:(mt + 1) * 128],
                                                     qst[p][0:KEXP, h, :], start=True, stop=True)
                                if i == 1:
                                    last.then_inc(s_s2, 1)
                                    previous_set(b, j, p, first, 0)
                                if not last_of_all:
                                    if h % HALF == 0:
                                        pe.wait_ge(s_ld[1 - p][h // HALF], (b + (2 + p)) * (LOADS // 2))
                                    scores_for_max(b + 1, h, 1 - p, True)
                            previous_set(b, j, p, first, 1)
                            if j == 0:
                                if isinstance(b, int) and b < 2:
                                    maxima_to_rows(b, 1, s_nmc, b * 2 + 1)
                                else:
                                    maxima_to_rows(b, 1, s_t2d, b - 1)
                            if not first and j in (1, 3):
                                to_tokens(b - 1, 1 - p, j // 2)
                            if not last_of_all and j == 4:
                                if first:
                                    maxima_to_rows(b + 1, 0, s_nmc, 2)
                                else:
                                    maxima_to_rows(b + 1, 0, s_t1d, b * 2)
                            if not first and j == 5:
                                to_features(b - 1, 1 - p, last_of_all)

                    for i in range(2):
                        pe.wait_ge(s_ld[0][i], LOADS)
                        for h in range(i * HALF, (i + 1) * HALF):
                            scores_for_max(0, h, 0, h >= 2)
                        if i == 0:
                            maxima_to_rows(0, 0, None, 0)
                    steps(pe, body)
                    for mt in range(2):
                        times_v(B - 1, SETS - 1, 1, False, mt)
                    for nt in range(2):
                        to_tokens(B - 1, 1, nt, True)
                    to_features(B - 1, 1, True)

                @block.scalar
                def _(act):
                    def out_of_psum(b, p, half):
                        act.wait_ge(s_pv, b * SETS + (half + 1) * SETS // 2)
                        act.activation(yraw[p][:, 2 * half:2 * half + 2, :], PV[:, :, :], ACT.Copy).then_inc(s_ev, 1)

                    def body(b, p, first, last_of_all):
                        for j in range(PAIRS):
                            act.wait_ge(s_s2, b * PAIRS + (j + 1))
                            st = j // 2
                            if j % 2 == 0 and (st >= 2 or not first):
                                act.wait_ge(s_pv, b * SETS + (st - 1))
                            act.activation(E[st % 2][:, 2 * (j % 2):2 * (j % 2) + 2, :, :], S2[j % 2][:, :, :, :],
                                           ACT.Exp).then_inc(s_e, 1)
                            if j == 0 and not first:
                                out_of_psum(b - 1, 1 - p, 1)
                            if j == 4:
                                out_of_psum(b, p, 0)

                    for i in range(2):
                        load(act, 1, 1, i)
                    for n in "qk":
                        for j in range(3):
                            write(act, 1, n, j)
                    steps(act, body)
                    out_of_psum(B - 1, 1, 1)

                @block.vector
                def _(dve):
                    def head_max(at, h):
                        dve.wait_ge(s_s1, at * H3 + (h + 1))
                        dve.tensor_reduce(mx[:, h, :], S1[h % 2][:, :, :], AX.X, ALU.max).then_inc(s_mx, 1)

                    def maxima_parts(at, i):
                        m = mx[:, i * HALF:(i + 1) * HALF, :].rearrange("p h t -> p t h")
                        before = at * 8 + i * 4
                        dve.wait_ge(s_mx, at * H3 + (i + 1) * HALF)
                        dve.tensor_scalar(nm[:, i, :, 0, :], m, -1.0, None, ALU.mult).then_inc(s_np, 1)
                        dve.wait_ge(s_np, before + 1)
                        dve.scalar_tensor_tensor(nleft[:, :, :], m, -1.0, nm[:, i, :, 0, :], ALU.mult, ALU.subtract).then_inc(s_np, 1)
                        dve.wait_ge(s_np, before + 2)
                        dve.tensor_copy(nm[:, i, :, 1, :], nleft[:, :, :]).then_inc(s_np, 1)
                        dve.wait_ge(s_np, before + 3)
                        dve.tensor_tensor(nm[:, i, :, 2, :], nleft[:, :, :], nm[:, i, :, 1, :], ALU.subtract).then_inc(s_np, 1)

                    def rows_out(at, i, any_before=True):
                        dve.wait_ge(s_nm, at * 2 + (i + 1))
                        if any_before:
                            dve.wait_ge(s_neg, at * 96 + i * 48)
                        dve.tensor_copy(nmT[i][:, :], Pm[0:3 * HALF, 0:128].bitcast(bf16)).then_inc(s_nmc, 1)

                    def normalise(b, p, nt):
                        dve.wait_ge(s_t1, b * 2 + (nt + 1))
                        v = Pm[:, :].rearrange("p (h w) -> p h w", w=VW)
                        dve.reciprocal(rec[p][:, nt, :], v[:, :, W3]).then_inc(s_rc, 1)
                        dve.wait_ge(s_rc, b * 2 + (nt + 1))
                        dve.tensor_tensor(ytok[p][:, nt, :].rearrange("p (h w) -> p h w", w=W3), v[:, :, 0:W3],
                                          rec[p][:, nt, :].unsqueeze(2).to_broadcast([128, H3, W3]), ALU.mult).then_inc(s_t1d, 1)

                    def features_out(b):
                        dve.wait_ge(s_t2, b + 1)
                        dve.tensor_copy(yT[:, bass.ds(b * T, T)], Pm[:, 0:T]).then_inc(s_t2d, 1)

                    def body(b, p, first, last_of_all):
                        for j in range(PAIRS):
                            if not last_of_all:
                                if j % (PAIRS // 2) == 0:
                                    dve.wait_ge(s_np, b * 8 + (1 + j // (PAIRS // 2)) * 4)
                                for h in range(2 * j, 2 * j + 2):
                                    head_max(b + 1, h)
                                if j % (PAIRS // 2) == PAIRS // 2 - 1:
                                    maxima_parts(b + 1, j // (PAIRS // 2))
                            if j == 0:
                                rows_out(b, 1, True)
                            if not first and j in (1, 3):
                                normalise(b - 1, 1 - p, j // 2)
                            if not last_of_all and j == 4:
                                rows_out(b + 1, 0)
                            if not first and j == 5:
                                features_out(b - 1)

                    dve.memset(nm[:, :, :, :, :], 0.0).then_inc(s_nz, 1)
                    dve.wait_ge(s_nz, 1)
                    for i in range(2):
                        for h in range(i * HALF, (i + 1) * HALF):
                            head_max(0, h)
                        maxima_parts(0, i)
                        if i == 0:
                            rows_out(0, 0, False)
                    steps(dve, body)
                    for nt in range(2):
                        normalise(B - 1, 1, nt)
                    features_out(B - 1)

        def softmax_output(yT):
            with ExitStack() as on:
                s = s_layer
                before = 2 * QUARTERS
                s_stored = sem("s_stored", on)
                two = range(HALVES)

                def pair(n, shape):
                    return [sb(f"o{n}_{h}", shape, f32, on) for h in two]

                tmp, rstd, z, hs = (pair(n, [D, NH]) for n in ("tmp", "rstd", "z", "hs"))
                Pa = [ps(f"oPa_{h}", [128, NH], f32, on) for h in two]
                Pb = [ps(f"oPb_{h}", [128, NH], f32, on) for h in two]

                def toks(h):
                    return slice(h * NH, (h + 1) * NH)

                block = on.enter_context(nc.Block())

                @block.sync
                def _(sp):
                    for q in four:
                        n = quarter(q)[2]
                        sp.wait_ge(s["x"], before + q + 1)
                        sp.dma_start(out[:, n], xT[:, n]).then_inc(s_stored, 16)
                    sp.wait_ge(s_stored, 16 * QUARTERS)

                @block.tensor
                def _(pe):
                    for first, q in NORM_ORDER:
                        h, c, n = quarter(q)
                        if first:
                            pe.matmul(Pa[h][:, c], center[:, :], yT[:, n], start=True, stop=True).then_inc(s["mean1"], 1)
                        else:
                            pe.wait_ge(s["sq2"], before + q + 1)
                            pe.matmul(Pb[h][:, c], mean[:, :], tmp[h][:, c], start=True, stop=True).then_inc(s["var2"], 1)
                    for q in four:
                        h, c, _ = quarter(q)
                        pe.wait_ge(s["hs"], before + q + 1)
                        pe.matmul(Pb[h][:, c], mat("out3"), hs[h][:, c], start=True, stop=True).then_inc(s["o"], 1)

                @block.scalar
                def _(act):
                    for first, q in NORM_ORDER:
                        h, c, _ = quarter(q)
                        if first:
                            act.wait_ge(s["mean1"], before + q + 1)
                            act.activation(tmp[h][:, c], Pa[h][:, c], ACT.Square).then_inc(s["sq2"], 1)
                        else:
                            act.wait_ge(s["var2"], before + q + 1)
                            act.activation(tmp[h][:, c], Pb[h][:, c], ACT.Ln, bias=eps[:, :]).then_inc(s["lnv2"], 1)
                            act.wait_ge(s["lnv2"], before + q + 1)
                            act.activation(rstd[h][:, c], tmp[h][:, c], ACT.Exp, scale=-0.5).then_inc(s["rstd2"], 1)
                    for q in four:
                        h, c, _ = quarter(q)
                        act.wait_ge(s["z2"], before + q + 1)
                        for g in (2 * q, 2 * q + 1):
                            b = g % BH
                            last = act.activation(hs[h][:, b * T:(b + 1) * T], z[h][:, b * T:(b + 1) * T], ACT.Silu,
                                                  bias=film_t[2][:, g:g + 1], scale=film_s[2][:, g:g + 1])
                        last.then_inc(s["hs"], 1)

                @block.vector
                def _(dve):
                    for q in four:
                        h, c, _ = quarter(q)
                        dve.wait_ge(s["rstd2"], before + q + 1)
                        dve.tensor_tensor(z[h][:, c], Pa[h][:, c], rstd[h][:, c], ALU.mult).then_inc(s["z2"], 1)
                    for q in four:
                        h, c, n = quarter(q)
                        dve.wait_ge(s["o"], before + q + 1)
                        dve.scalar_tensor_tensor(xT[:, n], Pb[h][:, c], col("bout3"), xT[:, n],
                                                 ALU.add, ALU.add).then_inc(s["x"], 1)

        with keep2:
            with front:
                block = front.enter_context(nc.Block())

                @block.sync
                def _(sp):
                    sp.dma_start(cond[:, :], a_cond).then_inc(s_cols, 16)
                    sp.dma_start(cols[:, :], a_cols).then_inc(s_cols, 16)
                    sp.dma_start(xT[:, toks(0)], a_x[:, toks(0)]).then_inc(s_x[0], 16)
                    sp.dma_start(xT[:, toks(1)], a_x[:, toks(1)]).then_inc(s_x[1], 16)
                    sp.dma_start(rows[:, :], a_rows).then_inc(s_cols, 16)
                    sp.wait_ge(s_mpart, 1)
                    for j in range(3):
                        for i in range(3):
                            sp.dma_start(mrow[j:j + 1, i * N:(i + 1) * N].rearrange("p (a b) -> p a b", b=128),
                                         mpart[j][:, i * 128:(i + 1) * 128]).then_inc(s_mrow, 16)
                    sp.dma_start(w1[:, :], a_w1).then_inc(s_w1, 16)
                    for i in range(3):
                        sp.wait_ge(s_bpart, i + 1)
                        r = slice(0, 2 * D) if i < 2 else slice(D, 2 * D)
                        for j in range(3):
                            sp.dma_start(brow[i][j:j + 1, r], bpart[i][j][:, r]).then_inc(s_brow[i], 16)
                        if i == 0:
                            sp.dma_start(w2[:, :], a_w2).then_inc(s_w2, 16)
                            sp.dma_start(dtp[:, :], a_dtp).then_inc(s_w2, 16)
                    for i in range(3):
                        sp.wait_ge(s_brow[i], 16 * 3)

                @block.gpsimd
                def _(pool):
                    setup_gpsimd(pool)
                    link = linker(pool, s_folding)
                    fold_gpsimd(pool, link, 0)
                    attention_gpsimd(pool, 0)
                    fold_gpsimd(pool, link, 1)
                    attention_gpsimd(pool, 1)
                    fold_gpsimd(pool, link, 3)
                    fold_gpsimd(pool, link, 2)
                    mamba_gpsimd(pool)

                @block.tensor
                def _(pe):
                    pe.wait_ge(s_cst, 7)
                    for i in range(2):
                        attention_tensor(pe, i)
                    mamba_tensor(pe)

                @block.scalar
                def _(act):
                    setup_scalar(act)
                    for i in range(2):
                        attention_scalar(act, i)
                    mamba_scalar(act)

                @block.vector
                def _(dve):
                    setup_vector(dve)
                    for i in range(2):
                        attention_vector(dve, i)
                    mamba_vector(dve)

            mamba_scan(u, zs, dt, dtu, bc, sel, acoef)
        softmax_layer()


def kernel(**inputs):
    import numpy as np
    import concourse.bacc as bacc
    from concourse import mybir
    from concourse.bass_utils import run_bass_kernel_spmd

    a = {k: np.asarray(v) for k, v in inputs.items()}
    names = {"0": ("L0_cond_", "Wq Wk Wv W_emb W_out ln_w ln_b bq bk bv b_emb ln2_w ln2_b b_out"),
             "1": ("L1_cond_", "Wq Wk Wv film_emb_W film_out_W norm_scale norm_bias bq bk bv film_emb_b "
                               "film_norm_scale film_norm_bias film_out_b"),
             "3": ("L3_cond_", "q_w k_w v_w emb_w out_w norm_w norm_b q_b k_b v_b emb_b sb_norm_w sb_norm_b out_b")}
    keys = ["q", "k", "v", "emb", "out", "lnw", "lnb", "bq", "bk", "bv", "bemb", "ln2w", "ln2b", "bout"]
    m = {}

    def halves(w):
        return np.concatenate([w[i:i + 128] for i in range(0, w.shape[0], 128)], axis=1)

    for n, (prefix, parts) in names.items():
        for key, part in zip(keys, parts.split()):
            m[key + n] = a[prefix + part]
        m["emb" + n] = halves(m["emb" + n])
        if n == "3":
            for key in ("q3", "k3", "bq3", "bk3"):
                m[key] = m[key].reshape(-1, HEADS[2], D // HEADS[2]).swapaxes(1, 2).reshape(m[key].shape)
        m["embs" + n], m["embt" + n] = m["bemb" + n][:D], m["bemb" + n][D:]
    p = "L2_cond_"
    m["ada"] = halves(a[p + "ada_w"].T)
    m["adat"], m["adas"], m["adag"] = a[p + "ada_b"].reshape(3, D)
    m["inp"] = a[p + "in_proj_w"].T
    xp = halves(a[p + "x_proj_w"].T).reshape(128, CH, RANK + 2 * NS)
    m["xdt"] = xp[:, :, :RANK].reshape(128, -1)
    m["xbc"] = xp[:, :, RANK:].reshape(128, -1)
    m["outp"] = halves(a[p + "out_proj_w"].T)
    m["alog"] = halves(a[p + "A_log"])
    m["convw"] = halves(a[p + "conv_w"])
    m["g2"], m["b2"] = a[p + "ln_g"], a[p + "ln_b"]
    for c in range(CH):
        for key, part in (("convb", "conv_b"), ("dtb", "dt_proj_b"), ("dp", "D_param")):
            m[f"{key}_{c}"] = a[p + part][c * 128:(c + 1) * 128]
    arrays = {
        "a_x": a["x"].reshape(N, D).T,
        "a_cond": halves(a["cond_2048"].T),
        "a_w0": np.concatenate([m[n] for n, _ in MATS0], axis=1),
        "a_w1": np.concatenate([m[n] for n, _ in MATS1], axis=1),
        "a_w2": np.concatenate([m[n] for n, _ in MATS2], axis=1),
        "a_dtp": a[p + "dt_proj_w"].T,
        "a_cols": np.stack([m[c] for c in COLS], axis=1),
        "a_rows": np.concatenate([m[r] for r in ROWS]).reshape(1, -1),
        "a_keep0": a["mask_BxSx1_fk1"].reshape(N // 128, 128),
        "a_mask1": a["mask_BxS_ik0"].reshape(N // 128, 128),
        "a_keep3": a["mask_BxS_ff1"].reshape(N // 128, 128),
    }
    nc = bacc.Bacc("TRN2", target_bir_lowering=False, num_devices=1)
    args = []
    for name in arrays:
        arrays[name] = np.ascontiguousarray(arrays[name])
        args.append(nc.dram_tensor(name, arrays[name].shape, mybir.dt.from_np(arrays[name].dtype),
                                   kind="ExternalInput").ap())
    args.append(nc.dram_tensor("out", (D, N), mybir.dt.float32, kind="ExternalOutput").ap())
    cond_seq_kernel(nc, *args)
    got = run_bass_kernel_spmd(nc, [arrays], core_ids=[0]).results[0]["out"]
    return np.ascontiguousarray(got.T).reshape(B, T, D)
```
